# Optimizing a Trainium2 kernel written in Bass

```python
import numpy as np
import jax
import jax.numpy as jnp

def _softmax(x, axis=-1):
    return jax.nn.softmax(x, axis=axis)

def _gelu(x):
    return jax.nn.gelu(x, approximate=True)

def _silu(x):
    return jax.nn.silu(x)

def _sigmoid(x):
    return jax.nn.sigmoid(x)

def _layernorm(x, axis=-1, eps=1e-05):
    m = jnp.mean(x, axis=axis, keepdims=True)
    v = jnp.var(x, axis=axis, keepdims=True)
    return (x - m) / jnp.sqrt(v + eps)

def _scatter_add(tgt, idx, src, axis=0):
    return tgt.at[idx].add(src)

def _segment_sum(src, seg, n):
    return jax.ops.segment_sum(src, seg, n)
kernel_name = 'mk_adj_resnorm_d2_adj_r2_b460ab'

def setup_inputs(seed: int=0):
    np.random.seed(seed)
    _w = jnp.asarray

    def _rec_inputs():
        import jax
        import jax.numpy as jnp
        _gk = jax.random.key(seed)
        x = -0.0002928 + 1 * jax.random.normal(jax.random.fold_in(_gk, 1), (8, 1024, 128), jnp.float32)
        _a = jax.random.bernoulli(jax.random.fold_in(_gk, 2), 0.00195312, (8, 1024, 1024))
        _a = jnp.logical_or(_a, jnp.swapaxes(_a, -1, -2))
        _a = jnp.logical_or(_a, jnp.eye(1024, dtype=bool))
        _af = _a.astype(jnp.float32)
        _af = _af * jax.random.uniform(jax.random.fold_in(_gk, 3), (8, 1024, 1024), jnp.float32, 0.05, 1)
        adj = _af
        return (x, adj)
    x, adj = _rec_inputs()

    def _L0_gnn_setup():
        import jax, jax.numpy as jnp
        import numpy as np
        EPS = 1e-05
        N_LAYERS_TOTAL = 4
        key = jax.random.key(seed)
        ks = jax.random.split(key, 6)
        B, N, C = (16, 1024, 128)
        x = jax.random.normal(ks[0], (B, N, C), dtype=jnp.float32)
        adj = jax.random.uniform(ks[1], (B, N, N), dtype=jnp.float32)
        W = jax.random.normal(ks[2], (N_LAYERS_TOTAL, C, C), dtype=jnp.float32) * (1.0 / np.sqrt(C))
        b = jnp.zeros((N_LAYERS_TOTAL, C), dtype=jnp.float32)
        gamma = jnp.ones((N_LAYERS_TOTAL, C), dtype=jnp.float32)
        beta = jnp.zeros((N_LAYERS_TOTAL, C), dtype=jnp.float32)
        return {'x': x, 'adj': adj, 'W': W, 'b': b, 'gamma': gamma, 'beta': beta}
    _L0_gnn_all = _L0_gnn_setup()
    _L0_gnn_in = {k: v for k, v in _L0_gnn_all.items() if k in ('W', 'b', 'gamma', 'beta')}
    del _L0_gnn_all

    def _L1_gnn_setup():
        import jax, jax.numpy as jnp
        import numpy as np
        B, T, IN_CH, OUT_CH = (4, 256, 128, 128)
        NEG_INF = -1e+22
        key = jax.random.key(seed)
        kx, ka, kq, kk, kp = jax.random.split(key, 5)
        x = jax.random.normal(kx, (B, T, IN_CH), dtype=jnp.float32)
        adj = jax.random.normal(ka, (B, T, T), dtype=jnp.float32)
        s_qk = float(np.sqrt(6.0 / (IN_CH + OUT_CH)))
        WQ = jax.random.uniform(kq, (IN_CH, OUT_CH), jnp.float32, -s_qk, s_qk)
        WK = jax.random.uniform(kk, (IN_CH, OUT_CH), jnp.float32, -s_qk, s_qk)
        s_p = float(np.sqrt(6.0 / (OUT_CH + 1)))
        p = jax.random.uniform(kp, (OUT_CH,), jnp.float32, -s_p, s_p)
        return {'x': x, 'adj': adj, 'WQ': WQ, 'WK': WK, 'p': p}
    _L1_gnn_all = _L1_gnn_setup()
    _L1_gnn_in = {k: v for k, v in _L1_gnn_all.items() if k in ('WQ', 'WK', 'p')}
    del _L1_gnn_all
    return {'x': x, 'adj': adj, 'L0_gnn_W': _L0_gnn_in['W'], 'L0_gnn_b': _L0_gnn_in['b'], 'L0_gnn_gamma': _L0_gnn_in['gamma'], 'L0_gnn_beta': _L0_gnn_in['beta'], 'L1_gnn_WQ': _L1_gnn_in['WQ'], 'L1_gnn_WK': _L1_gnn_in['WK'], 'L1_gnn_p': _L1_gnn_in['p']}

def reference(x, adj, L0_gnn_W, L0_gnn_b, L0_gnn_gamma, L0_gnn_beta, L1_gnn_WQ, L1_gnn_WK, L1_gnn_p):
    import jax
    import jax.numpy as jnp

    def _L0_gnn_ref(x, adj, W, b, gamma, beta):
        import jax, jax.numpy as jnp
        import numpy as np
        EPS = 1e-05
        N_LAYERS_TOTAL = 4
        h = x
        for i in range(N_LAYERS_TOTAL):
            h = jnp.einsum('bnm,bmc->bnc', adj, h @ W[i]) + b[i]
            h = jax.nn.relu(h)
            mu = jnp.mean(h, axis=(0, 1))
            var = jnp.mean(jnp.square(h - mu), axis=(0, 1))
            h = gamma[i] * (h - mu) * jax.lax.rsqrt(var + EPS) + beta[i]
        return h

    def _L1_gnn_ref(x, adj, WQ, WK, p):
        import jax, jax.numpy as jnp
        import numpy as np
        B, T, IN_CH, OUT_CH = (4, 256, 128, 128)
        NEG_INF = -1e+22
        'Faithful LGCN forward (eval mode: dropout is identity).\n\n            att[b,i,j] = p . relu(q[b,j] + k[b,i])   (note torch indexing:\n            feat_q broadcast over dim 1, feat_k broadcast over dim 2)\n            out[b,i]  = sum_j softmax_j(att + mask)[b,i,j] * x[b,j]\n            '
        mask = jnp.where(adj > 0, jnp.float32(0.0), jnp.float32(NEG_INF))
        q = x @ WQ
        k = x @ WK
        h = jax.nn.relu(q[:, None, :, :] + k[:, :, None, :])
        score = jnp.einsum('bijd,d->bij', h, p)
        att = jax.nn.softmax(score + mask, axis=-1)
        return jnp.matmul(att, x)
    x = _layernorm(x + _L0_gnn_ref(x, adj, L0_gnn_W, L0_gnn_b, L0_gnn_gamma, L0_gnn_beta), axis=-1)
    x = _layernorm(x + _L1_gnn_ref(x, adj, L1_gnn_WQ, L1_gnn_WK, L1_gnn_p), axis=-1)
    return x

_drawn_inputs = setup_inputs


def setup_inputs(seed=0):
    import zlib

    import numpy as np

    out = dict(_drawn_inputs(seed))
    spreads = {'L0_gnn_b': (0.0, 0.1), 'L0_gnn_gamma': (1.0, 0.2), 'L0_gnn_beta': (0.0, 0.1)}
    factors = {}
    for name, (base, spread) in spreads.items():
        noise = np.random.default_rng([zlib.crc32(name.encode()), seed]).standard_normal(out[name].shape)
        drawn = base * np.exp(spread * noise) if base else spread * noise
        out[name] = jnp.asarray(drawn.astype(out[name].dtype))
    for name, factor in factors.items():
        out[name] = (out[name] * factor).astype(out[name].dtype)
    return out
```

```python
from contextlib import ExitStack

import numpy as np

import concourse.bass as bass
from concourse import mybir
from concourse.alu_op_type import AluOpType as ALU

ACT = mybir.ActivationFunctionType
AX = mybir.AxisListType
f32, f16, i32 = mybir.dt.float32, mybir.dt.float16, mybir.dt.int32
ds = bass.ds

P = 128
B, N, C = 8, 1024, 128
LAYERS = 4
MT = N // P
NODES = B * N
TILES = NODES // P
HALF = N // 2
QH = MT // 2
CHUNKS = 2 * B
RES = 3
STREAM = B - RES
UNIT = MT * HALF
SUB = UNIT // 2
RING = 4
K = 24
ROUNDS = K // 8
EPS = 1e-5
NEG = -1e22


def hold(eng, sem, value, passed):
    eng.wait_ge(sem, value)
    eng.sem_inc(passed, 1)


def part_one(nc, ctx, io, mem):
    sem = lambda name: ctx.enter_context(nc.semaphore(name))
    bank = mem["bank"]
    tp, hwp, acc = bank[0:4], bank[4:6], bank[6:8]
    A, hT, hst, hws, xs, nat = mem["A"], mem["hT"], mem["hst"], mem["hws"], mem["xs"], mem["nat"]
    ring = [mem["A"][:, (2 * RES + h) * UNIT:(2 * RES + h + 1) * UNIT] for h in range(2)]
    x3 = io["x"].rearrange("b (t p) c -> b p t c", p=P)
    adj4 = io["adj"].rearrange("b (t p) m -> b t p m", p=P)
    adjT = io["adjT"]

    const_ready = sem("const_ready")
    par_in = sem("par_in")
    x_in = sem("x_in")
    nat_in = [sem(f"nat_in{k}") for k in range(QH)]
    again_in = [sem(f"again_in{h}") for h in range(2)]
    xT_full = sem("xT_full")
    hst_ready = sem("hst_ready")
    hw_full = sem("hw_full")
    hws_ready = sem("hws_ready")
    tp_full = sem("tp_full")
    tp_free = sem("tp_free")
    acc_full = sem("acc_full")
    r_ready = sem("r_ready")
    store_done = [sem(f"store_done{h}") for h in range(2)]
    ring_in = [sem(f"ring_in{i}") for i in range(4)]
    ring_used = sem("ring_used")
    stats = sem("stats")
    norm = sem("norm")
    var_ready = sem("var_ready")
    std_ready = sem("std_ready")
    mask_done = sem("mask_done")
    key_ready = sem("key_ready")
    ext = sem("ext")
    sp_on, pool_on, dve_on = sem("sp_on"), sem("pool_on"), sem("dve_on")
    ext_done = sem("ext_done")
    const_act = sem("const_act")

    NORM_STEPS = 6

    block = ctx.enter_context(nc.Block())

    def each_graph(eng, resident, streamed):
        with eng.Fori(0, RES) as b:
            resident(b)
        with eng.Fori(RES, B) as b:
            streamed(b)

    @block.sync
    def _(sp):
        sp.dma_start(mem["W"][:, :].rearrange("p (l c) -> p l c", l=LAYERS), io["W"].rearrange("l i c -> i l c")).then_inc(par_in, 16)
        for name, col in (("b", 0), ("gamma", 1), ("beta", 2)):
            with nc.allow_non_contiguous_dma(reason="the small vectors, once"):
                sp.dma_start(mem["vec"][:, col * LAYERS:(col + 1) * LAYERS], io[name].rearrange("l c -> c l")).then_inc(par_in, 16)
        def loads(b, first):
            if not first:
                sp.wait_ge(xT_full, 2 * b)
            sp.dma_start(xs[:, :].rearrange("p (t c) -> p t c", t=MT), x3[ds(b, 1)].rearrange("o p t c -> p (o t) c")).then_inc(x_in, 16)
            for h in range(2):
                for k in range(QH):
                    if not (first and h == 0):
                        hold(sp, tp_full, 8 * (2 * b + h - 1) + 2 * k + 2, sp_on)
                        if k == 0:
                            sp.wait_ge(key_ready, 2 * b + h)
                    sp.dma_start(nat[k][:, :], adj4[ds(b, 1), h * QH + k].rearrange("o p m -> (o p) m")).then_inc(nat_in[k], 16)
        loads(0, True)
        with sp.Fori(1, B) as b:
            loads(b, False)
        sp.wait_ge(acc_full, CHUNKS)
        for h in range(2):
            sp.wait_ge(store_done[h], 16 * STREAM)
        def stream(L, b, first):
            for h in range(2):
                for q in range(2):
                    if first and q == 0:
                        if not isinstance(L, int):
                            sp.wait_ge(ring_used, 2 * STREAM * (L - 1) - 1 + h)
                    elif q == 0:
                        sp.wait_ge(ring_used, 2 * STREAM * (L - 1) + 2 * (b - RES) + h - 1)
                    elif first:
                        if not isinstance(L, int):
                            sp.wait_ge(acc_full, CHUNKS * L - 1 + h)
                    else:
                        sp.wait_ge(acc_full, CHUNKS * L + 2 * (b - 1) + h + 1)
                    sp.dma_start(ring[h][:, q * SUB:(q + 1) * SUB],
                                 adjT[ds(b - RES, 1), h, :, q * SUB:(q + 1) * SUB].rearrange("o p e -> (o p) e")).then_inc(ring_in[2 * h + q], 16)
        stream(1, RES, True)
        with sp.Fori(RES + 1, B) as b:
            stream(1, b, False)
        with sp.Fori(2, LAYERS) as L:
            stream(L, RES, True)
            with sp.Fori(RES + 1, B) as b:
                stream(L, b, False)

    @block.gpsimd
    def _(pool):
        pool.memset(mem["ident"][:, :], 0.0).then_inc(const_ready, 1)
        pool.wait_ge(const_ready, 1)
        pool.affine_select(out=mem["ident"][:, :], in_=mem["ident"][:, :], compare_op=ALU.not_equal, fill=1.0,
                           base=0, pattern=[[-1, P]], channel_multiplier=1).then_inc(const_ready, 1)
        pool.iota(mem["hst"][:, :].bitcast(i32), pattern=[[1, N]], base=1, channel_multiplier=0).then_inc(const_ready, 1)
        pool.wait_ge(const_ready, 3)
        pool.tensor_copy(mem["iota"][:, :], mem["hst"][:, :].bitcast(i32)).then_inc(const_ready, 1)
        pool.wait_ge(const_ready, 4)

        def make_key(e, slot, par, first):
            if not first:
                hold(pool, ext_done, e - 1, pool_on)
            key = mem["key"][par]
            pool.tensor_scalar(key[:, :], nat[slot][:, :], 0.0, None, ALU.is_gt).then_inc(mask_done, 1)
            pool.wait_ge(mask_done, e + 1)
            pool.tensor_tensor(key[:, :], key[:, :], mem["iota"][:, :], ALU.mult).then_inc(key_ready, 1)

        def layer0(b, first):
            for h in range(2):
                hold(pool, nat_in[0], 16 * (2 * b + h + 1), pool_on)
                make_key(2 * b + h, 0, h, first)
        layer0(0, True)
        with pool.Fori(1, B) as b:
            layer0(b, False)
        pool.wait_ge(tp_full, 8 * CHUNKS)

        def fetch(L, b, h):
            pool.dma_start(nat[h][:, :], adj4[ds(b, 1), ds(h * QH + L, 1)].rearrange("o u p m -> (o u p) m")).then_inc(again_in[h], 16)
        def keys(L, b, h):
            hold(pool, again_in[h], 16 * (B * (L - 1) + b + 1), pool_on)
            make_key(CHUNKS * L + 2 * b + h, h, h, False)
            pool.wait_ge(key_ready, CHUNKS * L + 2 * b + h + 1)
        pool.wait_ge(key_ready, CHUNKS)
        fetch(1, 0, 0)
        fetch(1, 0, 1)

        def later(L, last):
            with pool.Fori(0, B - 1) as b:
                for h in range(2):
                    keys(L, b, h)
                    fetch(L, b + 1, h)
            for h in range(2):
                keys(L, B - 1, h)
                if not last:
                    fetch(L + 1, 0, h)
        with pool.Fori(1, LAYERS - 1) as L:
            later(L, False)
        later(LAYERS - 1, True)

    @block.tensor
    def _(pe):
        pe.wait_ge(const_ready, 4)
        pe.wait_ge(par_in, 64)

        def h_times_w(L, b, Wl):
            for q in range(2):
                pe.wait_ge(hst_ready, 2 * (B * L + b) + q + 1)
                for t in range(QH):
                    m = q * QH + t
                    last = nc.tensor.matmul(hwp[q][:, t * C:(t + 1) * C], hst[:, m * P:(m + 1) * P], Wl, start=True, stop=True)
                last.then_inc(hw_full, 1)

        def chunk(L, b, h, unit, first=False, ring_round=None):
            if not first:
                pe.wait_ge(r_ready, CHUNKS * L + 2 * b + h - 1)
            for q in range(2):
                if h == 0:
                    pe.wait_ge(hws_ready, 2 * (B * L + b) + q + 1)
                if ring_round is not None:
                    pe.wait_ge(ring_in[2 * h + q], 16 * ring_round)
                for t in range(QH):
                    m = q * QH + t
                    last = nc.tensor.matmul(acc[h][:, :], hws[:, m * C:(m + 1) * C], unit(m), start=(m == 0), stop=(m == MT - 1))
                if q == 0 and ring_round is not None:
                    last.then_inc(ring_used, 1)
            last.then_inc(acc_full, 1)

        def layer0(b, unit, first):
            pe.wait_ge(x_in, 16 * (b + 1))
            for q in range(2):
                for t in range(QH):
                    m = q * QH + t
                    last = nc.tensor.transpose(hwp[q][:, t * P:(t + 1) * P], xs[:, m * C:(m + 1) * C], mem["ident"][:, :])
                last.then_inc(xT_full, 1)
            h_times_w(0, b, mem["W"][:, 0:C])
            for h in range(2):
                for k in range(QH):
                    pe.wait_ge(nat_in[k], 16 * (2 * b + h + 1))
                    for q in range(2):
                        if not (first and h == 0 and k < 2):
                            pe.wait_ge(tp_free, 8 * (2 * b + h) + 2 * k + q - 3)
                        for t in range(QH):
                            m = q * QH + t
                            last = nc.tensor.transpose(tp[(2 * k + q) % 4][:, t * P:(t + 1) * P], nat[k][:, m * P:(m + 1) * P], mem["ident"][:, :])
                        last.then_inc(tp_full, 1)
                pe.wait_ge(tp_free, 8 * (2 * b + h) + 8)
                chunk(0, b, h, lambda m: unit(h, m), first=first)

        def resident(b):
            return lambda h, m: A[:, ds((2 * b + h) * UNIT + m * HALF, HALF)]
        def in_ring(h, m):
            return ring[h][:, m * HALF:(m + 1) * HALF]

        layer0(0, resident(0), True)
        with pe.Fori(1, RES) as b:
            layer0(b, resident(b), False)
        with pe.Fori(RES, B) as b:
            layer0(b, in_ring, False)
        with pe.Fori(1, LAYERS) as L:
            with pe.Fori(0, RES) as b:
                h_times_w(L, b, mem["W"][:, ds(L * C, C)])
                for h in range(2):
                    chunk(L, b, h, lambda m: resident(b)(h, m))
            with pe.Fori(RES, B) as b:
                h_times_w(L, b, mem["W"][:, ds(L * C, C)])
                for h in range(2):
                    chunk(L, b, h, lambda m: in_ring(h, m), ring_round=STREAM * (L - 1) + b - RES + 1)

    @block.scalar
    def _(act):
        act.wait_ge(par_in, 64)

        def hw_out(L, b):
            for q in range(2):
                act.wait_ge(hw_full, 2 * (B * L + b) + q + 1)
                nc.scalar.activation(hws[:, q * HALF:(q + 1) * HALF], hwp[q][:, :], ACT.Copy).then_inc(hws_ready, 1)

        def relu(L, b, h):
            act.wait_ge(acc_full, CHUNKS * L + 2 * b + h + 1)
            nc.scalar.activation(hT[:, ds(b * N + h * HALF, HALF)], acc[h][:, :], ACT.Relu,
                                 bias=mem["bcol"][:, 0:1]).then_inc(r_ready, 1)

        def layer0(b, unit_at, first, stored):
            for q in range(2):
                act.wait_ge(xT_full, 2 * b + q + 1)
                if first:
                    act.wait_ge(const_ready, 4)
                nc.scalar.activation(hst[:, q * HALF:(q + 1) * HALF], hwp[q][:, :], ACT.Copy).then_inc(hst_ready, 1)
            hw_out(0, b)
            for h in range(2):
                if stored == 2:
                    act.wait_ge(store_done[h], 16 * (b - RES))
                for k in range(QH):
                    for q in range(2):
                        act.wait_ge(tp_full, 8 * (2 * b + h) + 2 * k + q + 1)
                        dst = unit_at(h, q).rearrange("p (m n) -> p m n", n=HALF)[:, :, k * P:(k + 1) * P]
                        nc.scalar.activation(dst, tp[(2 * k + q) % 4][:, :].rearrange("p (m n) -> p m n", n=P), ACT.Copy).then_inc(tp_free, 1)
                if stored:
                    act.wait_ge(tp_free, 8 * (2 * b + h) + 8)
                    act.dma_start(adjT[ds(b - RES, 1), h].rearrange("o p e -> (o p) e"), ring[h][:, :]).then_inc(store_done[h], 16)
                relu(0, b, h)

        def resident(b):
            return lambda h, q: A[:, ds((2 * b + h) * UNIT + q * SUB, SUB)]
        def in_ring(h, q):
            return ring[h][:, q * SUB:(q + 1) * SUB]

        def bias_of(L):
            nc.scalar.activation(mem["bcol"][:, 0:1], mem["vec"][:, ds(L, 1)], ACT.Copy).then_inc(const_act, 1)
            act.wait_ge(const_act, L + 1)

        bias_of(0)
        layer0(0, resident(0), True, 0)
        with act.Fori(1, RES) as b:
            layer0(b, resident(b), False, 0)
        layer0(RES, in_ring, False, 1)
        with act.Fori(RES + 1, B) as b:
            layer0(b, in_ring, False, 2)

        def root(L):
            act.wait_ge(var_ready, L + 1)
            nc.scalar.activation(mem["bn"][:, 3:4], mem["bn"][:, 2:3], ACT.Sqrt).then_inc(std_ready, 1)
        root(0)
        with act.Fori(1, LAYERS) as L:
            bias_of(L)
            with act.Fori(0, B) as b:
                hw_out(L, b)
                for h in range(2):
                    relu(L, b, h)
            root(L)

    @block.vector
    def _(dve):
        dve.wait_ge(par_in, 64)

        def extract(e, h, tile):
            key, top = mem["key"][h], mem["top"][h]
            dve.sem_clear(ext)
            hold(dve, key_ready, e + 1, dve_on)
            for r in range(ROUNDS):
                nc.vector.max(top[:, 8 * r:8 * r + 8], key[:, :]).then_inc(ext, 1)
                dve.wait_ge(ext, 2 * r + 1)
                if r < ROUNDS - 1:
                    nc.vector.match_replace(key[:, :], top[:, 8 * r:8 * r + 8], key[:, :], 0.0).then_inc(ext, 1)
                    dve.wait_ge(ext, 2 * r + 2)
            nc.vector.tensor_copy(mem["keys"][:, ds(tile * K, K)], top[:, :]).then_inc(ext_done, 1)

        def chunk(L, b, h):
            c = CHUNKS * L + 2 * b + h
            extract(c, h, QH * (2 * b + h) + L)
            dve.wait_ge(r_ready, c + 1)
            nc.vector.bn_stats(mem["st"][:, ds((2 * b + h) * 6, 6)], hT[:, ds(b * N + h * HALF, HALF)]).then_inc(stats, 1)

        def norm_steps(L):
            bn, base = mem["bn"], NORM_STEPS * L
            hold(dve, stats, CHUNKS * (L + 1), dve_on)
            nc.vector.bn_aggr(bn[:, 0:2], mem["st"][:, :]).then_inc(norm, 1)
            dve.wait_ge(norm, base + 1)
            nc.vector.tensor_scalar(bn[:, 2:3], bn[:, 1:2], EPS, None, ALU.add).then_inc(var_ready, 1)
            dve.wait_ge(std_ready, L + 1)
            nc.vector.reciprocal(bn[:, 4:5], bn[:, 3:4]).then_inc(norm, 1)
            dve.wait_ge(norm, base + 2)
            nc.vector.tensor_tensor(bn[:, 5:6], bn[:, 4:5], mem["vec"][:, ds(LAYERS + L, 1)], ALU.mult).then_inc(norm, 1)
            dve.wait_ge(norm, base + 3)
            nc.vector.tensor_tensor(bn[:, 6:7], bn[:, 0:1], bn[:, 5:6], ALU.mult).then_inc(norm, 1)
            dve.wait_ge(norm, base + 4)
            nc.vector.tensor_tensor(bn[:, 7:8], mem["vec"][:, ds(2 * LAYERS + L, 1)], bn[:, 6:7], ALU.subtract).then_inc(norm, 2)
            dve.wait_ge(norm, base + 6)

        def affine(L, b):
            for q in range(2):
                dve.wait_ge(hw_full, 2 * (B * L + b) - 2 + q + 1)
                nc.vector.tensor_scalar(hst[:, q * HALF:(q + 1) * HALF], hT[:, ds(b * N + q * HALF, HALF)],
                                        mem["bn"][:, 5:6], mem["bn"][:, 7:8], ALU.mult, ALU.add).then_inc(hst_ready, 1)

        with dve.Fori(0, B) as b:
            for h in range(2):
                chunk(0, b, h)
        norm_steps(0)
        with dve.Fori(1, LAYERS) as L:
            affine(L, 0)
            with dve.Fori(0, B - 1) as b:
                for h in range(2):
                    if h == 1:
                        affine(L, b + 1)
                    chunk(L, b, h)
            for h in range(2):
                chunk(L, B - 1, h)
            norm_steps(L)


def constants(nc, ctx, mem):
    made = ctx.enter_context(nc.semaphore("made"))
    block = ctx.enter_context(nc.Block())

    @block.gpsimd
    def _(pool):
        count = [0]

        def link(ins):
            count[0] += 1
            ins.then_inc(made, 1)
            pool.wait_ge(made, count[0])

        tmp = mem["tmpi"]
        link(pool.iota(mem["own"][:, :], pattern=[[P, TILES]], base=0, channel_multiplier=1))
        link(pool.iota(tmp[:, 0:TILES].rearrange("p (b t) -> p b t", b=B), pattern=[[N, B], [0, MT]], base=-1, channel_multiplier=0))
        link(pool.tensor_copy(mem["graph0"][:, :], tmp[:, 0:TILES]))
        link(pool.iota(tmp[:, 0:TILES].rearrange("p (b t) -> p b t", b=B), pattern=[[1 - N, B], [0, MT]], base=NODES, channel_multiplier=0))
        link(pool.tensor_copy(mem["tomean"][:, :], tmp[:, 0:TILES]))
        link(pool.iota(tmp[:, 0:K], pattern=[[-1, K]], base=K, channel_multiplier=0))
        link(pool.tensor_copy(mem["classes"][:, :], tmp[:, 0:K]))
        link(pool.iota(tmp[:, 0:TILES], pattern=[[P, TILES]], base=0, channel_multiplier=0))
        link(pool.tensor_copy(mem["rank0"][:, :], tmp[:, 0:TILES]))
        link(pool.iota(tmp[:, 0:K], pattern=[[1, K]], base=0, channel_multiplier=0))
        link(pool.tensor_copy(mem["slot"][:, :], tmp[:, 0:K]))
        link(pool.memset(mem["ones"][:, :], 1.0))
        link(pool.affine_select(out=mem["below"][:, :], in_=mem["ones"][:, :], compare_op=ALU.is_gt, fill=0.0,
                                base=0, pattern=[[1, P]], channel_multiplier=-1))


def part_two(nc, ctx, io, mem):
    sem = lambda name: ctx.enter_context(nc.semaphore(name))
    bank = mem["bank"]
    hp, xp, qp = bank[0:2], bank[2:4], bank[4:8]
    sp_rank = bank[0]
    hT, hst, bn = mem["hT"], mem["hst"], mem["bn"]
    A = mem["A"]
    at = [0]

    def carve(cols):
        a = at[0]
        at[0] += cols
        return A[:, a:a + cols]

    z = [carve(N) for _ in range(2)]
    x1 = [carve(N) for _ in range(2)]
    x1T = carve(N)
    qk = [carve(2 * N) for _ in range(2)]
    wqk = carve(2 * C)
    st = carve(6 * MT)
    mv = carve(2 * MT)
    std, rstd, veps = carve(MT), carve(MT), carve(MT)
    xsum = carve(2 * B)
    xmean = carve(B)
    means = carve(2 * C)
    M, S, T, ones24 = (carve(K * TILES) for _ in range(4))
    cnt0, nolist = carve(TILES), carve(TILES)
    last, of_class, incl, shift = carve(K + 1), carve(K), carve(K), carve(K)
    rankf, slotsf, cumf = carve(TILES), carve(TILES), carve(TILES)
    info = carve(26 * TILES)
    assert at[0] <= 2 * (RES + 1) * UNIT

    two_in = sem("two_in")
    xres_in = [sem(f"xres_in{u}") for u in range(2)]
    h_ready = sem("h_ready")
    hrow_full = sem("hrow_full")
    zst = sem("zst")
    var2 = sem("var2")
    std2 = sem("std2")
    dstep = sem("dstep")
    x1_ready = sem("x1_ready")
    x1T_full = sem("x1T_full")
    x1T_ready = sem("x1T_ready")
    qk_full = sem("qk_full")
    qk_ready = sem("qk_ready")
    tab_out = [sem(f"tab_out{u}") for u in range(2)]
    rank = sem("rank")
    cls_ready = sem("cls_ready")
    cls_full = sem("cls_full")
    rank_ready = sem("rank_ready")
    placed = sem("placed")
    mean_full = sem("mean_full")
    mean_ready = sem("mean_ready")
    mean_rows = sem("mean_rows")
    mean_out = sem("mean_out")
    sp_on2 = sem("sp_on2")

    block = ctx.enter_context(nc.Block())
    qx = io["qx"][0:NODES, :].rearrange("(b t p) c -> b p t c", b=B, p=P)
    kx = io["kx"].rearrange("(b t p) c -> b p t c", b=B, p=P)
    x3 = io["x"].rearrange("b (t p) c -> b p t c", p=P)

    @block.sync
    def _(sp):
        sp.dma_start(wqk[:, 0:C], io["WQ"]).then_inc(two_in, 16)
        sp.dma_start(wqk[:, C:2 * C], io["WK"]).then_inc(two_in, 16)

        def load_x(b, u):
            sp.dma_start(z[u].rearrange("p (t c) -> p t c", c=C), x3[ds(b, 1)].rearrange("o p t c -> p (o t) c")).then_inc(xres_in[u], 16)

        def store(b, u):
            sp.wait_ge(x1_ready, MT * (b + 1))
            x3d = x1[u].rearrange("p (t c) -> p t c", c=C)
            qk3 = qk[u].rearrange("p (t c) -> p t c", c=2 * C)
            sp.dma_start(qx[ds(b, 1), :, :, C:2 * C].rearrange("o p t c -> p (o t) c"), x3d).then_inc(tab_out[u], 16)
            sp.dma_start(kx[ds(b, 1), :, :, C:2 * C].rearrange("o p t c -> p (o t) c"), x3d).then_inc(tab_out[u], 16)
            hold(sp, qk_ready, 4 * b + 4, sp_on2)
            sp.dma_start(qx[ds(b, 1), :, :, 0:C].rearrange("o p t c -> p (o t) c"), qk3[:, :, 0:C]).then_inc(tab_out[u], 16)
            sp.dma_start(kx[ds(b, 1), :, :, 0:C].rearrange("o p t c -> p (o t) c"), qk3[:, :, C:2 * C]).then_inc(tab_out[u], 16)
        load_x(0, 0)
        load_x(1, 1)
        with sp.Fori(0, B // 2 - 1) as i:
            for u in range(2):
                sp.wait_ge(x1_ready, MT * (2 * i + u + 1))
                load_x(2 * i + u + 2, u)
                store(2 * i + u, u)
        for u in range(2):
            store(B - 2 + u, u)
        sp.wait_ge(mean_rows, 2)
        sp.dma_start(io["qx"][NODES:NODES + B, :], means[0:B, :]).then_inc(mean_out, 16)
        for u in range(2):
            sp.wait_ge(tab_out[u], 64 * (B // 2))
        sp.wait_ge(mean_out, 16)

    @block.gpsimd
    def _(pool):
        pool.wait_ge(rank_ready, 1)
        for t in range(TILES):
            pool.indirect_dma_start(io["lists"], bass.IndirectOffsetOnAxis(ap=mem["ranki"][:, t:t + 1], axis=0),
                                    info[:, 26 * t:26 * t + 26].bitcast(i32), None).then_inc(placed, 16)
        pool.wait_ge(placed, 16 * TILES)

    @block.vector
    def _(dve):
        n_rank = [0]

        def link(ins):
            n_rank[0] += 1
            ins.then_inc(rank, 1)
            dve.wait_ge(rank, n_rank[0])

        keys3 = mem["keys"][:, :].rearrange("p (t k) -> p t k", k=K)
        by_tile = lambda a: a.rearrange("p (t k) -> p t k", k=K)
        by_class = lambda a: a.rearrange("p (k t) -> p k t", k=K)
        over_k = lambda a: a.rearrange("p (t o) -> p t o", o=1).to_broadcast([P, TILES, K])
        cnt = mem["cnt"]
        link(nc.vector.memset(ones24, 1.0))
        link(nc.vector.tensor_scalar(by_tile(M), keys3, 0.0, None, ALU.is_gt))
        link(nc.vector.tensor_reduce(cnt0, by_tile(M), AX.X, ALU.add))
        link(nc.vector.tensor_scalar(cnt[:, :], cnt0, 1.0, None, ALU.max))
        link(nc.vector.scalar_tensor_tensor(by_tile(T), keys3, 1.0, over_k(mem["graph0"][:, :]), ALU.max, ALU.add))
        link(nc.vector.scalar_tensor_tensor(nolist, cnt0, 0.0, mem["tomean"][:, :], ALU.is_equal, ALU.mult))
        link(nc.vector.tensor_tensor(by_tile(T)[:, :, 0], by_tile(T)[:, :, 0], nolist, ALU.add))
        info3 = info.rearrange("p (t k) -> p t k", k=26)
        link(nc.vector.tensor_copy(info3[:, :, 0:K].bitcast(i32), by_tile(T)))
        link(nc.vector.tensor_copy(info3[:, :, K].bitcast(i32), mem["own"][:, :]))
        link(nc.vector.tensor_copy(info3[:, :, K + 1], cnt[:, :]))
        link(nc.vector.tensor_tensor(by_class(M), cnt[:, :].rearrange("p (o t) -> p o t", o=1).to_broadcast([P, K, TILES]),
                                     mem["classes"][:, :].rearrange("p (k o) -> p k o", o=1).to_broadcast([P, K, TILES]), ALU.is_equal))
        link(nc.vector.tensor_tensor_scan(S, ones24, M, 0.0, ALU.mult, ALU.add))
        link(nc.vector.memset(last[:, 0:1], 0.0))
        link(nc.vector.tensor_copy(last[:, 1:K + 1], by_class(S)[:, :, TILES - 1]))
        nc.vector.tensor_tensor(of_class, last[:, 1:K + 1], last[:, 0:K], ALU.subtract).then_inc(cls_ready, 1)
        dve.wait_ge(cls_full, 1)
        link(nc.vector.tensor_copy(shift, sp_rank[:, K:2 * K]))
        link(nc.vector.tensor_tensor_scan(incl, ones24[:, 0:K], shift, 0.0, ALU.mult, ALU.add))
        link(nc.vector.tensor_tensor(shift, incl, shift, ALU.subtract))
        link(nc.vector.tensor_tensor(shift, sp_rank[:, 0:K], shift, ALU.add))
        link(nc.vector.tensor_tensor(shift, shift, last[:, 0:K], ALU.subtract))
        link(nc.vector.tensor_tensor(by_class(S), by_class(S), shift.rearrange("p (k o) -> p k o", o=1).to_broadcast([P, K, TILES]), ALU.add))
        link(nc.vector.tensor_tensor(S, S, M, ALU.mult))
        link(nc.vector.tensor_reduce(rankf, S.rearrange("p (k t) -> p t k", k=K), AX.X, ALU.add))
        nc.vector.tensor_scalar(mem["ranki"][:, :], rankf, -1.0, None, ALU.add).then_inc(rank_ready, 1)
        link(nc.vector.tensor_tensor(by_tile(T), incl.rearrange("p (o k) -> p o k", o=1).to_broadcast([P, TILES, K]), over_k(mem["rank0"][:, :]), ALU.is_gt))
        link(nc.vector.tensor_reduce(slotsf, by_tile(T), AX.X, ALU.add))
        link(nc.vector.tensor_copy(mem["slots"][:, :], slotsf))
        for r in range(RING):
            link(nc.vector.tensor_tensor_scan(cumf[:, r:TILES:RING], ones24[:, 0:TILES // RING], slotsf[:, r:TILES:RING], 0.0, ALU.mult, ALU.add))
        link(nc.vector.tensor_scalar(mem["arrive"][:, :], cumf, 16.0, None, ALU.mult))
        link(nc.vector.tensor_copy(mem["full"][:, :], incl[:, 0:1]))

        def affine(b):
            for q in range(2):
                nc.vector.tensor_scalar(hst[:, q * HALF:(q + 1) * HALF], hT[:, ds(b * N + q * HALF, HALF)],
                                        bn[:, 5:6], bn[:, 7:8], ALU.mult, ALU.add).then_inc(h_ready, 1)

        def graph(b, u, first, last_one):
            dve.wait_ge(xres_in[u], 8 * (b - u) + 16)
            for q in range(2):
                dve.wait_ge(hrow_full, 2 * b + q + 1)
                nc.vector.tensor_tensor(z[u][:, q * HALF:(q + 1) * HALF], hp[q][:, :], z[u][:, q * HALF:(q + 1) * HALF], ALU.add).then_inc(zst, 1)
            if not last_one:
                affine(b + 1)
            dve.sem_clear(dstep)
            for t in range(MT):
                dve.wait_ge(zst, 2 * b + 1 + t // QH)
                nc.vector.bn_stats(st[:, 6 * t:6 * t + 6], z[u][:, t * C:(t + 1) * C]).then_inc(dstep, 1)
            for t in range(MT):
                dve.wait_ge(dstep, t + 1)
                nc.vector.bn_aggr(mv[:, 2 * t:2 * t + 2], st[:, 6 * t:6 * t + 6]).then_inc(dstep, 1)
            dve.wait_ge(dstep, 2 * MT)
            nc.vector.tensor_scalar(veps, mv[:, 1:2 * MT:2], EPS, None, ALU.add).then_inc(var2, 1)
            dve.wait_ge(std2, b + 1)
            nc.vector.reciprocal(rstd, std).then_inc(dstep, 1)
            dve.wait_ge(dstep, 2 * MT + 1)
            if not first:
                dve.wait_ge(tab_out[u], 32 * (b - u))
            for t in range(MT):
                nc.vector.tensor_scalar(x1[u][:, t * C:(t + 1) * C], z[u][:, t * C:(t + 1) * C], mv[:, 2 * t:2 * t + 1], rstd[:, t:t + 1],
                                        ALU.subtract, ALU.mult).then_inc(x1_ready, 1)

        affine(0)
        for u in range(2):
            graph(u, u, True, False)
        with dve.Fori(1, B // 2 - 1) as i:
            for u in range(2):
                graph(2 * i + u, u, False, False)
        for u in range(2):
            graph(B - 2 + u, u, False, u == 1)
        dve.wait_ge(x1T_ready, 2 * B)
        link(nc.vector.tensor_reduce(xmean, xsum.rearrange("p (b q) -> p b q", q=2), AX.X, ALU.add))
        nc.vector.tensor_scalar(xmean, xmean, 1.0 / N, None, ALU.mult).then_inc(mean_ready, 1)

    @block.tensor
    def _(pe):
        pe.wait_ge(cls_ready, 1)
        nc.tensor.matmul(sp_rank[:, 0:K], mem["below"][:, :], of_class, start=True, stop=True)
        nc.tensor.matmul(sp_rank[:, K:2 * K], mem["ones"][:, :], of_class, start=True, stop=True).then_inc(cls_full, 1)
        pe.wait_ge(rank_ready, 1)
        pe.wait_ge(two_in, 32)

        def rows_of_h(b):
            for q in range(2):
                pe.wait_ge(h_ready, 2 * b + q + 1)
                for t in range(QH):
                    m = q * QH + t
                    last = nc.tensor.transpose(hp[q][:, t * P:(t + 1) * P], hst[:, m * P:(m + 1) * P], mem["ident"][:, :])
                last.then_inc(hrow_full, 1)

        def project(b, u, first=False):
            pe.wait_ge(x1_ready, MT * (b + 1))
            for q in range(2):
                for t in range(QH):
                    m = q * QH + t
                    last = nc.tensor.transpose(xp[q][:, t * P:(t + 1) * P], x1[u][:, m * P:(m + 1) * P], mem["ident"][:, :])
                last.then_inc(x1T_full, 1)
            for j in range(4):
                if j % 2 == 0:
                    pe.wait_ge(x1T_ready, 2 * b + j // 2 + 1)
                if not first:
                    pe.wait_ge(qk_ready, 4 * b + j - 3)
                for t in range(2):
                    m = 2 * j + t
                    last = nc.tensor.matmul(qp[j][:, t * 2 * C:(t + 1) * 2 * C], x1T[:, m * P:(m + 1) * P], wqk, start=True, stop=True)
                last.then_inc(qk_full, 1)

        rows_of_h(0)
        rows_of_h(1)
        project(0, 0, True)
        with pe.Fori(0, B // 2 - 1) as i:
            rows_of_h(2 * i + 2)
            project(2 * i + 1, 1)
            rows_of_h(2 * i + 3)
            project(2 * i + 2, 0)
        project(B - 1, 1)
        pe.wait_ge(mean_ready, 1)
        nc.tensor.transpose(hp[0][0:B, 0:P], xmean, mem["ident"][:, :]).then_inc(mean_full, 1)

    @block.scalar
    def _(act):
        def root(b):
            act.wait_ge(var2, b + 1)
            nc.scalar.activation(std, veps, ACT.Sqrt).then_inc(std2, 1)

        def x1T_out(b):
            for q in range(2):
                act.wait_ge(x1T_full, 2 * b + q + 1)
                nc.scalar.activation(x1T[:, q * HALF:(q + 1) * HALF], xp[q][:, :], ACT.Copy,
                                     accum_out=xsum[:, ds(2 * b + q, 1)]).then_inc(x1T_ready, 1)

        def qk_out(b, u, first):
            if not first:
                act.wait_ge(tab_out[u], 32 * (b - u))
            for j in range(4):
                act.wait_ge(qk_full, 4 * b + j + 1)
                nc.scalar.activation(qk[u][:, j * HALF:(j + 1) * HALF], qp[j][:, :], ACT.Copy).then_inc(qk_ready, 1)

        root(0)
        for u in range(2):
            x1T_out(u)
            root(u + 1)
            qk_out(u, u, True)
        with act.Fori(1, B // 2 - 1) as i:
            for u in range(2):
                x1T_out(2 * i + u)
                root(2 * i + u + 1)
                qk_out(2 * i + u, u, False)
        x1T_out(B - 2)
        root(B - 1)
        qk_out(B - 2, 0, False)
        x1T_out(B - 1)
        qk_out(B - 1, 1, False)
        nc.scalar.activation(means[0:B, 0:C], mem["ident"][0:B, :], ACT.Copy).then_inc(mean_rows, 1)
        act.wait_ge(mean_full, 1)
        nc.scalar.activation(means[0:B, C:2 * C], hp[0][0:B, 0:P], ACT.Copy).then_inc(mean_rows, 1)


def part_three(nc, ctx, io, mem):
    sem = lambda name: ctx.enter_context(nc.semaphore(name))
    A = mem["A"]
    at = [0]

    def carve(cols):
        a = at[0]
        at[0] += cols
        return A[:, a:a + cols]

    R = range(RING)
    G = [carve(K * 2 * C) for _ in R]
    mine = [carve(2 * C) for _ in R]
    info = [carve(26) for _ in R]
    y, o = [carve(C) for _ in R], [carve(C) for _ in R]
    home = [carve(1) for _ in R]
    pb = carve(C)
    zz = [carve(C) for _ in range(3)]
    score = [carve(K) for _ in range(2)]
    mask, masked = [carve(K) for _ in range(2)], [carve(K) for _ in range(2)]
    wgt = [carve(K) for _ in range(2)]
    nmax, den, rden = ([carve(1) for _ in range(2)] for _ in range(3))
    st, mv = carve(6 * RING), carve(2 * RING)
    veps, std, rstd = carve(RING), carve(RING), carve(RING)
    assert at[0] <= 2 * (RES + 1) * UNIT
    GROUPS = TILES // RING

    p_in = sem("p_in")
    info_in = [sem(f"info_in{r}") for r in R]
    mine_in = [sem(f"mine_in{r}") for r in R]
    slot_in = [sem(f"slot_in{r}") for r in R]
    tile_done = sem("tile_done")
    home_set = sem("home_set")
    out_ready = sem("out_ready")
    out_done = [sem(f"out_done{r}") for r in R]
    step = sem("step")
    masked_ready = sem("masked_ready")
    wgt_ready = sem("wgt_ready")
    var3 = sem("var3")
    std3 = sem("std3")
    fin = sem("fin")
    pool_on3, dve_on3 = sem("pool_on3"), sem("dve_on3")
    block = ctx.enter_context(nc.Block())

    def for_slots(eng, n, body):
        body(0)
        for s in range(1, 4):
            with eng.If(n > s):
                body(s)
        with eng.If(n > 4):
            body(4)
            for s in range(5, 8):
                with eng.If(n > s):
                    body(s)
            with eng.If(n > 8):
                body(8)
                for s in range(9, K):
                    with eng.If(n > s):
                        body(s)
                eng.nop()
            eng.nop()

    @block.sync
    def _(sp):
        full = sp.value_load(mem["full"][0:1, 0:1], min_val=0, max_val=NODES)
        with sp.If(full < 1):
            sp.dma_start(pb, io["p"].rearrange("(o c) -> o c", o=1).to_broadcast([P, C])).then_inc(p_in, 16)

            def load(t, r, first):
                if not first:
                    sp.wait_ge(tile_done, t - RING + 1)
                sp.dma_start(info[r].bitcast(i32), io["lists"][ds(t * P, P), :]).then_inc(info_in[r], 16)
            for r in R:
                load(r, r, True)
            with sp.Fori(1, GROUPS) as g:
                for r in R:
                    load(RING * g + r, r, False)

    @block.gpsimd
    def _(pool):
        full = pool.value_load(mem["full"][0:1, 0:1], min_val=0, max_val=NODES)
        with pool.If(full < 1):
            def gathers(g, r, first):
                t = RING * g + r
                n = pool.value_load(mem["slots"][0:1, ds(t, 1)], min_val=1, max_val=K)
                hold(pool, info_in[r], 16 * (g + 1), pool_on3)
                if not first:
                    hold(pool, tile_done, t - RING + 1, pool_on3)
                rows = info[r].bitcast(i32)
                pool.indirect_dma_start(mine[r], None, io["kx"], bass.IndirectOffsetOnAxis(ap=rows[:, K:K + 1], axis=0)).then_inc(mine_in[r], 16)

                def slot(s):
                    pool.indirect_dma_start(G[r][:, s * 2 * C:(s + 1) * 2 * C], None, io["qx"],
                                            bass.IndirectOffsetOnAxis(ap=rows[:, s:s + 1], axis=0)).then_inc(slot_in[r], 16)
                for_slots(pool, n, slot)

            def scatter(g, r):
                hold(pool, out_ready, RING * g + r + 1, pool_on3)
                pool.indirect_dma_start(io["out"], bass.IndirectOffsetOnAxis(ap=home[r].bitcast(i32), axis=0), o[r], None).then_inc(out_done[r], 16)

            for r in R:
                gathers(0, r, True)
            with pool.Fori(1, GROUPS) as g:
                gathers(g, 0, False)
                gathers(g, 1, False)
                scatter(g - 1, 0)
                scatter(g - 1, 1)
                gathers(g, 2, False)
                scatter(g - 1, 2)
                gathers(g, 3, False)
                scatter(g - 1, 3)
            for r in R:
                scatter(GROUPS - 1, r)
            for r in R:
                pool.wait_ge(out_done[r], 16 * GROUPS)

    @block.scalar
    def _(act):
        full = act.value_load(mem["full"][0:1, 0:1], min_val=0, max_val=NODES)
        with act.If(full < 1):
            def weights(g, r):
                t, u = RING * g + r, r % 2
                act.wait_ge(masked_ready, t + 1)
                nc.scalar.activation(wgt[u], masked[u], ACT.Exp, bias=nmax[u], accum_out=den[u]).then_inc(wgt_ready, 1)

            with act.Fori(0, GROUPS) as g:
                for r in R:
                    weights(g, r)
                act.wait_ge(var3, g + 1)
                nc.scalar.activation(std, veps, ACT.Sqrt).then_inc(std3, 1)

    @block.vector
    def _(dve):
        full = dve.value_load(mem["full"][0:1, 0:1], min_val=0, max_val=NODES)
        with dve.If(full < 1):
            dve.wait_ge(p_in, 16)
            nc.vector.memset(score[0], 0.0).then_inc(fin, 1)
            nc.vector.memset(score[1], 0.0).then_inc(fin, 1)
            dve.wait_ge(fin, 2)
            FIN = 1

            def scores(g, r):
                t, u = RING * g + r, r % 2
                n = dve.value_load(mem["slots"][0:1, ds(t, 1)], min_val=1, max_val=K)
                arrive = dve.value_load(mem["arrive"][0:1, ds(t, 1)], min_val=16, max_val=16 * K * GROUPS)
                dve.sem_clear(step)
                dve.wait_ge(info_in[r], 16 * (g + 1))
                nc.vector.tensor_scalar(mask[u], mem["slot"][:, :], info[r][:, K + 1:K + 2], NEG, ALU.is_ge, ALU.mult)
                dve.wait_ge(mine_in[r], 16 * (g + 1))
                dve.wait_ge(slot_in[r], arrive)

                def slot(s):
                    q, k = G[r][:, s * 2 * C:s * 2 * C + C], mine[r][:, 0:C]
                    w = zz[s % 2]
                    nc.vector.tensor_tensor(w, q, k, ALU.add).then_inc(step, 1)
                    dve.wait_ge(step, 2 * s + 1)
                    nc.vector.scalar_tensor_tensor(w, w, 0.0, pb, ALU.max, ALU.mult, accum_out=score[u][:, s:s + 1]).then_inc(step, 1)
                for_slots(dve, n, slot)
                hold(dve, step, 2 * n, dve_on3)
                dve.sem_clear(step)
                nc.vector.tensor_tensor_reduce(out=masked[u], in0=score[u], in1=mask[u], scale=1.0, scalar=NEG * 10, op0=ALU.add, op1=ALU.max,
                                               accum_out=nmax[u]).then_inc(step, 1)
                dve.wait_ge(step, 1)
                nc.vector.tensor_scalar(nmax[u], nmax[u], -1.0, None, ALU.mult).then_inc(masked_ready, 1)
                return n

            def rows(g, r, n):
                t, u = RING * g + r, r % 2
                dve.sem_clear(step)
                dve.wait_ge(wgt_ready, t + 1)
                nc.vector.reciprocal(rden[u], den[u])
                acc = zz[2]

                def slot(s):
                    x = G[r][:, s * 2 * C + C:(s + 1) * 2 * C]
                    if s == 0:
                        nc.vector.tensor_scalar(acc, x, wgt[u][:, 0:1], None, ALU.mult).then_inc(step, 1)
                    else:
                        dve.wait_ge(step, s)
                        nc.vector.scalar_tensor_tensor(acc, x, wgt[u][:, s:s + 1], acc, ALU.mult, ALU.add).then_inc(step, 1)
                for_slots(dve, n, slot)
                hold(dve, step, n, dve_on3)
                dve.sem_clear(step)
                nc.vector.scalar_tensor_tensor(y[r], acc, rden[u], mine[r][:, C:2 * C], ALU.mult, ALU.add).then_inc(step, 1)
                dve.wait_ge(step, 1)
                nc.vector.bn_stats(st[:, 6 * r:6 * r + 6], y[r]).then_inc(step, 1)
                dve.wait_ge(step, 2)
                nc.vector.bn_aggr(mv[:, 2 * r:2 * r + 2], st[:, 6 * r:6 * r + 6]).then_inc(step, 1)
                dve.wait_ge(step, 3)

            def set_home(g, r, first):
                if not first:
                    dve.wait_ge(out_done[r], 16 * g)
                nc.vector.tensor_copy(home[r], info[r][:, K:K + 1]).then_inc(home_set, 1)
                dve.wait_ge(home_set, RING * g + r + 1)
                dve.sem_inc(tile_done, 1)

            def finish(g, first):
                dve.wait_ge(std3, g + 1)
                nc.vector.reciprocal(rstd, std).then_inc(fin, 1)
                dve.wait_ge(fin, g + 3)
                for r in R:
                    if not first:
                        dve.wait_ge(out_done[r], 16 * g)
                    nc.vector.tensor_scalar(o[r], y[r], mv[:, 2 * r:2 * r + 1], rstd[:, r:r + 1], ALU.subtract, ALU.mult).then_inc(out_ready, 1)

            def group(g, first, second=False):
                for r in R:
                    n = scores(g, r)
                    if r == 0 and not first:
                        finish(g - 1, second)
                    rows(g, r, n)
                    set_home(g, r, first)
                nc.vector.tensor_scalar(veps, mv[:, 1:2 * RING:2], EPS, None, ALU.add).then_inc(var3, 1)

            group(0, True)
            group(1, False, True)
            with dve.Fori(2, GROUPS) as g:
                group(g, False)
            finish(GROUPS - 1, False)


def part_four(nc, ctx, io, mem):
    sem = lambda name: ctx.enter_context(nc.semaphore(name))
    A, bank = mem["A"], mem["bank"]
    at = [0]

    def carve(cols):
        a = at[0]
        at[0] += cols
        return A[:, a:a + cols]

    qrow, krow, xrow, qT, kT = (carve(N) for _ in range(5))
    H, kcol = [carve(N) for _ in range(2)], [carve(1) for _ in range(2)]
    adj, mask, scT, masked, att, attT = (carve(N) for _ in range(6))
    pcol, nmax, den, rden, veps, std, rstd = (carve(1) for _ in range(7))
    st, mv, y, o = carve(6), carve(2), carve(C), carve(C)
    tb, sb_, ab, yb = bank[0:2], bank[2:4], bank[4:6], bank[6]

    d_in = sem("d_in")
    d_adj = sem("d_adj")
    d_out = sem("d_out")
    d_rowT = sem("d_rowT")
    d_colT = sem("d_colT")
    d_k = sem("d_k")
    d_h = sem("d_h")
    d_s = sem("d_s")
    d_sT = sem("d_sT")
    d_sc = sem("d_sc")
    d_m = sem("d_m")
    d_mx = sem("d_mx")
    d_e = sem("d_e")
    d_eT = sem("d_eT")
    d_w = sem("d_w")
    d_y = sem("d_y")
    d_v = sem("d_v")
    d_r = sem("d_r")
    d_o = sem("d_o")
    block = ctx.enter_context(nc.Block())
    qx = io["qx"][0:NODES, :].rearrange("(b t p) c -> b p t c", b=B, p=P)
    kx = io["kx"].rearrange("(b t p) c -> b p t c", b=B, p=P)
    adj4 = io["adj"].rearrange("b (t p) m -> b t p m", p=P)
    dve_on4 = sem("dve_on4")

    @block.sync
    def _(sp):
        full = sp.value_load(mem["full"][0:1, 0:1], min_val=0, max_val=NODES)
        with sp.If(full > 0):
            with nc.allow_non_contiguous_dma(reason="one column"):
                sp.dma_start(pcol, io["p"].rearrange("(c o) -> c o", o=1)).then_inc(d_in, 16)

            def graph(b, first):
                if not first:
                    sp.wait_ge(d_o, MT * b)
                for dst, src, c in ((qrow, qx, 0), (krow, kx, 0), (xrow, qx, C)):
                    sp.dma_start(dst.rearrange("p (t c) -> p t c", c=C), src[ds(b, 1), :, :, c:c + C].rearrange("o p t c -> p (o t) c")).then_inc(d_in, 16)

                def load(t):
                    sp.dma_start(adj, adj4[ds(b, 1), ds(t, 1)].rearrange("o u p m -> (o u p) m")).then_inc(d_adj, 16)

                def store(t):
                    sp.wait_ge(d_o, MT * b + t + 1)
                    sp.dma_start(io["out"][ds(b * N + t * P, P), :], o).then_inc(d_out, 16)
                load(0)
                with sp.Fori(0, MT - 1) as t:
                    store(t)
                    load(t + 1)
                store(MT - 1)
            graph(0, True)
            with sp.Fori(1, B) as b:
                graph(b, False)
            sp.wait_ge(d_out, 16 * TILES)

    @block.tensor
    def _(pe):
        full = pe.value_load(mem["full"][0:1, 0:1], min_val=0, max_val=NODES)
        with pe.If(full > 0):
            with pe.Fori(0, B) as b:
                pe.wait_ge(d_in, 48 * b + 64)
                for i in range(4):
                    if i >= 2:
                        pe.wait_ge(d_colT, 4 * b + i - 1)
                    for t in range(QH):
                        m = (i % 2) * QH + t
                        last = nc.tensor.transpose(tb[i % 2][:, t * P:(t + 1) * P], (qrow, krow)[i // 2][:, m * C:(m + 1) * C], mem["ident"][:, :])
                    last.then_inc(d_rowT, 1)
                with pe.Fori(0, MT) as t:
                    tile = MT * b + t
                    with pe.Fori(0, P // 2) as i:
                        for u in range(2):
                            pe.wait_ge(d_h, P * tile + 2 * i + u + 1)
                            for j in range(MT):
                                last = nc.tensor.matmul(sb_[j // QH][:, ds(2 * i + u + (j % QH) * P, 1)], H[u][:, j * P:(j + 1) * P], pcol, start=True, stop=True)
                            last.then_inc(d_s, 1)
                    for q in range(2):
                        pe.wait_ge(d_sT, 2 * tile + q + 1)
                        for j in range(QH):
                            last = nc.tensor.transpose(tb[q][:, j * P:(j + 1) * P], scT[:, (q * QH + j) * P:(q * QH + j + 1) * P], mem["ident"][:, :])
                        last.then_inc(d_sc, 1)
                    pe.wait_ge(d_e, tile + 1)
                    for q in range(2):
                        for j in range(QH):
                            last = nc.tensor.transpose(ab[q][:, j * P:(j + 1) * P], att[:, (q * QH + j) * P:(q * QH + j + 1) * P], mem["ident"][:, :])
                        last.then_inc(d_eT, 1)
                    for j in range(MT):
                        if j % QH == 0:
                            pe.wait_ge(d_w, 2 * tile + j // QH + 1)
                        last = nc.tensor.matmul(yb[:, 0:C], attT[:, j * P:(j + 1) * P], xrow[:, j * C:(j + 1) * C], start=(j == 0), stop=(j == MT - 1))
                    last.then_inc(d_y, 1)

    @block.scalar
    def _(act):
        full = act.value_load(mem["full"][0:1, 0:1], min_val=0, max_val=NODES)
        with act.If(full > 0):
            with act.Fori(0, B) as b:
                for i in range(4):
                    act.wait_ge(d_rowT, 4 * b + i + 1)
                    nc.scalar.activation((qT, kT)[i // 2][:, (i % 2) * HALF:(i % 2 + 1) * HALF], tb[i % 2][:, :], ACT.Copy).then_inc(d_colT, 1)
                with act.Fori(0, MT) as t:
                    tile = MT * b + t
                    act.wait_ge(d_s, P * (tile + 1))
                    for q in range(2):
                        nc.scalar.activation(scT[:, q * HALF:(q + 1) * HALF], sb_[q][:, :], ACT.Copy).then_inc(d_sT, 1)
                    act.wait_ge(d_mx, tile + 1)
                    nc.scalar.activation(att, masked, ACT.Exp, bias=nmax, accum_out=den).then_inc(d_e, 1)
                    for q in range(2):
                        act.wait_ge(d_eT, 2 * tile + q + 1)
                        nc.scalar.activation(attT[:, q * HALF:(q + 1) * HALF], ab[q][:, :], ACT.Copy).then_inc(d_w, 1)
                    act.wait_ge(d_v, tile + 1)
                    nc.scalar.activation(std, veps, ACT.Sqrt).then_inc(d_r, 1)

    @block.vector
    def _(dve):
        full = dve.value_load(mem["full"][0:1, 0:1], min_val=0, max_val=NODES)
        with dve.If(full > 0):
            def node(tile, t, i, u, first):
                n = P * tile + 2 * i + u
                if not first:
                    dve.wait_ge(d_s, n - 1)
                nc.vector.tensor_copy(kcol[u], kT[:, ds(t * P + 2 * i + u, 1)]).then_inc(d_k, 1)
                dve.wait_ge(d_k, n + 1)
                nc.vector.tensor_scalar(H[u], qT, kcol[u], 0.0, ALU.add, ALU.max).then_inc(d_h, 1)

            def tile_of(b, t, first_out):
                tile = MT * b + t
                dve.sem_clear(d_m)

                def step(ins, n):
                    ins.then_inc(d_m, 1)
                    dve.wait_ge(d_m, n)
                dve.wait_ge(d_adj, 16 * (tile + 1))
                step(nc.vector.tensor_scalar(mask, adj, 0.0, -NEG, ALU.is_gt, ALU.mult), 1)
                for q in range(2):
                    half = slice(q * HALF, (q + 1) * HALF)
                    dve.wait_ge(d_sc, 2 * tile + q + 1)
                    step(nc.vector.scalar_tensor_tensor(masked[:, half], mask[:, half], NEG, tb[q][:, :], ALU.add, ALU.add), 2 + q)
                step(nc.vector.tensor_reduce(nmax, masked, AX.X, ALU.max), 4)
                nc.vector.tensor_scalar(nmax, nmax, -1.0, None, ALU.mult).then_inc(d_mx, 1)
                dve.wait_ge(d_y, tile + 1)
                step(nc.vector.reciprocal(rden, den), 5)
                step(nc.vector.scalar_tensor_tensor(y, yb[:, 0:C], rden, xrow[:, ds(t * C, C)], ALU.mult, ALU.add), 6)
                step(nc.vector.bn_stats(st, y), 7)
                step(nc.vector.bn_aggr(mv, st), 8)
                nc.vector.tensor_scalar(veps, mv[:, 1:2], EPS, None, ALU.add).then_inc(d_v, 1)
                dve.wait_ge(d_r, tile + 1)
                step(nc.vector.reciprocal(rstd, std), 9)
                if not first_out:
                    dve.wait_ge(d_out, 16 * tile)
                nc.vector.tensor_scalar(o, y, mv[:, 0:1], rstd, ALU.subtract, ALU.mult).then_inc(d_o, 1)

            def whole(b, t, first):
                if first:
                    for u in range(2):
                        node(0, 0, 0, u, True)
                    with dve.Fori(1, P // 2) as i:
                        for u in range(2):
                            node(0, 0, i, u, False)
                else:
                    with dve.Fori(0, P // 2) as i:
                        for u in range(2):
                            node(MT * b + t, t, i, u, False)
                tile_of(b, t, first)

            dve.wait_ge(d_colT, 4)
            whole(0, 0, True)
            with dve.Fori(1, MT) as t:
                whole(0, t, False)
            with dve.Fori(1, B) as b:
                hold(dve, d_colT, 4 * b + 4, dve_on4)
                with dve.Fori(0, MT) as t:
                    whole(b, t, False)


def program(nc, io):
    ctx = ExitStack()
    with ctx:
        sb = lambda name, cols, dt=f32: ctx.enter_context(nc.sbuf_tensor(name, [P, cols], dt))
        mem = {
            "bank": [ctx.enter_context(nc.psum_tensor(f"bank{i}", [P, HALF], f32)) for i in range(8)],
            "A": sb("A", (2 * RES + 2) * UNIT), "hT": sb("hT", NODES), "hst": sb("hst", N), "hws": sb("hws", N),
            "xs": sb("xs", N), "nat": [sb(f"nat{k}", N) for k in range(QH)], "W": sb("W", LAYERS * C),
            "vec": sb("vec", 3 * LAYERS), "ident": sb("ident", P), "iota": sb("iota", N, f16),
            "key": [sb(f"key{k}", N, f16) for k in range(2)], "top": [sb(f"top{k}", K, f16) for k in range(2)],
            "keys": sb("keys", TILES * K, f16), "bcol": sb("bcol", 1), "st": sb("st", 6 * CHUNKS), "bn": sb("bn", 8),
            "own": sb("own", TILES, i32), "tmpi": sb("tmpi", TILES, i32), "graph0": sb("graph0", TILES),
            "tomean": sb("tomean", TILES), "classes": sb("classes", K), "rank0": sb("rank0", TILES), "slot": sb("slot", K),
            "ones": sb("ones", P), "below": sb("below", P), "cnt": sb("cnt", TILES), "ranki": sb("ranki", TILES, i32),
            "slots": sb("slots", TILES, i32), "arrive": sb("arrive", TILES, i32), "full": sb("full", 1, i32),
        }
        for part in (constants, part_one, part_two, part_three, part_four):
            with ExitStack() as own:
                if part is constants:
                    part(nc, own, mem)
                else:
                    part(nc, own, io, mem)


_NAMES = (("x", "x"), ("adj", "adj"), ("W", "L0_gnn_W"), ("b", "L0_gnn_b"), ("gamma", "L0_gnn_gamma"), ("beta", "L0_gnn_beta"),
          ("WQ", "L1_gnn_WQ"), ("WK", "L1_gnn_WK"), ("p", "L1_gnn_p"))


def kernel(**inputs):
    import concourse.bacc as bacc
    from concourse.bass_utils import run_bass_kernel_spmd

    nc = bacc.Bacc("TRN2", target_bir_lowering=False, num_devices=1)
    io, arrays = {}, {}
    for short, name in _NAMES:
        a = np.ascontiguousarray(inputs[name])
        arrays[f"in_{short}"] = a
        io[short] = nc.dram_tensor(f"in_{short}", a.shape, mybir.dt.from_np(a.dtype), kind="ExternalInput").ap()
    io["adjT"] = nc.dram_tensor("adj_transposed", [STREAM, 2, P, UNIT], f32, kind="Internal").ap()
    io["qx"] = nc.dram_tensor("rows_qx", [NODES + B, 2 * C], f32, kind="Internal").ap()
    io["kx"] = nc.dram_tensor("rows_kx", [NODES, 2 * C], f32, kind="Internal").ap()
    io["lists"] = nc.dram_tensor("lists", [NODES, K + 2], i32, kind="Internal").ap()
    io["out"] = nc.dram_tensor("out", [NODES, C], f32, kind="ExternalOutput").ap()
    program(nc, io)
    result = run_bass_kernel_spmd(nc, [arrays], core_ids=[0])
    return result.results[0]["out"].reshape(B, N, C)
```

```python
from contextlib import ExitStack

import numpy as np

import concourse.bass as bass
from concourse import mybir
from concourse.alu_op_type import AluOpType as ALU

ACT = mybir.ActivationFunctionType
AX = mybir.AxisListType
f32, f16, i32 = mybir.dt.float32, mybir.dt.float16, mybir.dt.int32
ds = bass.ds

P = 128
B, N, C = 8, 1024, 128
LAYERS = 4
MT = N // P
NODES = B * N
TILES = NODES // P
HALF = N // 2
QH = MT // 2
CHUNKS = 2 * B
RES = 3
STREAM = B - RES
UNIT = MT * HALF
SUB = UNIT // 2
RING = 4
GROUPS = TILES // RING
QUAD = 4
K = 24
ROUNDS = K // 8
EPS = 1e-5
NEG = -1e22
LIST, OWN, CNT, SELF, ROW = 3 * C, 3 * C + K, 3 * C + K + 1, 3 * C + K + 2, 3 * C + K + 4
INFO = ROW - LIST


def hold(eng, sem, value, passed):
    eng.wait_ge(sem, value)
    eng.sem_inc(passed, 1)


def load_values(nc, eng, words, least, most):
    _, values = nc.values_load_multi_w_load_instructions(words, engines=[eng.engine], min_val=least, max_val=most)
    return values


def later_tile(L, b, h):
    return 3 * B + CHUNKS * (L - 1) + 2 * b + h


def part_one(nc, ctx, io, mem):
    sem = lambda name: ctx.enter_context(nc.semaphore(name))
    bank = mem["bank"]
    tp, hwp, acc = bank[0:4], bank[4:6], bank[6:8]
    A, hT, hst, hws, xs, nat = mem["A"], mem["hT"], mem["hst"], mem["hws"], mem["xs"], mem["nat"]
    ring = [mem["A"][:, (2 * RES + h) * UNIT:(2 * RES + h + 1) * UNIT] for h in range(2)]
    x3 = io["x"].rearrange("b (t p) c -> b p t c", p=P)
    adj4 = io["adj"].rearrange("b (t p) m -> b t p m", p=P)
    adjT = io["adjT"]

    const_ready = sem("const_ready")
    par_in = sem("par_in")
    x_in = sem("x_in")
    nat_in = [sem(f"nat_in{k}") for k in range(QH)]
    again_in = [sem(f"again_in{h}") for h in range(2)]
    xT_full = sem("xT_full")
    hst_ready = sem("hst_ready")
    hw_full = sem("hw_full")
    hws_ready = sem("hws_ready")
    tp_full = sem("tp_full")
    tp_free = sem("tp_free")
    acc_full = sem("acc_full")
    r_ready = sem("r_ready")
    store_done = [sem(f"store_done{h}") for h in range(2)]
    ring_in = [sem(f"ring_in{i}") for i in range(4)]
    ring_used = sem("ring_used")
    stats = sem("stats")
    norm = sem("norm")
    var_ready = sem("var_ready")
    std_ready = sem("std_ready")
    mask_done = sem("mask_done")
    key_ready = sem("key_ready")
    ext = sem("ext")
    sp_on, pool_on, dve_on = sem("sp_on"), sem("pool_on"), sem("dve_on")
    ext_done = sem("ext_done")
    const_act = sem("const_act")
    diag_in = sem("diag_in")
    rank = sem("rank")
    cls_ready = sem("cls_ready")
    cls_full = sem("cls_full")

    NORM_STEPS = 6

    block = ctx.enter_context(nc.Block())

    def each_graph(eng, resident, streamed):
        with eng.Fori(0, RES) as b:
            resident(b)
        with eng.Fori(RES, B) as b:
            streamed(b)

    @block.sync
    def _(sp):
        sp.dma_start(mem["W"][:, :].rearrange("p (l c) -> p l c", l=LAYERS), io["W"].rearrange("l i c -> i l c")).then_inc(par_in, 16)
        for name, col in (("b", 0), ("gamma", 1), ("beta", 2)):
            with nc.allow_non_contiguous_dma(reason="the small vectors, once"):
                sp.dma_start(mem["vec"][:, col * LAYERS:(col + 1) * LAYERS], io[name].rearrange("l c -> c l")).then_inc(par_in, 16)
        def loads(b, first):
            if not first:
                sp.wait_ge(xT_full, 2 * b)
            sp.dma_start(xs[:, :].rearrange("p (t c) -> p t c", t=MT), x3[ds(b, 1)].rearrange("o p t c -> p (o t) c")).then_inc(x_in, 16)
            for h in range(2):
                for k in range(QH):
                    if not (first and h == 0):
                        hold(sp, tp_full, 8 * (2 * b + h - 1) + 2 * k + 2, sp_on)
                        if k == 0 or (k == 1 and h == 1):
                            hold(sp, key_ready, 3 * b + h + k, sp_on)
                    sp.dma_start(nat[k][:, :], adj4[ds(b, 1), h * QH + k].rearrange("o p m -> (o p) m")).then_inc(nat_in[k], 16)
        loads(0, True)
        with nc.allow_non_contiguous_dma(reason="the diagonal, once"):
            for b in range(B):
                sp.dma_start(mem["diag"][:, b * MT:(b + 1) * MT], diagonal(io["adj"], b)).then_inc(diag_in, 16)
        with sp.Fori(1, B) as b:
            loads(b, False)
        sp.wait_ge(acc_full, CHUNKS)
        for h in range(2):
            sp.wait_ge(store_done[h], 16 * STREAM)
        def stream(L, b, first):
            for h in range(2):
                for q in range(2):
                    if first and q == 0:
                        if not isinstance(L, int):
                            sp.wait_ge(ring_used, 2 * STREAM * (L - 1) - 1 + h)
                    elif q == 0:
                        sp.wait_ge(ring_used, 2 * STREAM * (L - 1) + 2 * (b - RES) + h - 1)
                    elif first:
                        if not isinstance(L, int):
                            sp.wait_ge(acc_full, CHUNKS * L - 1 + h)
                    else:
                        sp.wait_ge(acc_full, CHUNKS * L + 2 * (b - 1) + h + 1)
                    sp.dma_start(ring[h][:, q * SUB:(q + 1) * SUB],
                                 adjT[ds(b - RES, 1), h, :, q * SUB:(q + 1) * SUB].rearrange("o p e -> (o p) e")).then_inc(ring_in[2 * h + q], 16)
        stream(1, RES, True)
        with sp.Fori(RES + 1, B) as b:
            stream(1, b, False)
        with sp.Fori(2, LAYERS) as L:
            stream(L, RES, True)
            with sp.Fori(RES + 1, B) as b:
                stream(L, b, False)

    @block.gpsimd
    def _(pool):
        pool.memset(mem["ident"][:, :], 0.0).then_inc(const_ready, 1)
        pool.wait_ge(const_ready, 1)
        pool.affine_select(out=mem["ident"][:, :], in_=mem["ident"][:, :], compare_op=ALU.not_equal, fill=1.0,
                           base=0, pattern=[[-1, P]], channel_multiplier=1).then_inc(const_ready, 1)
        pool.iota(mem["hst"][:, :].bitcast(i32), pattern=[[1, N]], base=1, channel_multiplier=0).then_inc(const_ready, 1)
        pool.wait_ge(const_ready, 3)
        pool.tensor_copy(mem["iota"][:, :], mem["hst"][:, :].bitcast(i32)).then_inc(const_ready, 1)
        pool.wait_ge(const_ready, 4)

        def make_key(e, slot, buffer, tile, used):
            if used is not None:
                hold(pool, ext_done, used, pool_on)
            key = mem["key"][buffer]
            pool.tensor_scalar(key[:, :], nat[slot][:, :], 0.0, None, ALU.is_gt).then_inc(mask_done, 1)
            pool.wait_ge(mask_done, 2 * e + 1)
            pool.tensor_tensor(key[:, :], key[:, :], mem["iota"][:, :], ALU.mult).then_inc(mask_done, 1)
            pool.wait_ge(mask_done, 2 * e + 2)
            own = key[:, ds(tile * P, P)]
            pool.tensor_tensor(own, own, mem["others"][:, :], ALU.mult).then_inc(key_ready, 1)

        def layer0(b, first):
            for i, (h, slot) in enumerate(((0, 0), (0, 1), (1, 0))):
                hold(pool, nat_in[slot], 16 * (2 * b + h + 1), pool_on)
                make_key(3 * b + i, slot, i, h * QH + slot, None if first else 3 * b + i - 2)
        layer0(0, True)
        with pool.Fori(1, B) as b:
            layer0(b, False)
        pool.wait_ge(tp_full, 8 * CHUNKS)

        def fetch(L, b, h, rest=False):
            src = adj4[ds(2 * b + h, 1), QH + 1:QH + 2] if rest else adj4[ds(b, 1), ds(h * QH + L + 1, 1)]
            pool.dma_start(nat[h], src.rearrange("o u p m -> (o u p) m")).then_inc(again_in[h], 16)

        def keys(L, b, h, rest=False):
            hold(pool, again_in[h], 16 * (B * (L - 1) + b + 1), pool_on)
            e = later_tile(L, b, h)
            make_key(e, h, h, QH + 1 if rest else h * QH + L + 1, e - 1)
            pool.wait_ge(key_ready, e + 1)
        pool.wait_ge(key_ready, 3 * B)
        for h in range(2):
            fetch(1, 0, h)
        for L in (1, 2):
            with pool.Fori(0, B - 1) as b:
                for h in range(2):
                    keys(L, b, h)
                    fetch(L, b + 1, h)
            for h in range(2):
                keys(L, B - 1, h)
                fetch(L + 1, 0, h, rest=L == 2)
        with pool.Fori(0, B // 2 - 1) as b:
            for h in range(2):
                keys(3, b, h, rest=True)
                fetch(3, b + 1, h, rest=True)
        for h in range(2):
            keys(3, B // 2 - 1, h, rest=True)

    @block.tensor
    def _(pe):
        pe.wait_ge(const_ready, 4)
        pe.wait_ge(par_in, 64)

        def h_times_w(L, b, Wl):
            for q in range(2):
                pe.wait_ge(hst_ready, 2 * (B * L + b) + q + 1)
                for t in range(QH):
                    m = q * QH + t
                    last = nc.tensor.matmul(hwp[q][:, t * C:(t + 1) * C], hst[:, m * P:(m + 1) * P], Wl, start=True, stop=True)
                last.then_inc(hw_full, 1)

        def chunk(L, b, h, unit, first=False, ring_round=None):
            if not first:
                pe.wait_ge(r_ready, CHUNKS * L + 2 * b + h - 1)
            for q in range(2):
                if h == 0:
                    pe.wait_ge(hws_ready, 2 * (B * L + b) + q + 1)
                if ring_round is not None:
                    pe.wait_ge(ring_in[2 * h + q], 16 * ring_round)
                for t in range(QH):
                    m = q * QH + t
                    last = nc.tensor.matmul(acc[h][:, :], hws[:, m * C:(m + 1) * C], unit(m), start=(m == 0), stop=(m == MT - 1))
                if q == 0 and ring_round is not None:
                    last.then_inc(ring_used, 1)
            last.then_inc(acc_full, 1)

        def layer0(b, unit, first):
            pe.wait_ge(x_in, 16 * (b + 1))
            for q in range(2):
                for t in range(QH):
                    m = q * QH + t
                    last = nc.tensor.transpose(hwp[q][:, t * P:(t + 1) * P], xs[:, m * C:(m + 1) * C], mem["ident"][:, :])
                last.then_inc(xT_full, 1)
            h_times_w(0, b, mem["W"][:, 0:C])
            for h in range(2):
                for k in range(QH):
                    pe.wait_ge(nat_in[k], 16 * (2 * b + h + 1))
                    for q in range(2):
                        if not (first and h == 0 and k < 2):
                            pe.wait_ge(tp_free, 8 * (2 * b + h) + 2 * k + q - 3)
                        for t in range(QH):
                            m = q * QH + t
                            last = nc.tensor.transpose(tp[(2 * k + q) % 4][:, t * P:(t + 1) * P], nat[k][:, m * P:(m + 1) * P], mem["ident"][:, :])
                        last.then_inc(tp_full, 1)
                pe.wait_ge(tp_free, 8 * (2 * b + h) + 8)
                chunk(0, b, h, lambda m: unit(h, m), first=first)

        def resident(b):
            return lambda h, m: A[:, ds((2 * b + h) * UNIT + m * HALF, HALF)]
        def in_ring(h, m):
            return ring[h][:, m * HALF:(m + 1) * HALF]

        layer0(0, resident(0), True)
        with pe.Fori(1, RES) as b:
            layer0(b, resident(b), False)
        with pe.Fori(RES, B) as b:
            layer0(b, in_ring, False)
        def later_layer(L):
            with pe.Fori(0, RES) as b:
                h_times_w(L, b, mem["W"][:, ds(L * C, C)])
                for h in range(2):
                    chunk(L, b, h, lambda m: resident(b)(h, m))

            def streamed(b):
                h_times_w(L, b, mem["W"][:, ds(L * C, C)])
                for h in range(2):
                    chunk(L, b, h, lambda m: in_ring(h, m), ring_round=STREAM * (L - 1) + b - RES + 1)
            if isinstance(L, int):
                with pe.Fori(RES, B - 2) as b:
                    streamed(b)
                pe.wait_ge(cls_ready, 1)
                nc.tensor.matmul(tp[0][:, 0:K], mem["below"][:, :], mem["of_class"][:, :], start=True, stop=True)
                nc.tensor.matmul(tp[0][:, K:2 * K], mem["ones"][:, :], mem["of_class"][:, :], start=True, stop=True).then_inc(cls_full, 1)
                with pe.Fori(B - 2, B) as b:
                    streamed(b)
            else:
                with pe.Fori(RES, B) as b:
                    streamed(b)
        with pe.Fori(1, LAYERS - 1) as L:
            later_layer(L)
        later_layer(LAYERS - 1)

    @block.scalar
    def _(act):
        act.wait_ge(par_in, 64)

        def hw_out(L, b):
            for q in range(2):
                act.wait_ge(hw_full, 2 * (B * L + b) + q + 1)
                nc.scalar.activation(hws[:, q * HALF:(q + 1) * HALF], hwp[q][:, :], ACT.Copy).then_inc(hws_ready, 1)

        def relu(L, b, h):
            act.wait_ge(acc_full, CHUNKS * L + 2 * b + h + 1)
            nc.scalar.activation(hT[:, ds(b * N + h * HALF, HALF)], acc[h][:, :], ACT.Relu,
                                 bias=mem["bcol"][:, 0:1]).then_inc(r_ready, 1)

        def layer0(b, unit_at, first, stored):
            for q in range(2):
                act.wait_ge(xT_full, 2 * b + q + 1)
                if first:
                    act.wait_ge(const_ready, 4)
                nc.scalar.activation(hst[:, q * HALF:(q + 1) * HALF], hwp[q][:, :], ACT.Copy).then_inc(hst_ready, 1)
            hw_out(0, b)
            for h in range(2):
                if stored == 2:
                    act.wait_ge(store_done[h], 16 * (b - RES))
                for k in range(QH):
                    for q in range(2):
                        act.wait_ge(tp_full, 8 * (2 * b + h) + 2 * k + q + 1)
                        dst = unit_at(h, q).rearrange("p (m n) -> p m n", n=HALF)[:, :, k * P:(k + 1) * P]
                        nc.scalar.activation(dst, tp[(2 * k + q) % 4][:, :].rearrange("p (m n) -> p m n", n=P), ACT.Copy).then_inc(tp_free, 1)
                if stored:
                    act.wait_ge(tp_free, 8 * (2 * b + h) + 8)
                    act.dma_start(adjT[ds(b - RES, 1), h].rearrange("o p e -> (o p) e"), ring[h][:, :]).then_inc(store_done[h], 16)
                relu(0, b, h)

        def resident(b):
            return lambda h, q: A[:, ds((2 * b + h) * UNIT + q * SUB, SUB)]
        def in_ring(h, q):
            return ring[h][:, q * SUB:(q + 1) * SUB]

        def bias_of(L):
            nc.scalar.activation(mem["bcol"][:, 0:1], mem["vec"][:, ds(L, 1)], ACT.Copy).then_inc(const_act, 1)
            act.wait_ge(const_act, L + 1)

        bias_of(0)
        layer0(0, resident(0), True, 0)
        with act.Fori(1, RES) as b:
            layer0(b, resident(b), False, 0)
        layer0(RES, in_ring, False, 1)
        with act.Fori(RES + 1, B) as b:
            layer0(b, in_ring, False, 2)

        def root(L):
            act.wait_ge(var_ready, L + 1)
            nc.scalar.activation(mem["bn"][:, 3:4], mem["bn"][:, 2:3], ACT.Sqrt).then_inc(std_ready, 1)
        root(0)
        with act.Fori(1, LAYERS) as L:
            bias_of(L)
            with act.Fori(0, B) as b:
                hw_out(L, b)
                for h in range(2):
                    relu(L, b, h)
            root(L)

    @block.vector
    def _(dve):
        dve.wait_ge(par_in, 64)

        def extract(e, buffer, tile):
            key, top = mem["key"][buffer], mem["top"][buffer]
            dve.sem_clear(ext)
            hold(dve, key_ready, e + 1, dve_on)
            for r in range(ROUNDS):
                nc.vector.max(top[:, 8 * r:8 * r + 8], key[:, :]).then_inc(ext, 1)
                dve.wait_ge(ext, 2 * r + 1)
                if r < ROUNDS - 1:
                    nc.vector.match_replace(key[:, :], top[:, 8 * r:8 * r + 8], key[:, :], 0.0).then_inc(ext, 1)
                    dve.wait_ge(ext, 2 * r + 2)
            nc.vector.tensor_copy(mem["keys"][:, ds(tile * K, K)], top[:, :]).then_inc(ext_done, 1)

        def lists_beside(L, b, h):
            if isinstance(L, int) and L == 0:
                for i, tile in ((0, 0), (1, 1)) if h == 0 else ((2, QH),):
                    extract(3 * b + i, i, MT * b + tile)
            elif isinstance(L, int) and L == LAYERS - 1:
                if b < B // 2:
                    extract(later_tile(L, b, h), h, MT * (2 * b + h) + QH + 1)
            else:
                extract(later_tile(L, b, h), h, QH * (2 * b + h) + L + 1)

        def chunk_stats(L, b, h):
            dve.wait_ge(r_ready, CHUNKS * L + 2 * b + h + 1)
            nc.vector.bn_stats(mem["st"][:, ds((2 * b + h) * 6, 6)], hT[:, ds(b * N + h * HALF, HALF)]).then_inc(stats, 1)

        def norm_steps(L):
            bn, base = mem["bn"], NORM_STEPS * L
            hold(dve, stats, CHUNKS * (L + 1), dve_on)
            nc.vector.bn_aggr(bn[:, 0:2], mem["st"][:, :]).then_inc(norm, 1)
            dve.wait_ge(norm, base + 1)
            nc.vector.tensor_scalar(bn[:, 2:3], bn[:, 1:2], EPS, None, ALU.add).then_inc(var_ready, 1)
            dve.wait_ge(std_ready, L + 1)
            nc.vector.reciprocal(bn[:, 4:5], bn[:, 3:4]).then_inc(norm, 1)
            dve.wait_ge(norm, base + 2)
            nc.vector.tensor_tensor(bn[:, 5:6], bn[:, 4:5], mem["vec"][:, ds(LAYERS + L, 1)], ALU.mult).then_inc(norm, 1)
            dve.wait_ge(norm, base + 3)
            nc.vector.tensor_tensor(bn[:, 6:7], bn[:, 0:1], bn[:, 5:6], ALU.mult).then_inc(norm, 1)
            dve.wait_ge(norm, base + 4)
            nc.vector.tensor_tensor(bn[:, 7:8], mem["vec"][:, ds(2 * LAYERS + L, 1)], bn[:, 6:7], ALU.subtract).then_inc(norm, 2)
            dve.wait_ge(norm, base + 6)

        def affine(L, b):
            for q in range(2):
                dve.wait_ge(hw_full, 2 * (B * L + b) - 2 + q + 1)
                nc.vector.tensor_scalar(hst[:, q * HALF:(q + 1) * HALF], hT[:, ds(b * N + q * HALF, HALF)],
                                        mem["bn"][:, 5:6], mem["bn"][:, 7:8], ALU.mult, ALU.add).then_inc(hst_ready, 1)

        def graph(L, b, last):
            for h in range(2):
                if L != 0 and h == 1 and not last:
                    affine(L, b + 1)
                if not (last and h == 1):
                    lists_beside(L, b, h)
                chunk_stats(L, b, h)

        def turn(L):
            norm_steps(L)
            affine(L + 1, 0)
            lists_beside(L, B - 1, 1)

        with dve.Fori(0, B - 1) as b:
            graph(0, b, False)
        graph(0, B - 1, True)
        turn(0)
        for L in (1, 2):
            with dve.Fori(0, B - 1) as b:
                graph(L, b, False)
            graph(L, B - 1, True)
            turn(L)
        ranking = rank_nodes(nc, dve, mem, tp[0], rank, ext_done, diag_in, cls_ready, cls_full)
        for b in range(B):
            graph(LAYERS - 1, b, b == B - 1)
            for part in {3: (0, 1, 2), 5: (3,), 6: (4,)}.get(b, ()):
                ranking[part]()
        norm_steps(LAYERS - 1)


def diagonal(adj, b):
    a = adj[b]
    return bass.AP(tensor=a.tensor, offset=a.offset, ap=[[N + 1, P], [P * (N + 1), MT]])


def rank_nodes(nc, dve, mem, sums, rank, ext_done, diag_in, cls_ready, cls_full):
    count = [0]

    def link(ins):
        count[0] += 1
        ins.then_inc(rank, 1)
        dve.wait_ge(rank, count[0])

    E, small = mem["E"], mem["small"]
    info = E[:, 0:INFO * TILES].rearrange("p (t w) -> p t w", w=INFO)
    S = E[:, INFO * TILES:(INFO + K) * TILES]
    half = K * TILES // 2
    M, ones = (E[:, (INFO + K) * TILES + i * half:(INFO + K) * TILES + (i + 1) * half].bitcast(f16) for i in range(2))
    list_n, none, cnt, rankf, slotsf, cumf = (small[:, i * TILES:(i + 1) * TILES] for i in range(6))
    a = 6 * TILES
    last, incl, shift = small[:, a:a + K + 1], small[:, a + 32:a + 32 + K], small[:, a + 64:a + 64 + K]
    of_class = mem["of_class"][:, :]
    keys3 = mem["keys"][:, :].rearrange("p (t k) -> p t k", k=K)
    by_tile = lambda x: x.rearrange("p (t k) -> p t k", k=K)
    by_class = lambda x: x.rearrange("p (k t) -> p k t", t=TILES)
    over_k = lambda x: x.rearrange("p (t o) -> p t o", o=1).to_broadcast([P, TILES, K])
    over_t = lambda x: x.rearrange("p (k o) -> p k o", o=1).to_broadcast([P, K, TILES])
    v = nc.vector

    def lists():
        dve.wait_ge(ext_done, TILES)
        dve.wait_ge(diag_in, 16 * B)
        link(v.tensor_scalar(by_tile(M), keys3, 0.0, None, ALU.is_gt))
        link(v.tensor_reduce(list_n, by_tile(M), AX.X, ALU.add))
        link(v.tensor_scalar(none, mem["diag"][:, :], 0.0, None, ALU.is_gt))
        link(v.tensor_scalar(info[:, :, SELF - LIST], none, NEG, -NEG, ALU.mult, ALU.add))
        link(v.memset(info[:, :, SELF - LIST + 1], 0.0))
        link(v.tensor_tensor(none, none, list_n, ALU.add))
        link(v.tensor_scalar(none, none, 0.0, None, ALU.is_equal))
        link(v.tensor_tensor(cnt, list_n, none, ALU.add))
        link(v.tensor_tensor(none, none, mem["tomean"][:, :], ALU.mult))

    def rows():
        link(v.scalar_tensor_tensor(info[:, :, 0:K].bitcast(i32), keys3, 1.0, over_k(mem["graph0"][:, :]), ALU.max, ALU.add))
        link(v.tensor_tensor(info[:, :, 0].bitcast(i32), info[:, :, 0].bitcast(i32), none, ALU.add))
        link(v.tensor_copy(info[:, :, OWN - LIST].bitcast(i32), mem["own"][:, :]))
        link(v.tensor_copy(info[:, :, CNT - LIST], cnt))
        link(v.tensor_scalar(cnt, cnt, 1.0, None, ALU.max))
        link(v.tensor_tensor(by_class(M), cnt.rearrange("p (o t) -> p o t", o=1).to_broadcast([P, K, TILES]), over_t(mem["classes"][:, :]), ALU.is_equal))

    def classes():
        link(v.memset(ones, 1.0))
        link(v.tensor_tensor_scan(S, ones, M, 0.0, ALU.mult, ALU.add))
        link(v.memset(last[:, 0:1], 0.0))
        link(v.tensor_copy(last[:, 1:K + 1], by_class(S)[:, :, TILES - 1]))
        v.tensor_tensor(of_class, last[:, 1:K + 1], last[:, 0:K], ALU.subtract).then_inc(cls_ready, 1)

    def ranks():
        dve.wait_ge(cls_full, 1)
        link(v.tensor_copy(shift, sums[:, K:2 * K]))
        link(v.tensor_tensor_scan(incl, mem["ones"][:, 0:K], shift, 0.0, ALU.mult, ALU.add))
        link(v.tensor_tensor(shift, incl, shift, ALU.subtract))
        link(v.tensor_tensor(shift, sums[:, 0:K], shift, ALU.add))
        link(v.tensor_tensor(shift, shift, last[:, 0:K], ALU.subtract))
        link(v.tensor_tensor(by_class(S), by_class(S), over_t(shift), ALU.add))
        link(v.tensor_tensor(S, S, M, ALU.mult))
        link(v.tensor_reduce(rankf, S.rearrange("p (k t) -> p t k", t=TILES), AX.X, ALU.add))
        link(v.tensor_scalar(mem["ranki"][:, :], rankf, -1.0, None, ALU.add))

    def slots():
        plan = mem["plan"][:, :].rearrange("p (g w) -> p g w", w=2 * RING)
        link(v.tensor_tensor(by_tile(M), incl.rearrange("p (o k) -> p o k", o=1).to_broadcast([P, TILES, K]), over_k(mem["rank0"][:, :]), ALU.is_gt))
        link(v.tensor_reduce(slotsf, by_tile(M), AX.X, ALU.add))
        link(v.tensor_copy(plan[:, :, 0:RING], slotsf.rearrange("p (g r) -> p g r", r=RING)))
        for r in range(RING):
            link(v.tensor_tensor_scan(cumf[:, r:TILES:RING], mem["ones"][:, 0:TILES // RING], slotsf[:, r:TILES:RING], 0.0, ALU.mult, ALU.add))
        link(v.tensor_scalar(plan[:, :, RING:2 * RING], cumf.rearrange("p (g r) -> p g r", r=RING), 16.0, None, ALU.mult))
        link(v.tensor_scalar(mem["full"][:, :], incl[:, 0:1], 1.0, None, ALU.mult))

    return [lists, rows, classes, ranks, slots]


def constants(nc, ctx, mem):
    made = ctx.enter_context(nc.semaphore("made"))
    block = ctx.enter_context(nc.Block())

    @block.gpsimd
    def _(pool):
        count = [0]

        def link(ins):
            count[0] += 1
            ins.then_inc(made, 1)
            pool.wait_ge(made, count[0])

        tmp = mem["tmpi"]
        link(pool.iota(mem["own"][:, :], pattern=[[P, TILES]], base=0, channel_multiplier=1))
        link(pool.iota(tmp[:, 0:TILES].rearrange("p (b t) -> p b t", b=B), pattern=[[N, B], [0, MT]], base=-1, channel_multiplier=0))
        link(pool.tensor_copy(mem["graph0"][:, :], tmp[:, 0:TILES]))
        link(pool.iota(tmp[:, 0:TILES].rearrange("p (b t) -> p b t", b=B), pattern=[[1 - N, B], [0, MT]], base=NODES, channel_multiplier=0))
        link(pool.tensor_copy(mem["tomean"][:, :], tmp[:, 0:TILES]))
        link(pool.iota(tmp[:, 0:K], pattern=[[-1, K]], base=K, channel_multiplier=0))
        link(pool.tensor_copy(mem["classes"][:, :], tmp[:, 0:K]))
        turns = tmp[:, 0:TILES].rearrange("p (g h e) -> p g h e", h=RING // 2, e=2)
        for e in range(2):
            step = (1 - 2 * e) * P
            link(pool.iota(turns[:, :, :, e], pattern=[[step * RING // 2, GROUPS], [step, RING // 2]], base=e * (TILES - 1) * P, channel_multiplier=0))
        link(pool.tensor_copy(mem["rank0"][:, :], tmp[:, 0:TILES]))
        link(pool.iota(tmp[:, 0:K], pattern=[[1, K]], base=0, channel_multiplier=0))
        link(pool.tensor_copy(mem["slot"][:, :], tmp[:, 0:K]))
        link(pool.memset(mem["ones"][:, :], 1.0))
        link(pool.memset(mem["others"][:, :], 1.0))
        link(pool.affine_select(out=mem["others"][:, :], in_=mem["others"][:, :], compare_op=ALU.not_equal, fill=0.0,
                                base=0, pattern=[[-1, P]], channel_multiplier=1))
        link(pool.affine_select(out=mem["below"][:, :], in_=mem["ones"][:, :], compare_op=ALU.is_gt, fill=0.0,
                                base=0, pattern=[[1, P]], channel_multiplier=-1))


def part_two(nc, ctx, io, mem):
    sem = lambda name: ctx.enter_context(nc.semaphore(name))
    bank = mem["bank"]
    hp, xp, qp = bank[0:2], bank[2:4], bank[4:8]
    hT, hst, bn = mem["hT"], mem["hst"], mem["bn"]
    A = mem["A"]
    at = [0]

    def carve(cols):
        a = at[0]
        at[0] += cols
        return A[:, a:a + cols]

    z = [carve(N) for _ in range(2)]
    rows = [carve(ROW * MT) for _ in range(2)]
    rank_of = [carve(MT) for _ in range(2)]
    x1T = carve(N)
    wkq = carve(2 * C)
    st = carve(6 * MT)
    mv = carve(2 * MT)
    std, rstd, veps = carve(MT), carve(MT), carve(MT)
    xsum = carve(2 * B)
    xmean = carve(B)
    means = carve(2 * C)
    row3 = [rows[u].rearrange("p (t w) -> p t w", w=ROW) for u in range(2)]
    x1_of = lambda u, m: rows[u][:, m * ROW + 2 * C:m * ROW + 3 * C]

    two_in = sem("two_in")
    xres_in = [sem(f"xres_in{u}") for u in range(2)]
    h_ready = sem("h_ready")
    hrow_full = sem("hrow_full")
    zst = sem("zst")
    var2 = sem("var2")
    std2 = sem("std2")
    dstep = sem("dstep")
    x1_ready = sem("x1_ready")
    x1T_full = sem("x1T_full")
    x1T_ready = sem("x1T_ready")
    kq_full = sem("kq_full")
    kq_ready = sem("kq_ready")
    tab_out = [sem(f"tab_out{u}") for u in range(2)]
    info_set = sem("info_set")
    placed = [sem(f"placed{u}") for u in range(2)]
    mean_full = sem("mean_full")
    mean_ready = sem("mean_ready")
    mean_rows = sem("mean_rows")
    mean_out = sem("mean_out")
    sp_on2, pool_on2 = sem("sp_on2"), sem("pool_on2")

    block = ctx.enter_context(nc.Block())
    qx = io["qx"][0:NODES, :].rearrange("(b t p) c -> b p t c", b=B, p=P)
    x3 = io["x"].rearrange("b (t p) c -> b p t c", p=P)

    @block.sync
    def _(sp):
        def load_x(b, u):
            sp.dma_start(z[u].rearrange("p (t c) -> p t c", c=C), x3[ds(b, 1)].rearrange("o p t c -> p (o t) c")).then_inc(xres_in[u], 16)

        def store(b, u):
            hold(sp, kq_ready, 4 * b + 4, sp_on2)
            sp.dma_start(qx[ds(b, 1)].rearrange("o p t c -> p (o t) c"), row3[u][:, :, C:3 * C]).then_inc(tab_out[u], 16)
        load_x(0, 0)
        load_x(1, 1)
        sp.dma_start(wkq[:, 0:C], io["WK"]).then_inc(two_in, 16)
        sp.dma_start(wkq[:, C:2 * C], io["WQ"]).then_inc(two_in, 16)
        with sp.Fori(0, B // 2 - 1) as i:
            for u in range(2):
                hold(sp, x1_ready, MT * (2 * i + u + 1), sp_on2)
                load_x(2 * i + u + 2, u)
                store(2 * i + u, u)
        for u in range(2):
            store(B - 2 + u, u)
        sp.wait_ge(mean_rows, 2)
        sp.dma_start(io["qx"][NODES:NODES + B, :], means[0:B, :]).then_inc(mean_out, 16)
        for u in range(2):
            sp.wait_ge(tab_out[u], 16 * (B // 2))
        sp.wait_ge(mean_out, 16)

    @block.gpsimd
    def _(pool):
        info = mem["E"][:, 0:INFO * TILES]

        def place(b, u, first):
            if not first:
                pool.wait_ge(placed[u], 16 * MT // 2 * (b - u))
            pool.tensor_copy(row3[u][:, :, LIST:ROW], info[:, ds(b * INFO * MT, INFO * MT)].rearrange("p (t w) -> p t w", w=INFO)).then_inc(info_set, 1)
            pool.tensor_copy(rank_of[u].bitcast(i32), mem["ranki"][:, ds(b * MT, MT)]).then_inc(info_set, 1)
            hold(pool, info_set, 2 * b + 2, pool_on2)
            for t in range(MT):
                if t == 0:
                    hold(pool, x1_ready, MT * (b + 1), pool_on2)
                if t % 2 == 0:
                    hold(pool, kq_ready, 4 * b + t // 2 + 1, pool_on2)
                pool.indirect_dma_start(io["sorted"], bass.IndirectOffsetOnAxis(ap=rank_of[u][:, t:t + 1].bitcast(i32), axis=0),
                                        rows[u][:, t * ROW:(t + 1) * ROW], None).then_inc(placed[u], 16)
        for u in range(2):
            place(u, u, True)
        with pool.Fori(1, B // 2) as i:
            for u in range(2):
                place(2 * i + u, u, False)
        for u in range(2):
            pool.wait_ge(placed[u], 16 * MT * B // 2)

    @block.vector
    def _(dve):
        def affine(b):
            for q in range(2):
                nc.vector.tensor_scalar(hst[:, q * HALF:(q + 1) * HALF], hT[:, ds(b * N + q * HALF, HALF)],
                                        bn[:, 5:6], bn[:, 7:8], ALU.mult, ALU.add).then_inc(h_ready, 1)

        def graph(b, u, first, last_one):
            dve.sem_clear(dstep)
            dve.wait_ge(xres_in[u], 8 * (b - u) + 16)
            for q in range(2):
                dve.wait_ge(hrow_full, 2 * b + q + 1)
                nc.vector.tensor_tensor(z[u][:, q * HALF:(q + 1) * HALF], hp[q][:, :], z[u][:, q * HALF:(q + 1) * HALF], ALU.add).then_inc(zst, 1)
            if not last_one:
                affine(b + 1)
            for t in range(MT):
                dve.wait_ge(zst, 2 * b + 1 + t // QH)
                nc.vector.bn_stats(st[:, 6 * t:6 * t + 6], z[u][:, t * C:(t + 1) * C]).then_inc(dstep, 1)
            for t in range(MT):
                dve.wait_ge(dstep, t + 1)
                nc.vector.bn_aggr(mv[:, 2 * t:2 * t + 2], st[:, 6 * t:6 * t + 6]).then_inc(dstep, 1)
            dve.wait_ge(dstep, 2 * MT)
            nc.vector.tensor_scalar(veps, mv[:, 1:2 * MT:2], EPS, None, ALU.add).then_inc(var2, 1)
            dve.wait_ge(std2, b + 1)
            nc.vector.reciprocal(rstd, std).then_inc(dstep, 1)
            dve.wait_ge(dstep, 2 * MT + 1)
            if not first:
                dve.wait_ge(tab_out[u], 8 * (b - u))
                dve.wait_ge(placed[u], 16 * MT // 2 * (b - u))
            for t in range(MT):
                nc.vector.tensor_scalar(x1_of(u, t), z[u][:, t * C:(t + 1) * C], mv[:, 2 * t:2 * t + 1], rstd[:, t:t + 1],
                                        ALU.subtract, ALU.mult).then_inc(x1_ready, 1)

        affine(0)
        for u in range(2):
            graph(u, u, True, False)
        with dve.Fori(1, B // 2 - 1) as i:
            for u in range(2):
                graph(2 * i + u, u, False, False)
        for u in range(2):
            graph(B - 2 + u, u, False, u == 1)
        dve.wait_ge(x1T_ready, 2 * B)
        dve.sem_clear(dstep)
        nc.vector.tensor_reduce(xmean, xsum.rearrange("p (b q) -> p b q", q=2), AX.X, ALU.add).then_inc(dstep, 1)
        dve.wait_ge(dstep, 1)
        nc.vector.tensor_scalar(xmean, xmean, 1.0 / N, None, ALU.mult).then_inc(mean_ready, 1)

    @block.tensor
    def _(pe):
        def rows_of_h(b):
            for q in range(2):
                pe.wait_ge(h_ready, 2 * b + q + 1)
                for t in range(QH):
                    m = q * QH + t
                    last = nc.tensor.transpose(hp[q][:, t * P:(t + 1) * P], hst[:, m * P:(m + 1) * P], mem["ident"][:, :])
                last.then_inc(hrow_full, 1)

        def project(b, u, first=False):
            for q in range(2):
                pe.wait_ge(x1_ready, MT * b + QH * (q + 1))
                for t in range(QH):
                    m = q * QH + t
                    last = nc.tensor.transpose(xp[q][:, t * P:(t + 1) * P], x1_of(u, m), mem["ident"][:, :])
                last.then_inc(x1T_full, 1)
            for j in range(4):
                if j % 2 == 0:
                    pe.wait_ge(x1T_ready, 2 * b + j // 2 + 1)
                if not first:
                    pe.wait_ge(kq_ready, 4 * b + j - 3)
                for t in range(2):
                    m = 2 * j + t
                    last = nc.tensor.matmul(qp[j][:, t * 2 * C:(t + 1) * 2 * C], x1T[:, m * P:(m + 1) * P], wkq, start=True, stop=True)
                last.then_inc(kq_full, 1)

        rows_of_h(0)
        rows_of_h(1)
        pe.wait_ge(two_in, 32)
        project(0, 0, True)
        with pe.Fori(0, B // 2 - 1) as i:
            rows_of_h(2 * i + 2)
            project(2 * i + 1, 1)
            rows_of_h(2 * i + 3)
            project(2 * i + 2, 0)
        project(B - 1, 1)
        pe.wait_ge(mean_ready, 1)
        nc.tensor.transpose(hp[0][0:B, 0:P], xmean, mem["ident"][:, :]).then_inc(mean_full, 1)

    @block.scalar
    def _(act):
        def root(b):
            act.wait_ge(var2, b + 1)
            nc.scalar.activation(std, veps, ACT.Sqrt).then_inc(std2, 1)

        def x1T_out(b):
            for q in range(2):
                act.wait_ge(x1T_full, 2 * b + q + 1)
                nc.scalar.activation(x1T[:, q * HALF:(q + 1) * HALF], xp[q][:, :], ACT.Copy,
                                     accum_out=xsum[:, ds(2 * b + q, 1)]).then_inc(x1T_ready, 1)

        def kq_out(b, u, first):
            if not first:
                act.wait_ge(tab_out[u], 8 * (b - u))
                act.wait_ge(placed[u], 16 * MT // 2 * (b - u))
            for j in range(4):
                act.wait_ge(kq_full, 4 * b + j + 1)
                nc.scalar.activation(row3[u][:, 2 * j:2 * j + 2, 0:2 * C], qp[j][:, :].rearrange("p (t c) -> p t c", t=2), ACT.Copy).then_inc(kq_ready, 1)

        root(0)
        for u in range(2):
            x1T_out(u)
            root(u + 1)
            kq_out(u, u, True)
        with act.Fori(1, B // 2 - 1) as i:
            for u in range(2):
                x1T_out(2 * i + u)
                root(2 * i + u + 1)
                kq_out(2 * i + u, u, False)
        x1T_out(B - 2)
        root(B - 1)
        kq_out(B - 2, 0, False)
        x1T_out(B - 1)
        kq_out(B - 1, 1, False)
        nc.scalar.activation(means[0:B, 0:C], mem["ident"][0:B, :], ACT.Copy).then_inc(mean_rows, 1)
        act.wait_ge(mean_full, 1)
        nc.scalar.activation(means[0:B, C:2 * C], hp[0][0:B, 0:P], ACT.Copy).then_inc(mean_rows, 1)


def part_three(nc, ctx, io, mem):
    sem = lambda name: ctx.enter_context(nc.semaphore(name))
    A = mem["A"]
    at = [0]

    def carve(cols):
        a = at[0]
        at[0] += cols
        return A[:, a:a + cols]

    R = range(RING)
    G = [carve((K + QUAD - 1) * 2 * C) for _ in R]
    mine = [mem["E"][:, v * ROW:(v + 1) * ROW] for v in range(2 * RING)]
    o = [carve(C) for _ in R]
    home = [carve(RING) for _ in range(2)]
    minus_p = carve(C)
    w_self = carve(C)
    w = [carve(QUAD * C) for _ in range(2)]
    score, mask = ([carve(K + 1) for _ in range(2)] for _ in range(2))
    masked, least = [carve(K + 1) for _ in R], [carve(1) for _ in R]
    wgt, own_wgt = [carve(K + 1) for _ in range(2)], [carve(1) for _ in range(2)]
    den = [carve(RING) for _ in range(2)]
    st, mv = carve(6 * RING), carve(2 * RING)
    veps, std, rstd = carve(RING), carve(RING), carve(RING)
    assert at[0] <= 2 * (RES + 1) * UNIT
    D = [mem["hT"][:, u * (K + 1) * P:(u + 1) * (K + 1) * P] for u in range(2)]
    acc = mem["bank"]
    plan = mem["plan"][0:1, :].rearrange("p (g w) -> p g w", w=2 * RING)

    p_in = sem("p_in")
    mine_in = [sem(f"mine_in{v}") for v in range(2 * RING)]
    slot_in = [sem(f"slot_in{r}") for r in R]
    tile_done = sem("tile_done")
    out_ready = sem("out_ready")
    out_done = [sem(f"out_done{r}") for r in R]
    step = sem("step")
    masked_ready = sem("masked_ready")
    wgt_set = sem("wgt_set")
    diag_ready = sem("diag_ready")
    acc_ready = sem("acc_ready")
    var3 = sem("var3")
    std3 = sem("std3")
    fin = sem("fin")
    cleared = sem("cleared")
    pool_on3, sp_on3 = sem("pool_on3"), sem("sp_on3")
    block = ctx.enter_context(nc.Block())

    def slots_of(eng, g):
        return load_values(nc, eng, plan[:, ds(g, 1), 0:RING], 1, K)

    def for_slots(eng, n, body):
        body(0)
        for s in range(1, 4):
            with eng.If(n > s):
                body(s)
        with eng.If(n > 4):
            body(4)
            for s in range(5, 8):
                with eng.If(n > s):
                    body(s)
            with eng.If(n > 8):
                body(8)
                for s in range(9, K):
                    with eng.If(n > s):
                        body(s)
                eng.nop()
            eng.nop()

    @block.sync
    def _(sp):
        full = sp.value_load(mem["full"][0:1, 0:1], min_val=0, max_val=NODES)
        with sp.If(full < 1):
            sp.dma_start(minus_p, io["p"].rearrange("(o c) -> o c", o=1).to_broadcast([P, C])).then_inc(p_in, 16)

            def load(i, v, first):
                front = RING * i + v // 2
                at = front if v % 2 == 0 else TILES - 1 - front
                if not first:
                    hold(sp, tile_done, 2 * RING * (i - 1) + v + 1, sp_on3)
                sp.dma_start(mine[v], io["sorted"][ds(at * P, P), :]).then_inc(mine_in[v], 16)
            for v in range(2 * RING):
                load(0, v, True)
            with sp.Fori(1, GROUPS // 2) as i:
                for v in range(2 * RING):
                    load(i, v, False)

    @block.gpsimd
    def _(pool):
        full = pool.value_load(mem["full"][0:1, 0:1], min_val=0, max_val=NODES)
        with pool.If(full < 1):
            def gathers(i, half, r, n, first):
                if not first:
                    hold(pool, acc_ready, RING * (2 * i + half - 1) + r + 1, pool_on3)
                v = RING * half + r
                hold(pool, mine_in[v], 16 * (i + 1), pool_on3)
                lists = mine[v][:, LIST:LIST + K].bitcast(i32)

                def slot(s):
                    pool.indirect_dma_start(G[r][:, s * 2 * C:(s + 1) * 2 * C], None, io["qx"],
                                            bass.IndirectOffsetOnAxis(ap=lists[:, s:s + 1], axis=0)).then_inc(slot_in[r], 16)
                if first and r % 2:
                    pool.wait_ge(cleared, r // 2 + 1)
                for_slots(pool, n, slot)

            def scatter(g, half, r):
                hold(pool, out_ready, RING * g + r + 1, pool_on3)
                pool.indirect_dma_start(io["out"], bass.IndirectOffsetOnAxis(ap=home[half][:, r:r + 1].bitcast(i32), axis=0), o[r], None).then_inc(out_done[r], 16)

            def group(i, half, scatters):
                n = slots_of(pool, 2 * i + half)
                for r in R:
                    gathers(i, half, r, n[r], isinstance(i, int) and i + half == 0)
                    if r == 0 and scatters:
                        for k in R:
                            scatter(2 * i + half - 2, half, k)

            for half in range(2):
                group(0, half, False)
            with pool.Fori(1, GROUPS // 2) as i:
                for half in range(2):
                    group(i, half, True)
            for r in R:
                scatter(GROUPS - 2, 0, r)
            for r in R:
                scatter(GROUPS - 1, 1, r)
            for r in R:
                pool.wait_ge(out_done[r], 16 * GROUPS)

    @block.scalar
    def _(act):
        full = act.value_load(mem["full"][0:1, 0:1], min_val=0, max_val=NODES)
        with act.If(full < 1):
            def weights(g, half, r, n, first):
                t, u = RING * g + r, r % 2
                d = den[half][:, r:r + 1]
                act.wait_ge(masked_ready, t + 1)
                nc.scalar.activation(wgt[u], masked[r], ACT.Exp, bias=least[r], scale=-1.0, accum_out=d).then_inc(wgt_set, 1)
                act.wait_ge(wgt_set, 2 * t + 1)
                nc.scalar.activation(own_wgt[u], wgt[u][:, K:K + 1], ACT.Identity, bias=d).then_inc(wgt_set, 1)

                if not first:
                    act.wait_ge(acc_ready, t - 1)

                def diag(s):
                    nc.scalar.activation(D[u][:, s * P:(s + 1) * P], mem["ident"][:, :], ACT.Copy, scale=wgt[u][:, s:s + 1])
                for_slots(act, n, diag)
                act.wait_ge(wgt_set, 2 * t + 2)
                nc.scalar.activation(D[u][:, K * P:(K + 1) * P], mem["ident"][:, :], ACT.Copy, scale=own_wgt[u]).then_inc(diag_ready, 1)

            def group(g, half, first):
                n = slots_of(act, g)
                for r in R:
                    weights(g, half, r, n[r], first and r < 2)
                    if r == 1 and not first:
                        root(g - 1)

            def root(g):
                act.wait_ge(var3, g + 1)
                nc.scalar.activation(std, veps, ACT.Sqrt).then_inc(std3, 1)

            group(0, 0, True)
            group(1, 1, False)
            with act.Fori(1, GROUPS // 2) as i:
                for half in range(2):
                    group(2 * i + half, half, False)
            root(GROUPS - 1)

    @block.tensor
    def _(pe):
        full = pe.value_load(mem["full"][0:1, 0:1], min_val=0, max_val=NODES)
        with pe.If(full < 1):
            def tile_sum(g, half, r, n):
                t, u = RING * g + r, r % 2
                out = acc[RING * half + r][:, 0:C]
                pe.wait_ge(diag_ready, t + 1)

                def slot(s):
                    nc.tensor.matmul(out, D[u][:, s * P:(s + 1) * P], G[r][:, s * 2 * C + C:(s + 1) * 2 * C], start=(s == 0), stop=False)
                for_slots(pe, n, slot)
                nc.tensor.matmul(out, D[u][:, K * P:(K + 1) * P], mine[RING * half + r][:, 2 * C:3 * C], start=False, stop=True).then_inc(acc_ready, 1)

            with pe.Fori(0, GROUPS // 2) as i:
                for half in range(2):
                    n = slots_of(pe, 2 * i + half)
                    for r in R:
                        tile_sum(2 * i + half, half, r, n[r])

    @block.vector
    def _(dve):
        full = dve.value_load(mem["full"][0:1, 0:1], min_val=0, max_val=NODES)
        with dve.If(full < 1):
            for u in range(2):
                nc.vector.memset(score[u], 0.0).then_inc(fin, 1)
            for r in range(1, RING, 2):
                nc.vector.memset(G[r], 0.0).then_inc(cleared, 1)
            n = slots_of(dve, 0)
            for r in range(0, RING, 2):
                nc.vector.tensor_scalar(G[r][:, ds(n[r] * 2 * C, (QUAD - 1) * 2 * C)], mem["ones"][:, 0:1].to_broadcast([P, (QUAD - 1) * 2 * C]), 0.0, None, ALU.mult).then_inc(fin, 1)
            dve.wait_ge(p_in, 16)
            nc.vector.tensor_scalar(minus_p, minus_p, -1.0, None, ALU.mult).then_inc(fin, 1)
            dve.wait_ge(fin, RING // 2 + 3)
            dve.wait_ge(cleared, RING // 2)

            def scores(g, half, r, n, arrive):
                u, v = r % 2, RING * half + r
                dve.sem_clear(step)
                dve.wait_ge(mine_in[v], 8 * (g - half) + 16)
                k = mine[v][:, 0:C]
                k_quad = mine[v][:, 0:C].rearrange("p (o c) -> p o c", o=1).to_broadcast([P, QUAD, C])

                def add_k(j):
                    q = G[r][:, j * QUAD * 2 * C:(j + 1) * QUAD * 2 * C].rearrange("p (s c) -> p s c", s=QUAD)[:, :, 0:C]
                    nc.vector.tensor_tensor(w[j % 2].rearrange("p (s c) -> p s c", s=QUAD), q, k_quad, ALU.add).then_inc(step, 1)

                def dot(row, s):
                    return nc.vector.scalar_tensor_tensor(row, row, 0.0, minus_p, ALU.max, ALU.mult, accum_out=score[u][:, s:s + 1])

                def quad(j):
                    for s in range(QUAD):
                        last = dot(w[j % 2][:, s * C:(s + 1) * C], j * QUAD + s)
                    last.then_inc(step, 1)

                def more(j):
                    with dve.If(n > QUAD * j):
                        add_k(j)
                        dve.wait_ge(step, 2 * j + 2)
                        quad(j)
                        dve.wait_ge(step, 2 * j + 3)
                        if (j + 1) * QUAD < K:
                            more(j + 1)
                        dve.nop()

                nc.vector.tensor_tensor(w_self, mine[v][:, C:2 * C], k, ALU.add).then_inc(step, 1)
                nc.vector.tensor_scalar(mask[u][:, 0:K], mem["slot"][:, :], mine[v][:, CNT:CNT + 1], -NEG, ALU.is_ge, ALU.mult)
                nc.vector.tensor_copy(mask[u][:, K:K + 1], mine[v][:, SELF:SELF + 1])
                dve.wait_ge(step, 1)
                dot(w_self, K)
                dve.wait_ge(slot_in[r], arrive)
                add_k(0)
                dve.wait_ge(step, 2)
                quad(0)
                dve.wait_ge(step, 3)
                more(1)
                dve.sem_clear(step)
                nc.vector.tensor_tensor_reduce(out=masked[r], in0=score[u], in1=mask[u], scale=1.0, scalar=-NEG * 10, op0=ALU.add, op1=ALU.min,
                                               accum_out=least[r]).then_inc(masked_ready, 1)

            def summed(g, half, r):
                t = RING * g + r
                dve.wait_ge(acc_ready, t + 1)
                nc.vector.tensor_copy(home[half][:, r:r + 1], mine[RING * half + r][:, OWN:OWN + 1]).then_inc(tile_done, 1)
                nc.vector.bn_stats(st[:, 6 * r:6 * r + 6], acc[RING * half + r][:, 0:C]).then_inc(step, 1)
                dve.wait_ge(step, 1)
                nc.vector.bn_aggr(mv[:, 2 * r:2 * r + 2], st[:, 6 * r:6 * r + 6])
                if r == RING - 1:
                    nc.vector.scalar_tensor_tensor(veps, den[half], EPS, den[half], ALU.mult, ALU.mult).then_inc(step, 1)
                    dve.wait_ge(step, 2)
                    nc.vector.tensor_tensor(veps, mv[:, 1:2 * RING:2], veps, ALU.add).then_inc(var3, 1)

            def finish(g, half, first):
                dve.wait_ge(std3, g + 1)
                nc.vector.reciprocal(rstd, std).then_inc(fin, 1)
                dve.wait_ge(fin, g + RING // 2 + 4)
                for r in R:
                    if not first:
                        dve.wait_ge(out_done[r], 16 * g)
                    nc.vector.tensor_scalar(o[r], acc[RING * half + r][:, 0:C], mv[:, 2 * r:2 * r + 1], rstd[:, r:r + 1], ALU.subtract, ALU.mult).then_inc(out_ready, 1)

            def group(g, half, stage):
                v = load_values(nc, dve, plan[:, ds(g, 1), :], 1, 16 * K * GROUPS)
                for r in R:
                    scores(g, half, r, v[r], v[RING + r])
                    if r < 2:
                        if stage > 0:
                            summed(g - 1, 1 - half, RING - 2 + r)
                    else:
                        if r == 2 and stage > 0:
                            finish(g - 1, 1 - half, stage == 1)
                        summed(g, half, r - 2)

            group(0, 0, 0)
            group(1, 1, 1)
            with dve.Fori(1, GROUPS // 2) as i:
                for half in range(2):
                    group(2 * i + half, half, 2)
            for r in (RING - 2, RING - 1):
                dve.sem_clear(step)
                summed(GROUPS - 1, 1, r)
            finish(GROUPS - 1, 1, False)


def part_four(nc, ctx, io, mem):
    sem = lambda name: ctx.enter_context(nc.semaphore(name))
    A, bank = mem["A"], mem["bank"]
    at = [0]

    def carve(cols):
        a = at[0]
        at[0] += cols
        return A[:, a:a + cols]

    qrow, xrow, qT, xT, kT = (carve(N) for _ in range(5))
    wk = carve(C)
    H, kcol = [carve(N) for _ in range(2)], [carve(1) for _ in range(2)]
    adj, mask, scT, masked, att, attT = (carve(N) for _ in range(6))
    pcol, nmax, den, rden, veps, std, rstd = (carve(1) for _ in range(7))
    st, mv, y, o = carve(6), carve(2), carve(C), carve(C)
    tb, sb_, ab, yb = bank[0:2], bank[2:4], bank[4:6], bank[6]

    d_in = sem("d_in")
    d_adj = sem("d_adj")
    d_out = sem("d_out")
    d_rowT = sem("d_rowT")
    d_colT = sem("d_colT")
    d_k = sem("d_k")
    d_h = sem("d_h")
    d_s = sem("d_s")
    d_sT = sem("d_sT")
    d_sc = sem("d_sc")
    d_m = sem("d_m")
    d_mx = sem("d_mx")
    d_e = sem("d_e")
    d_eT = sem("d_eT")
    d_w = sem("d_w")
    d_y = sem("d_y")
    d_v = sem("d_v")
    d_r = sem("d_r")
    d_o = sem("d_o")
    block = ctx.enter_context(nc.Block())
    qx = io["qx"][0:NODES, :].rearrange("(b t p) c -> b p t c", b=B, p=P)
    adj4 = io["adj"].rearrange("b (t p) m -> b t p m", p=P)
    dve_on4 = sem("dve_on4")

    @block.sync
    def _(sp):
        full = sp.value_load(mem["full"][0:1, 0:1], min_val=0, max_val=NODES)
        with sp.If(full > 0):
            with nc.allow_non_contiguous_dma(reason="one column"):
                sp.dma_start(pcol, io["p"].rearrange("(c o) -> c o", o=1)).then_inc(d_in, 16)
            sp.dma_start(wk, io["WK"]).then_inc(d_in, 16)

            def graph(b, first):
                if not first:
                    sp.wait_ge(d_o, MT * b)
                for dst, c in ((qrow, 0), (xrow, C)):
                    sp.dma_start(dst.rearrange("p (t c) -> p t c", c=C), qx[ds(b, 1), :, :, c:c + C].rearrange("o p t c -> p (o t) c")).then_inc(d_in, 16)

                def load(t):
                    sp.dma_start(adj, adj4[ds(b, 1), ds(t, 1)].rearrange("o u p m -> (o u p) m")).then_inc(d_adj, 16)

                def store(t):
                    sp.wait_ge(d_o, MT * b + t + 1)
                    sp.dma_start(io["out"][ds(b * N + t * P, P), :], o).then_inc(d_out, 16)
                load(0)
                with sp.Fori(0, MT - 1) as t:
                    store(t)
                    load(t + 1)
                store(MT - 1)
            graph(0, True)
            with sp.Fori(1, B) as b:
                graph(b, False)
            sp.wait_ge(d_out, 16 * TILES)

    @block.tensor
    def _(pe):
        full = pe.value_load(mem["full"][0:1, 0:1], min_val=0, max_val=NODES)
        with pe.If(full > 0):
            with pe.Fori(0, B) as b:
                pe.wait_ge(d_in, 32 * b + 64)
                for i in range(6):
                    if i >= 2:
                        pe.wait_ge(d_colT, 6 * b + i - 1)
                    if i >= 4:
                        last = nc.tensor.matmul(tb[i % 2][:, :], wk, xT[:, (i - 4) * HALF:(i - 3) * HALF], start=True, stop=True)
                    else:
                        for t in range(QH):
                            m = (i % 2) * QH + t
                            last = nc.tensor.transpose(tb[i % 2][:, t * P:(t + 1) * P], (qrow, xrow)[i // 2][:, m * C:(m + 1) * C], mem["ident"][:, :])
                    last.then_inc(d_rowT, 1)
                with pe.Fori(0, MT) as t:
                    tile = MT * b + t
                    with pe.Fori(0, P // 2) as i:
                        for u in range(2):
                            pe.wait_ge(d_h, P * tile + 2 * i + u + 1)
                            for j in range(MT):
                                last = nc.tensor.matmul(sb_[j // QH][:, ds(2 * i + u + (j % QH) * P, 1)], H[u][:, j * P:(j + 1) * P], pcol, start=True, stop=True)
                            last.then_inc(d_s, 1)
                    for q in range(2):
                        pe.wait_ge(d_sT, 2 * tile + q + 1)
                        for j in range(QH):
                            last = nc.tensor.transpose(tb[q][:, j * P:(j + 1) * P], scT[:, (q * QH + j) * P:(q * QH + j + 1) * P], mem["ident"][:, :])
                        last.then_inc(d_sc, 1)
                    pe.wait_ge(d_e, tile + 1)
                    for q in range(2):
                        for j in range(QH):
                            last = nc.tensor.transpose(ab[q][:, j * P:(j + 1) * P], att[:, (q * QH + j) * P:(q * QH + j + 1) * P], mem["ident"][:, :])
                        last.then_inc(d_eT, 1)
                    for j in range(MT):
                        if j % QH == 0:
                            pe.wait_ge(d_w, 2 * tile + j // QH + 1)
                        last = nc.tensor.matmul(yb[:, 0:C], attT[:, j * P:(j + 1) * P], xrow[:, j * C:(j + 1) * C], start=(j == 0), stop=(j == MT - 1))
                    last.then_inc(d_y, 1)

    @block.scalar
    def _(act):
        full = act.value_load(mem["full"][0:1, 0:1], min_val=0, max_val=NODES)
        with act.If(full > 0):
            with act.Fori(0, B) as b:
                for i in range(6):
                    act.wait_ge(d_rowT, 6 * b + i + 1)
                    nc.scalar.activation((qT, xT, kT)[i // 2][:, (i % 2) * HALF:(i % 2 + 1) * HALF], tb[i % 2][:, :], ACT.Copy).then_inc(d_colT, 1)
                with act.Fori(0, MT) as t:
                    tile = MT * b + t
                    act.wait_ge(d_s, P * (tile + 1))
                    for q in range(2):
                        nc.scalar.activation(scT[:, q * HALF:(q + 1) * HALF], sb_[q][:, :], ACT.Copy).then_inc(d_sT, 1)
                    act.wait_ge(d_mx, tile + 1)
                    nc.scalar.activation(att, masked, ACT.Exp, bias=nmax, accum_out=den).then_inc(d_e, 1)
                    for q in range(2):
                        act.wait_ge(d_eT, 2 * tile + q + 1)
                        nc.scalar.activation(attT[:, q * HALF:(q + 1) * HALF], ab[q][:, :], ACT.Copy).then_inc(d_w, 1)
                    act.wait_ge(d_v, tile + 1)
                    nc.scalar.activation(std, veps, ACT.Sqrt).then_inc(d_r, 1)

    @block.vector
    def _(dve):
        full = dve.value_load(mem["full"][0:1, 0:1], min_val=0, max_val=NODES)
        with dve.If(full > 0):
            def node(tile, t, i, u, first):
                n = P * tile + 2 * i + u
                if not first:
                    dve.wait_ge(d_s, n - 1)
                nc.vector.tensor_copy(kcol[u], kT[:, ds(t * P + 2 * i + u, 1)]).then_inc(d_k, 1)
                dve.wait_ge(d_k, n + 1)
                nc.vector.tensor_scalar(H[u], qT, kcol[u], 0.0, ALU.add, ALU.max).then_inc(d_h, 1)

            def tile_of(b, t, first_out):
                tile = MT * b + t
                dve.sem_clear(d_m)

                def step(ins, n):
                    ins.then_inc(d_m, 1)
                    dve.wait_ge(d_m, n)
                dve.wait_ge(d_adj, 16 * (tile + 1))
                step(nc.vector.tensor_scalar(mask, adj, 0.0, -NEG, ALU.is_gt, ALU.mult), 1)
                for q in range(2):
                    half = slice(q * HALF, (q + 1) * HALF)
                    dve.wait_ge(d_sc, 2 * tile + q + 1)
                    step(nc.vector.scalar_tensor_tensor(masked[:, half], mask[:, half], NEG, tb[q][:, :], ALU.add, ALU.add), 2 + q)
                step(nc.vector.tensor_reduce(nmax, masked, AX.X, ALU.max), 4)
                nc.vector.tensor_scalar(nmax, nmax, -1.0, None, ALU.mult).then_inc(d_mx, 1)
                dve.wait_ge(d_y, tile + 1)
                step(nc.vector.reciprocal(rden, den), 5)
                step(nc.vector.scalar_tensor_tensor(y, yb[:, 0:C], rden, xrow[:, ds(t * C, C)], ALU.mult, ALU.add), 6)
                step(nc.vector.bn_stats(st, y), 7)
                step(nc.vector.bn_aggr(mv, st), 8)
                nc.vector.tensor_scalar(veps, mv[:, 1:2], EPS, None, ALU.add).then_inc(d_v, 1)
                dve.wait_ge(d_r, tile + 1)
                step(nc.vector.reciprocal(rstd, std), 9)
                if not first_out:
                    dve.wait_ge(d_out, 16 * tile)
                nc.vector.tensor_scalar(o, y, mv[:, 0:1], rstd, ALU.subtract, ALU.mult).then_inc(d_o, 1)

            def whole(b, t, first):
                if first:
                    for u in range(2):
                        node(0, 0, 0, u, True)
                    with dve.Fori(1, P // 2) as i:
                        for u in range(2):
                            node(0, 0, i, u, False)
                else:
                    with dve.Fori(0, P // 2) as i:
                        for u in range(2):
                            node(MT * b + t, t, i, u, False)
                tile_of(b, t, first)

            dve.wait_ge(d_colT, 6)
            whole(0, 0, True)
            with dve.Fori(1, MT) as t:
                whole(0, t, False)
            with dve.Fori(1, B) as b:
                hold(dve, d_colT, 6 * b + 6, dve_on4)
                with dve.Fori(0, MT) as t:
                    whole(b, t, False)


def program(nc, io):
    ctx = ExitStack()
    with ctx:
        sb = lambda name, cols, dt=f32: ctx.enter_context(nc.sbuf_tensor(name, [P, cols], dt))
        mem = {
            "bank": [ctx.enter_context(nc.psum_tensor(f"bank{i}", [P, HALF], f32)) for i in range(8)],
            "A": sb("A", (2 * RES + 2) * UNIT), "hT": sb("hT", NODES), "hst": sb("hst", N), "hws": sb("hws", N),
            "E": sb("E", (QH + 1) * N), "W": sb("W", LAYERS * C),
            "vec": sb("vec", 3 * LAYERS), "ident": sb("ident", P), "iota": sb("iota", N, f16),
            "key": [sb(f"key{k}", N, f16) for k in range(3)], "top": [sb(f"top{k}", K, f16) for k in range(3)],
            "keys": sb("keys", TILES * K, f16), "bcol": sb("bcol", 1), "st": sb("st", 6 * CHUNKS), "bn": sb("bn", 8),
            "others": sb("others", P, f16), "diag": sb("diag", TILES), "small": sb("small", 6 * TILES + 96), "of_class": sb("of_class", K),
            "own": sb("own", TILES, i32),  "graph0": sb("graph0", TILES),
            "tomean": sb("tomean", TILES), "classes": sb("classes", K), "rank0": sb("rank0", TILES), "slot": sb("slot", K),
            "ones": sb("ones", P), "below": sb("below", P), "ranki": sb("ranki", TILES, i32),
            "plan": sb("plan", 2 * TILES, i32), "full": sb("full", 1, i32),
        }
        mem["nat"] = [mem["E"][:, k * N:(k + 1) * N] for k in range(QH)]
        mem["xs"] = mem["E"][:, QH * N:(QH + 1) * N]
        mem["tmpi"] = mem["E"][:, 0:TILES].bitcast(i32)
        for part in (constants, part_one, part_two, part_three, part_four):
            with ExitStack() as own:
                if part is constants:
                    part(nc, own, mem)
                else:
                    part(nc, own, io, mem)


_NAMES = (("x", "x"), ("adj", "adj"), ("W", "L0_gnn_W"), ("b", "L0_gnn_b"), ("gamma", "L0_gnn_gamma"), ("beta", "L0_gnn_beta"),
          ("WQ", "L1_gnn_WQ"), ("WK", "L1_gnn_WK"), ("p", "L1_gnn_p"))


def kernel(**inputs):
    import concourse.bacc as bacc
    from concourse.bass_utils import run_bass_kernel_spmd

    nc = bacc.Bacc("TRN2", target_bir_lowering=False, num_devices=1)
    io, arrays = {}, {}
    for short, name in _NAMES:
        a = np.ascontiguousarray(inputs[name])
        arrays[f"in_{short}"] = a
        io[short] = nc.dram_tensor(f"in_{short}", a.shape, mybir.dt.from_np(a.dtype), kind="ExternalInput").ap()
    io["adjT"] = nc.dram_tensor("adj_transposed", [STREAM, 2, P, UNIT], f32, kind="Internal").ap()
    io["qx"] = nc.dram_tensor("rows_qx", [NODES + B, 2 * C], f32, kind="Internal").ap()
    io["sorted"] = nc.dram_tensor("rows_sorted", [NODES, ROW], f32, kind="Internal").ap()
    io["out"] = nc.dram_tensor("out", [NODES, C], f32, kind="ExternalOutput").ap()
    program(nc, io)
    result = run_bass_kernel_spmd(nc, [arrays], core_ids=[0])
    return result.results[0]["out"].reshape(B, N, C)
```

```python
from contextlib import ExitStack

import numpy as np

import concourse.bass as bass
from concourse import mybir
from concourse.alu_op_type import AluOpType as ALU

ACT = mybir.ActivationFunctionType
AX = mybir.AxisListType
f32, f16, i32 = mybir.dt.float32, mybir.dt.float16, mybir.dt.int32
ds = bass.ds

P = 128
B, N, C = 8, 1024, 128
LAYERS = 4
MT = N // P
NODES = B * N
TILES = NODES // P
HALF = N // 2
QH = MT // 2
CHUNKS = 2 * B
RES = 3
STREAM = B - RES
UNIT = MT * HALF
SUB = UNIT // 2
HEAD = 8
AHEAD = 4
RING = 4
GROUPS = TILES // RING
QUAD = 4
K = 24
ROUNDS = K // 8
BLOCKS = (0, 4, 6, 8, 12, 16, 20, K)
EPS = 1e-5
NEG = -1e22
TABLE_STEPS = 15
LIST, OWN, CNT, SELF, ROW = 3 * C, 3 * C + K, 3 * C + K + 1, 3 * C + K + 2, 3 * C + K + 4
INFO = ROW - LIST


def hold(eng, sem, value, passed):
    eng.wait_ge(sem, value)
    eng.sem_inc(passed, 1)


def load_values(nc, eng, words, least, most):
    _, values = nc.values_load_multi_w_load_instructions(words, engines=[eng.engine], min_val=least, max_val=most)
    return values


def later_tile(L, b, h):
    return 3 * B + CHUNKS * (L - 1) + 2 * b + h


def part_one(nc, ctx, io, mem):
    sem = lambda name: ctx.enter_context(nc.semaphore(name))
    bank = mem["bank"]
    tp, hwp, acc = bank[0:4], bank[4:6], bank[6:8]
    A, hT, hst, hws, xs, nat = mem["A"], mem["hT"], mem["hst"], mem["hws"], mem["xs"], mem["nat"]
    ring = [mem["A"][:, (2 * RES + h) * UNIT:(2 * RES + h + 1) * UNIT] for h in range(2)]
    x3 = io["x"].rearrange("b (t p) c -> b p t c", p=P)
    adj4 = io["adj"].rearrange("b (t p) m -> b t p m", p=P)
    adjT = io["adjT"]

    const_ready = sem("const_ready")
    numbers_ready = sem("numbers_ready")
    made = sem("made")
    w_in = sem("w_in")
    par_in = sem("par_in")
    x_in = [sem(f"x_in{q}") for q in range(2)]
    x_used = sem("x_used")
    nat_in = [sem(f"nat_in{k}") for k in range(QH)]
    again_in = [sem(f"again_in{h}") for h in range(2)]
    ax_ready = sem("ax_ready")
    axw_full = sem("axw_full")
    hst_ready = sem("hst_ready")
    hw_full = sem("hw_full")
    hws_ready = sem("hws_ready")
    tp_full = sem("tp_full")
    tp_free = sem("tp_free")
    acc_full = sem("acc_full")
    r_ready = sem("r_ready")
    store_done = [sem(f"store_done{h}") for h in range(2)]
    ring_in = [sem(f"ring_in{i}") for i in range(4)]
    ring_used = sem("ring_used")
    stats = sem("stats")
    norm = sem("norm")
    var_ready = sem("var_ready")
    std_ready = sem("std_ready")
    mask_done = sem("mask_done")
    key_ready = sem("key_ready")
    ext = sem("ext")
    sp_on, pool_on, dve_on = sem("sp_on"), sem("pool_on"), sem("dve_on")
    ext_done = sem("ext_done")
    const_act = sem("const_act")
    diag_in = sem("diag_in")
    rank = sem("rank")
    cls_ready = sem("cls_ready")
    cls_full = sem("cls_full")

    NORM_STEPS = 6

    block = ctx.enter_context(nc.Block())

    @block.sync
    def _(sp):
        def loads(b, first):
            for h in range(2):
                for k in range(QH):
                    if not (first and h == 0):
                        hold(sp, tp_full, 8 * (2 * b + h - 1) + 2 * k + 2, sp_on)
                        if k == 0 or (k == 1 and h == 1):
                            hold(sp, key_ready, 3 * b + h + k, sp_on)
                    sp.dma_start(nat[k][:, :], adj4[ds(b, 1), h * QH + k].rearrange("o p m -> (o p) m")).then_inc(nat_in[k], 16)
                    if first and h + k == 0:
                        sp.dma_start(mem["W"][:, :].rearrange("p (l c) -> p l c", l=LAYERS), io["W"].rearrange("l i c -> i l c")).then_inc(w_in, 16)
                if first and h == 0:
                    for name, col in (("b", 0), ("gamma", 1), ("beta", 2)):
                        with nc.allow_non_contiguous_dma(reason="the small vectors, once"):
                            sp.dma_start(mem["vec"][:, col * LAYERS:(col + 1) * LAYERS], io[name].rearrange("l c -> c l")).then_inc(par_in, 16)
        loads(0, True)
        with nc.allow_non_contiguous_dma(reason="the diagonal, once"):
            for b in range(B):
                sp.dma_start(mem["diag"][:, b * MT:(b + 1) * MT], diagonal(io["adj"], b)).then_inc(diag_in, 16)
        with sp.Fori(1, B) as b:
            loads(b, False)
        sp.wait_ge(acc_full, CHUNKS)
        for h in range(2):
            sp.wait_ge(store_done[h], 16 * STREAM)
        def stream(L, s, before):
            for h in range(2):
                for q in range(2):
                    if not (isinstance(L, int) and isinstance(s, int) and s == 0):
                        if q == 0:
                            sp.wait_ge(ring_used, 2 * STREAM * (L - 1) + 2 * s + h - 1)
                        else:
                            sp.wait_ge(acc_full, CHUNKS * L + 2 * before + h + 1)
                    sp.dma_start(ring[h][:, q * SUB:(q + 1) * SUB],
                                 adjT[ds(s, 1), h, :, q * SUB:(q + 1) * SUB].rearrange("o p e -> (o p) e")).then_inc(ring_in[2 * h + q], 16)

        def layer(L):
            stream(L, 0, -1)
            with sp.Fori(1, RES + 1) as s:
                stream(L, s, 2 * s - 1)
            with sp.Fori(RES + 1, STREAM) as s:
                stream(L, s, RES + s - 1)
        layer(1)
        with sp.Fori(2, LAYERS) as L:
            layer(L)

    @block.gpsimd
    def _(pool):
        pool.memset(mem["ident"][:, :], 0.0).then_inc(const_ready, 1)
        pool.wait_ge(const_ready, 1)
        pool.affine_select(out=mem["ident"][:, :], in_=mem["ident"][:, :], compare_op=ALU.not_equal, fill=1.0,
                           base=0, pattern=[[-1, P]], channel_multiplier=1).then_inc(const_ready, 1)
        whole = hT[:, (B - 1) * N:B * N].bitcast(i32)
        pool.iota(whole, pattern=[[1, N]], base=1, channel_multiplier=0).then_inc(const_ready, 1)
        pool.memset(mem["others"][:, :], 1.0).then_inc(const_ready, 1)
        pool.wait_ge(const_ready, 4)
        pool.affine_select(out=mem["others"][:, :], in_=mem["others"][:, :], compare_op=ALU.not_equal, fill=0.0,
                           base=0, pattern=[[-1, P]], channel_multiplier=1).then_inc(const_ready, 1)
        pool.wait_ge(const_ready, 5)
        pool.wait_ge(numbers_ready, 1)

        def make_key(e, slot, buffer, tile, used):
            if used is not None:
                hold(pool, ext_done, used, pool_on)
            key = mem["key"][buffer]
            pool.tensor_scalar(key[:, :], nat[slot][:, :], 0.0, None, ALU.is_gt).then_inc(mask_done, 1)
            pool.wait_ge(mask_done, 2 * e + 1)
            pool.tensor_tensor(key[:, :], key[:, :], mem["iota"][:, :], ALU.mult).then_inc(mask_done, 1)
            pool.wait_ge(mask_done, 2 * e + 2)
            own = key[:, ds(tile * P, P)]
            pool.tensor_tensor(own, own, mem["others"][:, :], ALU.mult).then_inc(key_ready, 1)

        def layer0(b, first):
            for i, (h, slot) in enumerate(((0, 0), (0, 1), (1, 0))):
                hold(pool, nat_in[slot], 16 * (2 * b + h + 1), pool_on)
                make_key(3 * b + i, slot, i, h * QH + slot, None if first else 3 * b + i - 2)
        layer0(0, True)
        with pool.Fori(1, B) as b:
            layer0(b, False)
        pool.wait_ge(tp_full, 8 * CHUNKS)
        tables(pool, mem, made)

        def fetch(L, b, h, rest=False):
            src = adj4[ds(2 * b + h, 1), QH + 1:QH + 2] if rest else adj4[ds(b, 1), ds(h * QH + L + 1, 1)]
            pool.dma_start(nat[h], src.rearrange("o u p m -> (o u p) m")).then_inc(again_in[h], 16)

        def keys(L, b, h, rest=False):
            hold(pool, again_in[h], 16 * (B * (L - 1) + b + 1), pool_on)
            e = later_tile(L, b, h)
            make_key(e, h, h, QH + 1 if rest else h * QH + L + 1, e - 1)
            pool.wait_ge(key_ready, e + 1)
        pool.wait_ge(key_ready, 3 * B)
        for h in range(2):
            fetch(1, 0, h)
        for L in (1, 2):
            with pool.Fori(0, B - 1) as b:
                for h in range(2):
                    keys(L, b, h)
                    fetch(L, b + 1, h)
            for h in range(2):
                keys(L, B - 1, h)
                fetch(L + 1, 0, h, rest=L == 2)
        with pool.Fori(0, B // 2 - 1) as b:
            for h in range(2):
                keys(3, b, h, rest=True)
                fetch(3, b + 1, h, rest=True)
        for h in range(2):
            keys(3, B // 2 - 1, h, rest=True)

    @block.tensor
    def _(pe):
        def h_times_w(L, b, Wl):
            for q in range(2):
                pe.wait_ge(hst_ready, 2 * (B * (L - 1) + b) + q + 1)
                for t in range(QH):
                    m = q * QH + t
                    last = nc.tensor.matmul(hwp[q][:, t * C:(t + 1) * C], hst[:, m * P:(m + 1) * P], Wl, start=True, stop=True)
                last.then_inc(hw_full, 1)

        def chunk(L, b, h, unit, ring_round=None):
            pe.wait_ge(r_ready, CHUNKS * L + 2 * b + h - 1)
            for q in range(2):
                if h == 0:
                    pe.wait_ge(hws_ready, 2 * (B * (L - 1) + b) + q + 1)
                if ring_round is not None:
                    pe.wait_ge(ring_in[2 * h + q], 16 * ring_round)
                for t in range(QH):
                    m = q * QH + t
                    last = nc.tensor.matmul(acc[h][:, :], hws[:, m * C:(m + 1) * C], unit(m), start=(m == 0), stop=(m == MT - 1))
                if q == 0 and ring_round is not None:
                    last.then_inc(ring_used, 1)
            last.then_inc(acc_full, 1)

        def adj_times_x(b, h, unit, first):
            if not first:
                pe.wait_ge(ax_ready, 2 * b + h - 1)
            for q in range(2):
                if h == 0:
                    pe.wait_ge(x_in[q], 16 * (b + 1))
                pe.wait_ge(tp_free, 8 * (2 * b + h) + 7 + q)
                for t in range(QH):
                    m = q * QH + t
                    last = nc.tensor.matmul(acc[h][:, :], xs[:, m * C:(m + 1) * C], unit(h, m), start=(m == 0), stop=(m == MT - 1))
                if q == 0 and h == 1:
                    last.then_inc(x_used, 1)
            last.then_inc(acc_full, 1)

        def times_w(b, h, first=False):
            pe.wait_ge(ax_ready, 2 * b + h + 1)
            if not first:
                pe.wait_ge(r_ready, 2 * b + h - 1)
            nc.tensor.matmul(hwp[h][:, :], mem["W"][:, 0:C], hst[:, h * HALF:(h + 1) * HALF], start=True, stop=True).then_inc(axw_full, 1)

        def adj_transposed(b, h, k, first=False):
            pe.wait_ge(nat_in[k], 16 * (2 * b + h + 1))
            for q in range(2):
                if not first:
                    pe.wait_ge(tp_free, 8 * (2 * b + h) + 2 * k + q - 3)
                for t in range(QH):
                    m = q * QH + t
                    last = nc.tensor.transpose(tp[(2 * k + q) % 4][:, t * P:(t + 1) * P], nat[k][:, m * P:(m + 1) * P], mem["ident"][:, :])
                last.then_inc(tp_full, 1)

        def layer0(b, unit, first=False, last=False):
            for h in range(2):
                for k in range(1, QH):
                    adj_transposed(b, h, k, first and h == 0 and k < 2)
                    if k == 1 and h == 1:
                        times_w(b, 0, first)
                    elif k == 1 and not first:
                        times_w(b - 1, 1, isinstance(b, int) and b == 1)
                if h == 0:
                    adj_transposed(b, 1, 0)
                elif not last:
                    adj_transposed(b + 1, 0, 0)
                adj_times_x(b, h, unit, first)

        def resident(i):
            return lambda h, m: A[:, ds((2 * i + h) * UNIT + m * HALF, HALF)]
        def in_ring(h, m):
            return ring[h][:, m * HALF:(m + 1) * HALF]

        pe.wait_ge(const_ready, 2)
        adj_transposed(0, 0, 0, True)
        pe.wait_ge(w_in, 16)
        layer0(0, resident(0), first=True)
        layer0(1, in_ring)
        with pe.Fori(1, RES) as i:
            layer0(2 * i, resident(i))
            layer0(2 * i + 1, in_ring)
        with pe.Fori(2 * RES, B - 1) as b:
            layer0(b, in_ring)
        layer0(B - 1, in_ring, last=True)
        times_w(B - 1, 1)

        def later_layer(L):
            def streamed(b, s):
                h_times_w(L, b, mem["W"][:, ds(L * C, C)])
                for h in range(2):
                    chunk(L, b, h, lambda m: in_ring(h, m), ring_round=STREAM * (L - 1) + s + 1)
            with pe.Fori(0, RES) as i:
                h_times_w(L, 2 * i, mem["W"][:, ds(L * C, C)])
                for h in range(2):
                    chunk(L, 2 * i, h, lambda m: resident(i)(h, m))
                streamed(2 * i + 1, i)
            if isinstance(L, int):
                pe.wait_ge(cls_ready, 1)
                nc.tensor.matmul(tp[0][:, 0:K], mem["below"][:, :], mem["of_class"][:, :], start=True, stop=True)
                nc.tensor.matmul(tp[0][:, K:2 * K], mem["ones"][:, :], mem["of_class"][:, :], start=True, stop=True).then_inc(cls_full, 1)
            with pe.Fori(2 * RES, B) as b:
                streamed(b, b - RES)
        with pe.Fori(1, LAYERS - 1) as L:
            later_layer(L)
        later_layer(LAYERS - 1)

    @block.scalar
    def _(act):
        def hw_out(L, b):
            for q in range(2):
                act.wait_ge(hw_full, 2 * (B * (L - 1) + b) + q + 1)
                nc.scalar.activation(hws[:, q * HALF:(q + 1) * HALF], hwp[q][:, :], ACT.Copy).then_inc(hws_ready, 1)

        def relu(L, b, h):
            act.wait_ge(acc_full, CHUNKS * L + 2 * b + h + 1)
            nc.scalar.activation(hT[:, ds(b * N + h * HALF, HALF)], acc[h][:, :], ACT.Relu,
                                 bias=mem["bcol"][:, 0:1]).then_inc(r_ready, 1)

        def load_x(b, q):
            act.dma_start(xs[:, q * HALF:(q + 1) * HALF].rearrange("p (t c) -> p t c", t=QH),
                          x3[ds(b, 1), :, q * QH:(q + 1) * QH].rearrange("o p t c -> p (o t) c")).then_inc(x_in[q], 16)

        def ax_out(b, h):
            act.wait_ge(acc_full, 2 * b + h + 1)
            nc.scalar.activation(hst[:, h * HALF:(h + 1) * HALF], acc[h][:, :], ACT.Copy).then_inc(ax_ready, 1)

        def relu0(b, h):
            act.wait_ge(axw_full, 2 * b + h + 1)
            nc.scalar.activation(hT[:, ds(b * N + h * HALF, HALF)], hwp[h][:, :], ACT.Relu,
                                 bias=mem["bcol"][:, 0:1]).then_inc(r_ready, 1)

        def adj_out(b, h, k, unit_at):
            for q in range(2):
                act.wait_ge(tp_full, 8 * (2 * b + h) + 2 * k + q + 1)
                dst = unit_at(h, q).rearrange("p (m n) -> p m n", n=HALF)[:, :, k * P:(k + 1) * P]
                nc.scalar.activation(dst, tp[(2 * k + q) % 4][:, :].rearrange("p (m n) -> p m n", n=P), ACT.Copy).then_inc(tp_free, 1)

        def layer0(b, unit_at, next_at, s=None, next_s=None, first=False):
            for h in range(2):
                for k in range(1, QH):
                    adj_out(b, h, k, unit_at)
                    if k == 1 and h == 1:
                        if first:
                            act.wait_ge(par_in, 48)
                            bias_of(0)
                        relu0(b, 0)
                    elif k == 1 and not first:
                        relu0(b - 1, 1)
                if s is not None:
                    act.wait_ge(tp_free, 8 * (2 * b + h) + 8)
                    act.dma_start(adjT[ds(s, 1), h].rearrange("o p e -> (o p) e"), ring[h][:, :]).then_inc(store_done[h], 16)
                if h == 0:
                    if not (s is None or isinstance(s, int) and s == 0):
                        act.wait_ge(store_done[1], 16 * s)
                    adj_out(b, 1, 0, unit_at)
                elif next_at is not None:
                    if not (next_s is None or isinstance(next_s, int) and next_s == 0):
                        act.wait_ge(store_done[0], 16 * next_s)
                    adj_out(b + 1, 0, 0, next_at)
                    act.wait_ge(x_used, b + 1)
                    load_x(b + 1, 0)
                ax_out(b, h)
                if h == 1 and next_at is not None:
                    load_x(b + 1, 1)

        def resident(i):
            return lambda h, q: A[:, ds((2 * i + h) * UNIT + q * SUB, SUB)]
        def in_ring(h, q):
            return ring[h][:, q * SUB:(q + 1) * SUB]

        def bias_of(L):
            nc.scalar.activation(mem["bcol"][:, 0:1], mem["vec"][:, ds(L, 1)], ACT.Copy).then_inc(const_act, 1)
            act.wait_ge(const_act, L + 1)

        for q in range(2):
            load_x(0, q)
        adj_out(0, 0, 0, resident(0))
        layer0(0, resident(0), in_ring, next_s=0, first=True)
        layer0(1, in_ring, resident(1), s=0)
        with act.Fori(1, RES - 1) as i:
            layer0(2 * i, resident(i), in_ring, next_s=i)
            layer0(2 * i + 1, in_ring, resident(i + 1), s=i)
        layer0(2 * RES - 2, resident(RES - 1), in_ring, next_s=RES - 1)
        layer0(2 * RES - 1, in_ring, in_ring, s=RES - 1, next_s=RES)
        with act.Fori(2 * RES, B - 1) as b:
            layer0(b, in_ring, in_ring, s=b - RES, next_s=b + 1 - RES)
        layer0(B - 1, in_ring, None, s=STREAM - 1)
        relu0(B - 1, 1)

        def root(L):
            act.wait_ge(var_ready, L + 1)
            nc.scalar.activation(mem["bn"][:, 3:4], mem["bn"][:, 2:3], ACT.Sqrt).then_inc(std_ready, 1)
        root(0)
        with act.Fori(1, LAYERS) as L:
            bias_of(L)
            with act.Fori(0, B) as b:
                hw_out(L, b)
                for h in range(2):
                    relu(L, b, h)
            root(L)

    @block.vector
    def _(dve):
        dve.wait_ge(const_ready, 3)
        nc.vector.tensor_copy(mem["iota"][:, :], hT[:, (B - 1) * N:B * N].bitcast(i32)).then_inc(numbers_ready, 1)
        dve.wait_ge(par_in, 48)

        def extract(e, buffer, tile):
            key, top = mem["key"][buffer], mem["top"][buffer]
            dve.sem_clear(ext)
            hold(dve, key_ready, e + 1, dve_on)
            for r in range(ROUNDS):
                nc.vector.max(top[:, 8 * r:8 * r + 8], key[:, :]).then_inc(ext, 1)
                dve.wait_ge(ext, 2 * r + 1)
                if r < ROUNDS - 1:
                    nc.vector.match_replace(key[:, :], top[:, 8 * r:8 * r + 8], key[:, :], 0.0).then_inc(ext, 1)
                    dve.wait_ge(ext, 2 * r + 2)
            nc.vector.tensor_copy(mem["keys"][:, ds(tile * K, K)], top[:, :]).then_inc(ext_done, 1)

        def lists_beside(L, b, h):
            if isinstance(L, int) and L == 0:
                for i, tile in ((0, 0), (1, 1)) if h == 0 else ((2, QH),):
                    extract(3 * b + i, i, MT * b + tile)
            elif isinstance(L, int) and L == LAYERS - 1:
                if b < B // 2:
                    extract(later_tile(L, b, h), h, MT * (2 * b + h) + QH + 1)
            else:
                extract(later_tile(L, b, h), h, QH * (2 * b + h) + L + 1)

        def chunk_stats(L, b, h):
            dve.wait_ge(r_ready, CHUNKS * L + 2 * b + h + 1)
            nc.vector.bn_stats(mem["st"][:, ds((2 * b + h) * 6, 6)], hT[:, ds(b * N + h * HALF, HALF)]).then_inc(stats, 1)

        def norm_steps(L):
            bn, base = mem["bn"], NORM_STEPS * L
            hold(dve, stats, CHUNKS * (L + 1), dve_on)
            nc.vector.bn_aggr(bn[:, 0:2], mem["st"][:, :]).then_inc(norm, 1)
            dve.wait_ge(norm, base + 1)
            nc.vector.tensor_scalar(bn[:, 2:3], bn[:, 1:2], EPS, None, ALU.add).then_inc(var_ready, 1)
            dve.wait_ge(std_ready, L + 1)
            nc.vector.reciprocal(bn[:, 4:5], bn[:, 3:4]).then_inc(norm, 1)
            dve.wait_ge(norm, base + 2)
            nc.vector.tensor_tensor(bn[:, 5:6], bn[:, 4:5], mem["vec"][:, ds(LAYERS + L, 1)], ALU.mult).then_inc(norm, 1)
            dve.wait_ge(norm, base + 3)
            nc.vector.tensor_tensor(bn[:, 6:7], bn[:, 0:1], bn[:, 5:6], ALU.mult).then_inc(norm, 1)
            dve.wait_ge(norm, base + 4)
            nc.vector.tensor_tensor(bn[:, 7:8], mem["vec"][:, ds(2 * LAYERS + L, 1)], bn[:, 6:7], ALU.subtract).then_inc(norm, 2)
            dve.wait_ge(norm, base + 6)

        def affine(L, b):
            for q in range(2):
                if not (isinstance(L, int) and L == 1 and isinstance(b, int) and b == 0):
                    dve.wait_ge(hw_full, 2 * (B * (L - 1) + b) - 2 + q + 1)
                nc.vector.tensor_scalar(hst[:, q * HALF:(q + 1) * HALF], hT[:, ds(b * N + q * HALF, HALF)],
                                        mem["bn"][:, 5:6], mem["bn"][:, 7:8], ALU.mult, ALU.add).then_inc(hst_ready, 1)

        def graph(L, b, last):
            for h in range(2):
                if L != 0 and h == 1 and not last:
                    affine(L, b + 1)
                if not (last and h == 1):
                    lists_beside(L, b, h)
                chunk_stats(L, b, h)

        def turn(L):
            norm_steps(L)
            affine(L + 1, 0)
            lists_beside(L, B - 1, 1)

        with dve.Fori(0, B - 1) as b:
            graph(0, b, False)
        graph(0, B - 1, True)
        turn(0)
        for L in (1, 2):
            with dve.Fori(0, B - 1) as b:
                graph(L, b, False)
            graph(L, B - 1, True)
            turn(L)
        ranking = rank_nodes(nc, dve, mem, tp[0], rank, made, ext_done, diag_in, cls_ready, cls_full)
        for b in range(B):
            graph(LAYERS - 1, b, b == B - 1)
            for part in {3: (0, 1, 2), 5: (3,), 6: (4,)}.get(b, ()):
                ranking[part]()
        norm_steps(LAYERS - 1)


def diagonal(adj, b):
    a = adj[b]
    return bass.AP(tensor=a.tensor, offset=a.offset, ap=[[N + 1, P], [P * (N + 1), MT]])


def rank_nodes(nc, dve, mem, sums, rank, made, ext_done, diag_in, cls_ready, cls_full):
    count = [0]

    def link(ins):
        count[0] += 1
        ins.then_inc(rank, 1)
        dve.wait_ge(rank, count[0])

    E, small = mem["E"], mem["small"]
    info = E[:, 0:INFO * TILES].rearrange("p (t w) -> p t w", w=INFO)
    S = E[:, INFO * TILES:(INFO + K) * TILES]
    half = K * TILES // 2
    M, ones = (E[:, (INFO + K) * TILES + i * half:(INFO + K) * TILES + (i + 1) * half].bitcast(f16) for i in range(2))
    list_n, none, cnt, rankf, slotsf, cumf = (small[:, i * TILES:(i + 1) * TILES] for i in range(6))
    a = 6 * TILES
    last, incl, shift = small[:, a:a + K + 1], small[:, a + 32:a + 32 + K], small[:, a + 64:a + 64 + K]
    of_class = mem["of_class"][:, :]
    keys3 = mem["keys"][:, :].rearrange("p (t k) -> p t k", k=K)
    by_tile = lambda x: x.rearrange("p (t k) -> p t k", k=K)
    by_class = lambda x: x.rearrange("p (k t) -> p k t", t=TILES)
    over_k = lambda x: x.rearrange("p (t o) -> p t o", o=1).to_broadcast([P, TILES, K])
    over_t = lambda x: x.rearrange("p (k o) -> p k o", o=1).to_broadcast([P, K, TILES])
    v = nc.vector

    def lists():
        dve.wait_ge(made, TABLE_STEPS)
        dve.wait_ge(ext_done, TILES)
        dve.wait_ge(diag_in, 16 * B)
        link(v.tensor_scalar(by_tile(M), keys3, 0.0, None, ALU.is_gt))
        link(v.tensor_reduce(list_n, by_tile(M), AX.X, ALU.add))
        link(v.tensor_scalar(none, mem["diag"][:, :], 0.0, None, ALU.is_gt))
        link(v.tensor_scalar(info[:, :, SELF - LIST], none, NEG, -NEG, ALU.mult, ALU.add))
        link(v.memset(info[:, :, SELF - LIST + 1], 0.0))
        link(v.tensor_tensor(none, none, list_n, ALU.add))
        link(v.tensor_scalar(none, none, 0.0, None, ALU.is_equal))
        link(v.tensor_tensor(cnt, list_n, none, ALU.add))
        link(v.tensor_tensor(none, none, mem["tomean"][:, :], ALU.mult))

    def rows():
        link(v.scalar_tensor_tensor(info[:, :, 0:K].bitcast(i32), keys3, 1.0, over_k(mem["graph0"][:, :]), ALU.max, ALU.add))
        link(v.tensor_tensor(info[:, :, 0].bitcast(i32), info[:, :, 0].bitcast(i32), none, ALU.add))
        link(v.tensor_copy(info[:, :, OWN - LIST].bitcast(i32), mem["own"][:, :]))
        link(v.tensor_copy(info[:, :, CNT - LIST], cnt))
        link(v.tensor_scalar(cnt, cnt, 1.0, None, ALU.max))
        link(v.tensor_tensor(by_class(M), cnt.rearrange("p (o t) -> p o t", o=1).to_broadcast([P, K, TILES]), over_t(mem["classes"][:, :]), ALU.is_equal))

    def classes():
        link(v.memset(ones, 1.0))
        link(v.tensor_tensor_scan(S, ones, M, 0.0, ALU.mult, ALU.add))
        link(v.memset(last[:, 0:1], 0.0))
        link(v.tensor_copy(last[:, 1:K + 1], by_class(S)[:, :, TILES - 1]))
        v.tensor_tensor(of_class, last[:, 1:K + 1], last[:, 0:K], ALU.subtract).then_inc(cls_ready, 1)

    def ranks():
        dve.wait_ge(cls_full, 1)
        link(v.tensor_copy(shift, sums[:, K:2 * K]))
        link(v.tensor_tensor_scan(incl, mem["ones"][:, 0:K], shift, 0.0, ALU.mult, ALU.add))
        link(v.tensor_tensor(shift, incl, shift, ALU.subtract))
        link(v.tensor_tensor(shift, sums[:, 0:K], shift, ALU.add))
        link(v.tensor_tensor(shift, shift, last[:, 0:K], ALU.subtract))
        link(v.tensor_tensor(by_class(S), by_class(S), over_t(shift), ALU.add))
        link(v.tensor_tensor(S, S, M, ALU.mult))
        link(v.tensor_reduce(rankf, S.rearrange("p (k t) -> p t k", t=TILES), AX.X, ALU.add))
        link(v.tensor_scalar(mem["ranki"][:, :], rankf, -1.0, None, ALU.add))

    def slots():
        plan = mem["plan"][:, :].rearrange("p (g w) -> p g w", w=2 * RING)
        link(v.tensor_tensor(by_tile(M), incl.rearrange("p (o k) -> p o k", o=1).to_broadcast([P, TILES, K]), over_k(mem["rank0"][:, :]), ALU.is_gt))
        link(v.tensor_reduce(slotsf, by_tile(M), AX.X, ALU.add))
        link(v.tensor_copy(plan[:, :, 0:RING], slotsf.rearrange("p (g r) -> p g r", r=RING)))
        for r in range(RING):
            link(v.tensor_tensor_scan(cumf[:, r:TILES:RING], mem["ones"][:, 0:TILES // RING], slotsf[:, r:TILES:RING], 0.0, ALU.mult, ALU.add))
        link(v.tensor_scalar(plan[:, :, RING:2 * RING], cumf.rearrange("p (g r) -> p g r", r=RING), 16.0, None, ALU.mult))
        link(v.tensor_scalar(mem["full"][:, :], incl[:, 0:1], 1.0, None, ALU.mult))

    return [lists, rows, classes, ranks, slots]


def tables(pool, mem, made):
    count = [0]

    def link(ins):
        count[0] += 1
        ins.then_inc(made, 1)
        pool.wait_ge(made, count[0])

    tmp = mem["small"][:, 0:TILES].bitcast(i32)
    link(pool.iota(mem["own"][:, :], pattern=[[P, TILES]], base=0, channel_multiplier=1))
    link(pool.iota(tmp[:, 0:TILES].rearrange("p (b t) -> p b t", b=B), pattern=[[N, B], [0, MT]], base=-1, channel_multiplier=0))
    link(pool.tensor_copy(mem["graph0"][:, :], tmp[:, 0:TILES]))
    link(pool.iota(tmp[:, 0:TILES].rearrange("p (b t) -> p b t", b=B), pattern=[[1 - N, B], [0, MT]], base=NODES, channel_multiplier=0))
    link(pool.tensor_copy(mem["tomean"][:, :], tmp[:, 0:TILES]))
    link(pool.iota(tmp[:, 0:K], pattern=[[-1, K]], base=K, channel_multiplier=0))
    link(pool.tensor_copy(mem["classes"][:, :], tmp[:, 0:K]))
    link(pool.iota(tmp[:, 0:HEAD], pattern=[[P, HEAD]], base=0, channel_multiplier=0))
    turns = tmp[:, HEAD:TILES].rearrange("p (j e) -> p j e", e=2)
    for e in range(2):
        link(pool.iota(turns[:, :, e], pattern=[[(1 - 2 * e) * P, (TILES - HEAD) // 2]], base=(HEAD, TILES - 1)[e] * P, channel_multiplier=0))
    link(pool.tensor_copy(mem["rank0"][:, :], tmp[:, 0:TILES]))
    link(pool.iota(tmp[:, 0:K], pattern=[[1, K]], base=0, channel_multiplier=0))
    link(pool.tensor_copy(mem["slot"][:, :], tmp[:, 0:K]))
    link(pool.memset(mem["ones"][:, :], 1.0))
    link(pool.affine_select(out=mem["below"][:, :], in_=mem["ones"][:, :], compare_op=ALU.is_gt, fill=0.0,
                            base=0, pattern=[[1, P]], channel_multiplier=-1))
    assert count[0] == TABLE_STEPS


def part_two(nc, ctx, io, mem):
    sem = lambda name: ctx.enter_context(nc.semaphore(name))
    bank = mem["bank"]
    hp, xp, qp = bank[0:2], bank[2:4], bank[4:8]
    hT, hst, bn = mem["hT"], mem["hst"], mem["bn"]
    A = mem["A"]
    at = [0]

    def carve(cols):
        a = at[0]
        at[0] += cols
        return A[:, a:a + cols]

    z = [carve(N) for _ in range(2)]
    rows = [carve(ROW * MT) for _ in range(AHEAD)]
    rank_of = [carve(MT) for _ in range(AHEAD)]
    x1T = carve(N)
    wkq = carve(2 * C)
    st = carve(6 * MT)
    mv = carve(2 * MT)
    std, rstd, veps = carve(MT), carve(MT), carve(MT)
    xsum = carve(2 * B)
    xmean = carve(B)
    means = carve(2 * C)
    row3 = [rows[u].rearrange("p (t w) -> p t w", w=ROW) for u in range(AHEAD)]
    x1_of = lambda b, m: rows[b % AHEAD][:, m * ROW + 2 * C:m * ROW + 3 * C]

    two_in = sem("two_in")
    xres_in = [sem(f"xres_in{u}") for u in range(2)]
    h_ready = sem("h_ready")
    hrow_full = sem("hrow_full")
    zst = sem("zst")
    var2 = sem("var2")
    std2 = sem("std2")
    dstep = sem("dstep")
    x1_ready = sem("x1_ready")
    x1T_full = sem("x1T_full")
    x1T_ready = sem("x1T_ready")
    kq_full = sem("kq_full")
    kq_ready = sem("kq_ready")
    tab_out = [sem(f"tab_out{u}") for u in range(AHEAD)]
    info_set = sem("info_set")
    placed = [sem(f"placed{u}") for u in range(AHEAD)]
    mean_full = sem("mean_full")
    mean_ready = sem("mean_ready")
    mean_rows = sem("mean_rows")
    mean_out = sem("mean_out")

    def rows_free(eng, b):
        if b >= AHEAD:
            eng.wait_ge(tab_out[b % AHEAD], 16 * (b // AHEAD))
            eng.wait_ge(placed[b % AHEAD], 16 * MT * (b // AHEAD))

    block = ctx.enter_context(nc.Block())
    qx = io["qx"][0:NODES, :].rearrange("(b t p) c -> b p t c", b=B, p=P)
    x3 = io["x"].rearrange("b (t p) c -> b p t c", p=P)

    @block.sync
    def _(sp):
        def load_x(b):
            sp.dma_start(z[b % 2].rearrange("p (t c) -> p t c", c=C), x3[b:b + 1].rearrange("o p t c -> p (o t) c")).then_inc(xres_in[b % 2], 16)

        load_x(0)
        load_x(1)
        sp.dma_start(wkq[:, 0:C], io["WK"]).then_inc(two_in, 16)
        sp.dma_start(wkq[:, C:2 * C], io["WQ"]).then_inc(two_in, 16)
        for b in range(B):
            if b + 2 < B:
                sp.wait_ge(x1_ready, MT * (b + 1))
                load_x(b + 2)
            sp.wait_ge(kq_ready, 4 * b + 4)
            sp.dma_start(qx[b:b + 1].rearrange("o p t c -> p (o t) c"), row3[b % AHEAD][:, :, C:3 * C]).then_inc(tab_out[b % AHEAD], 16)
        sp.wait_ge(mean_rows, 2)
        sp.dma_start(io["qx"][NODES:NODES + B, :], means[0:B, :]).then_inc(mean_out, 16)
        for u in range(AHEAD):
            sp.wait_ge(tab_out[u], 16 * (B // AHEAD))
        sp.wait_ge(mean_out, 16)

    @block.gpsimd
    def _(pool):
        for b in range(B):
            rank = rank_of[b % AHEAD].bitcast(i32)
            pool.wait_ge(info_set, 2 * b + 2)
            pool.wait_ge(x1_ready, MT * (b + 1))
            for t in range(MT):
                if t % 2 == 0:
                    pool.wait_ge(kq_ready, 4 * b + t // 2 + 1)
                pool.indirect_dma_start(io["sorted"], bass.IndirectOffsetOnAxis(ap=rank[:, t:t + 1], axis=0),
                                        rows[b % AHEAD][:, t * ROW:(t + 1) * ROW], None).then_inc(placed[b % AHEAD], 16)
        for u in range(AHEAD):
            pool.wait_ge(placed[u], 16 * MT * (B // AHEAD))

    @block.vector
    def _(dve):
        info = mem["E"][:, 0:INFO * TILES]

        def lists_into_rows(b):
            u = b % AHEAD
            nc.vector.tensor_copy(row3[u][:, :, LIST:ROW], info[:, ds(b * INFO * MT, INFO * MT)].rearrange("p (t w) -> p t w", w=INFO)).then_inc(info_set, 1)
            nc.vector.tensor_copy(rank_of[u].bitcast(i32), mem["ranki"][:, ds(b * MT, MT)]).then_inc(info_set, 1)

        def affine(b):
            for q in range(2):
                nc.vector.tensor_scalar(hst[:, q * HALF:(q + 1) * HALF], hT[:, ds(b * N + q * HALF, HALF)],
                                        bn[:, 5:6], bn[:, 7:8], ALU.mult, ALU.add).then_inc(h_ready, 1)

        def graph(b):
            u = b % 2
            dve.sem_clear(dstep)
            dve.wait_ge(xres_in[u], 16 * (b // 2 + 1))
            for q in range(2):
                dve.wait_ge(hrow_full, 2 * b + q + 1)
                nc.vector.tensor_tensor(z[u][:, q * HALF:(q + 1) * HALF], hp[q][:, :], z[u][:, q * HALF:(q + 1) * HALF], ALU.add).then_inc(zst, 1)
            for t in range(MT):
                dve.wait_ge(zst, 2 * b + 1 + t // QH)
                nc.vector.bn_stats(st[:, 6 * t:6 * t + 6], z[u][:, t * C:(t + 1) * C]).then_inc(dstep, 1)
            for t in range(MT):
                dve.wait_ge(dstep, t + 1)
                nc.vector.bn_aggr(mv[:, 2 * t:2 * t + 2], st[:, 6 * t:6 * t + 6]).then_inc(dstep, 1)
            dve.wait_ge(dstep, 2 * MT)
            nc.vector.tensor_scalar(veps, mv[:, 1:2 * MT:2], EPS, None, ALU.add).then_inc(var2, 1)
            if b + 1 < B:
                affine(b + 1)
            dve.wait_ge(std2, b + 1)
            nc.vector.reciprocal(rstd, std).then_inc(dstep, 1)
            dve.wait_ge(dstep, 2 * MT + 1)
            if b >= AHEAD:
                rows_free(dve, b)
                lists_into_rows(b)
            for t in range(MT):
                nc.vector.tensor_scalar(x1_of(b, t), z[u][:, t * C:(t + 1) * C], mv[:, 2 * t:2 * t + 1], rstd[:, t:t + 1],
                                        ALU.subtract, ALU.mult).then_inc(x1_ready, 1)

        affine(0)
        for b in range(AHEAD):
            lists_into_rows(b)
        for b in range(B):
            graph(b)
        dve.wait_ge(x1T_ready, 2 * B)
        dve.sem_clear(dstep)
        nc.vector.tensor_reduce(xmean, xsum.rearrange("p (b q) -> p b q", q=2), AX.X, ALU.add).then_inc(dstep, 1)
        dve.wait_ge(dstep, 1)
        nc.vector.tensor_scalar(xmean, xmean, 1.0 / N, None, ALU.mult).then_inc(mean_ready, 1)

    @block.tensor
    def _(pe):
        def rows_of_h(b):
            for q in range(2):
                pe.wait_ge(h_ready, 2 * b + q + 1)
                for t in range(QH):
                    m = q * QH + t
                    last = nc.tensor.transpose(hp[q][:, t * P:(t + 1) * P], hst[:, m * P:(m + 1) * P], mem["ident"][:, :])
                last.then_inc(hrow_full, 1)

        def project(b):
            for q in range(2):
                pe.wait_ge(x1_ready, MT * b + QH * (q + 1))
                for t in range(QH):
                    m = q * QH + t
                    last = nc.tensor.transpose(xp[q][:, t * P:(t + 1) * P], x1_of(b, m), mem["ident"][:, :])
                last.then_inc(x1T_full, 1)
            for j in range(4):
                if j % 2 == 0:
                    pe.wait_ge(x1T_ready, 2 * b + j // 2 + 1)
                if b > 0:
                    pe.wait_ge(kq_ready, 4 * b + j - 3)
                for t in range(2):
                    m = 2 * j + t
                    last = nc.tensor.matmul(qp[j][:, t * 2 * C:(t + 1) * 2 * C], x1T[:, m * P:(m + 1) * P], wkq, start=True, stop=True)
                last.then_inc(kq_full, 1)

        rows_of_h(0)
        rows_of_h(1)
        pe.wait_ge(two_in, 32)
        for b in range(B):
            project(b)
            if b + 2 < B:
                rows_of_h(b + 2)
        pe.wait_ge(mean_ready, 1)
        nc.tensor.transpose(hp[0][0:B, 0:P], xmean, mem["ident"][:, :]).then_inc(mean_full, 1)

    @block.scalar
    def _(act):
        def root(b):
            act.wait_ge(var2, b + 1)
            nc.scalar.activation(std, veps, ACT.Sqrt).then_inc(std2, 1)

        def x1T_out(b):
            for q in range(2):
                act.wait_ge(x1T_full, 2 * b + q + 1)
                nc.scalar.activation(x1T[:, q * HALF:(q + 1) * HALF], xp[q][:, :], ACT.Copy,
                                     accum_out=xsum[:, ds(2 * b + q, 1)]).then_inc(x1T_ready, 1)

        def kq_out(b):
            rows_free(act, b)
            for j in range(4):
                act.wait_ge(kq_full, 4 * b + j + 1)
                nc.scalar.activation(row3[b % AHEAD][:, 2 * j:2 * j + 2, 0:2 * C], qp[j][:, :].rearrange("p (t c) -> p t c", t=2), ACT.Copy).then_inc(kq_ready, 1)

        root(0)
        for b in range(B):
            x1T_out(b)
            if b + 1 < B:
                root(b + 1)
            kq_out(b)
        nc.scalar.activation(means[0:B, 0:C], mem["ident"][0:B, :], ACT.Copy).then_inc(mean_rows, 1)
        act.wait_ge(mean_full, 1)
        nc.scalar.activation(means[0:B, C:2 * C], hp[0][0:B, 0:P], ACT.Copy).then_inc(mean_rows, 1)


def part_three(nc, ctx, io, mem):
    sem = lambda name: ctx.enter_context(nc.semaphore(name))
    A = mem["A"]
    at = [0]

    def carve(cols):
        a = at[0]
        at[0] += cols
        return A[:, a:a + cols]

    R = range(RING)
    G = [carve((K + QUAD - 1) * 2 * C) for _ in R]
    mine = [mem["E"][:, v * ROW:(v + 1) * ROW] for v in range(2 * RING)]
    o = [carve(C) for _ in R]
    home = [carve(RING) for _ in range(2)]
    minus_p = carve(C)
    w_self = carve(C)
    w = [carve(QUAD * C) for _ in range(2)]
    score, mask = ([carve(K + 1) for _ in range(2)] for _ in range(2))
    masked, least = [carve(K + 1) for _ in R], [carve(1) for _ in R]
    wgt, own_wgt = [carve(K + 1) for _ in range(2)], [carve(1) for _ in range(2)]
    den = [carve(RING) for _ in range(2)]
    st, mv = carve(6 * RING), carve(2 * RING)
    veps, std, rstd = carve(RING), carve(RING), carve(RING)
    assert at[0] <= 2 * (RES + 1) * UNIT
    D = [mem["hT"][:, u * (K + 1) * P:(u + 1) * (K + 1) * P] for u in range(2)]
    acc = mem["bank"]
    plan = mem["plan"][0:1, :].rearrange("p (g w) -> p g w", w=2 * RING)

    p_in = sem("p_in")
    mine_in = [sem(f"mine_in{v}") for v in range(2 * RING)]
    slot_in = [sem(f"slot_in{r}") for r in R]
    tile_done = sem("tile_done")
    out_ready = sem("out_ready")
    out_done = [sem(f"out_done{r}") for r in R]
    step = sem("step")
    masked_ready = sem("masked_ready")
    wgt_set = sem("wgt_set")
    diag_step = [sem(f"diag_step{u}") for u in range(2)]
    diag_ready = sem("diag_ready")
    acc_ready = sem("acc_ready")
    var3 = sem("var3")
    std3 = sem("std3")
    fin = sem("fin")
    cleared = sem("cleared")
    pool_on3, sp_on3 = sem("pool_on3"), sem("sp_on3")
    block = ctx.enter_context(nc.Block())

    def slots_of(eng, g):
        return load_values(nc, eng, plan[:, ds(g, 1), 0:RING], 1, K)

    def for_slots(eng, n, body):
        body(0)
        for s in range(1, 4):
            with eng.If(n > s):
                body(s)
        with eng.If(n > 4):
            body(4)
            for s in range(5, 8):
                with eng.If(n > s):
                    body(s)
            with eng.If(n > 8):
                body(8)
                for s in range(9, K):
                    with eng.If(n > s):
                        body(s)
                eng.nop()
            eng.nop()

    @block.sync
    def _(sp):
        full = sp.value_load(mem["full"][0:1, 0:1], min_val=0, max_val=NODES)
        with sp.If(full < 1):
            sp.dma_start(minus_p, io["p"].rearrange("(o c) -> o c", o=1).to_broadcast([P, C])).then_inc(p_in, 16)

            def load(i, v, first):
                if first:
                    at = v
                else:
                    turn = RING * i + v // 2 - HEAD // 2
                    at = HEAD + turn if v % 2 == 0 else TILES - 1 - turn
                if not first:
                    hold(sp, tile_done, 2 * RING * (i - 1) + v + 1, sp_on3)
                sp.dma_start(mine[v], io["sorted"][ds(at * P, P), :]).then_inc(mine_in[v], 16)
            for v in range(2 * RING):
                load(0, v, True)
            with sp.Fori(1, GROUPS // 2) as i:
                for v in range(2 * RING):
                    load(i, v, False)

    @block.gpsimd
    def _(pool):
        full = pool.value_load(mem["full"][0:1, 0:1], min_val=0, max_val=NODES)
        with pool.If(full < 1):
            def gathers(i, half, r, n, first):
                if not first:
                    hold(pool, acc_ready, RING * (2 * i + half - 1) + r + 1, pool_on3)
                v = RING * half + r
                hold(pool, mine_in[v], 16 * (i + 1), pool_on3)
                lists = mine[v][:, LIST:LIST + K].bitcast(i32)

                def slot(s):
                    pool.indirect_dma_start(G[r][:, s * 2 * C:(s + 1) * 2 * C], None, io["qx"],
                                            bass.IndirectOffsetOnAxis(ap=lists[:, s:s + 1], axis=0)).then_inc(slot_in[r], 16)
                if first and r % 2:
                    pool.wait_ge(cleared, r // 2 + 1)
                for_slots(pool, n, slot)

            def scatter(g, half, r):
                hold(pool, out_ready, RING * g + r + 1, pool_on3)
                pool.indirect_dma_start(io["out"], bass.IndirectOffsetOnAxis(ap=home[half][:, r:r + 1].bitcast(i32), axis=0), o[r], None).then_inc(out_done[r], 16)

            def group(i, half, scatters):
                n = slots_of(pool, 2 * i + half)
                for r in R:
                    gathers(i, half, r, n[r], isinstance(i, int) and i + half == 0)
                    if scatters:
                        for k in ((), (0, 1), (2, 3), ())[r]:
                            scatter(2 * i + half - 2, half, k)

            for half in range(2):
                group(0, half, False)
            with pool.Fori(1, GROUPS // 2) as i:
                for half in range(2):
                    group(i, half, True)
            for r in R:
                scatter(GROUPS - 2, 0, r)
            for r in R:
                scatter(GROUPS - 1, 1, r)
            for r in R:
                pool.wait_ge(out_done[r], 16 * GROUPS)

    @block.scalar
    def _(act):
        full = act.value_load(mem["full"][0:1, 0:1], min_val=0, max_val=NODES)
        with act.If(full < 1):
            def weights(g, half, r, n, first):
                t, u = RING * g + r, r % 2
                d = den[half][:, r:r + 1]
                act.wait_ge(masked_ready, t + 1)
                nc.scalar.activation(wgt[u], masked[r], ACT.Exp, bias=least[r], scale=-1.0, accum_out=d).then_inc(wgt_set, 1)
                act.wait_ge(wgt_set, 2 * t + 1)
                nc.scalar.activation(own_wgt[u], wgt[u][:, K:K + 1], ACT.Identity, bias=d).then_inc(wgt_set, 1)

                if not first:
                    act.wait_ge(acc_ready, t - 1)

                def diag(s):
                    nc.scalar.activation(D[u][:, s * P:(s + 1) * P], mem["ident"][:, :], ACT.Copy, scale=wgt[u][:, s:s + 1]).then_inc(diag_step[u], 1)
                for_slots(act, n, diag)
                act.wait_ge(wgt_set, 2 * t + 2)
                nc.scalar.activation(D[u][:, K * P:(K + 1) * P], mem["ident"][:, :], ACT.Copy, scale=own_wgt[u]).then_inc(diag_ready, 1)

            def group(g, half, first):
                n = slots_of(act, g)
                for r in R:
                    weights(g, half, r, n[r], first and r < 2)
                    if r == 1 and not first:
                        root(g - 1)

            def root(g):
                act.wait_ge(var3, g + 1)
                nc.scalar.activation(std, veps, ACT.Sqrt).then_inc(std3, 1)

            group(0, 0, True)
            group(1, 1, False)
            with act.Fori(1, GROUPS // 2) as i:
                for half in range(2):
                    group(2 * i + half, half, False)
            root(GROUPS - 1)

    @block.tensor
    def _(pe):
        full = pe.value_load(mem["full"][0:1, 0:1], min_val=0, max_val=NODES)
        with pe.If(full < 1):
            def tile_sum(g, half, r, n):
                t, u = RING * g + r, r % 2
                out = acc[RING * half + r][:, 0:C]

                def slot(s):
                    pe.wait_ge(diag_step[u], s + 1)
                    nc.tensor.matmul(out, D[u][:, s * P:(s + 1) * P], G[r][:, s * 2 * C + C:(s + 1) * 2 * C], start=(s == 0), stop=False)
                for_slots(pe, n, slot)
                pe.sem_clear(diag_step[u])
                pe.wait_ge(diag_ready, t + 1)
                nc.tensor.matmul(out, D[u][:, K * P:(K + 1) * P], mine[RING * half + r][:, 2 * C:3 * C], start=False, stop=True).then_inc(acc_ready, 1)

            with pe.Fori(0, GROUPS // 2) as i:
                for half in range(2):
                    n = slots_of(pe, 2 * i + half)
                    for r in R:
                        tile_sum(2 * i + half, half, r, n[r])

    @block.vector
    def _(dve):
        full = dve.value_load(mem["full"][0:1, 0:1], min_val=0, max_val=NODES)
        with dve.If(full < 1):
            for u in range(2):
                nc.vector.memset(score[u], 0.0).then_inc(fin, 1)
            for r in range(1, RING, 2):
                nc.vector.memset(G[r], 0.0).then_inc(cleared, 1)
            n = slots_of(dve, 0)
            for r in range(0, RING, 2):
                nc.vector.tensor_scalar(G[r][:, ds(n[r] * 2 * C, (QUAD - 1) * 2 * C)], mem["ones"][:, 0:1].to_broadcast([P, (QUAD - 1) * 2 * C]), 0.0, None, ALU.mult).then_inc(fin, 1)
            dve.wait_ge(p_in, 16)
            nc.vector.tensor_scalar(minus_p, minus_p, -1.0, None, ALU.mult).then_inc(fin, 1)
            dve.wait_ge(fin, RING // 2 + 3)
            dve.wait_ge(cleared, RING // 2)

            def scores(g, half, r, n, arrive):
                u, v = r % 2, RING * half + r
                dve.sem_clear(step)
                dve.wait_ge(mine_in[v], 8 * (g - half) + 16)
                k = mine[v][:, 0:C]

                def add_k(j):
                    a, slots = BLOCKS[j], BLOCKS[j + 1] - BLOCKS[j]
                    q = G[r][:, a * 2 * C:(a + slots) * 2 * C].rearrange("p (s c) -> p s c", s=slots)[:, :, 0:C]
                    k_each = k.rearrange("p (o c) -> p o c", o=1).to_broadcast([P, slots, C])
                    nc.vector.tensor_tensor(w[j % 2][:, 0:slots * C].rearrange("p (s c) -> p s c", s=slots), q, k_each, ALU.add).then_inc(step, 1)

                def dot(row, s):
                    return nc.vector.scalar_tensor_tensor(row, row, 0.0, minus_p, ALU.max, ALU.mult, accum_out=score[u][:, s:s + 1])

                def dots(j):
                    for s in range(BLOCKS[j], BLOCKS[j + 1]):
                        i = s - BLOCKS[j]
                        last = dot(w[j % 2][:, i * C:(i + 1) * C], s)
                    last.then_inc(step, 1)

                def more(j):
                    with dve.If(n > BLOCKS[j]):
                        add_k(j)
                        dve.wait_ge(step, 2 * j + 2)
                        dots(j)
                        dve.wait_ge(step, 2 * j + 3)
                        if BLOCKS[j + 1] < K:
                            more(j + 1)
                        dve.nop()

                nc.vector.tensor_tensor(w_self, mine[v][:, C:2 * C], k, ALU.add).then_inc(step, 1)
                nc.vector.tensor_scalar(mask[u][:, 0:K], mem["slot"][:, :], mine[v][:, CNT:CNT + 1], -NEG, ALU.is_ge, ALU.mult)
                nc.vector.tensor_copy(mask[u][:, K:K + 1], mine[v][:, SELF:SELF + 1])
                dve.wait_ge(step, 1)
                dot(w_self, K)
                dve.wait_ge(slot_in[r], arrive)
                add_k(0)
                dve.wait_ge(step, 2)
                dots(0)
                dve.wait_ge(step, 3)
                more(1)
                dve.sem_clear(step)
                nc.vector.tensor_tensor_reduce(out=masked[r], in0=score[u], in1=mask[u], scale=1.0, scalar=-NEG * 10, op0=ALU.add, op1=ALU.min,
                                               accum_out=least[r]).then_inc(masked_ready, 1)

            def summed(g, half, r):
                t = RING * g + r
                dve.wait_ge(acc_ready, t + 1)
                nc.vector.tensor_copy(home[half][:, r:r + 1], mine[RING * half + r][:, OWN:OWN + 1]).then_inc(tile_done, 1)
                nc.vector.bn_stats(st[:, 6 * r:6 * r + 6], acc[RING * half + r][:, 0:C]).then_inc(step, 1)
                dve.wait_ge(step, 1)
                nc.vector.bn_aggr(mv[:, 2 * r:2 * r + 2], st[:, 6 * r:6 * r + 6])
                if r == RING - 1:
                    nc.vector.scalar_tensor_tensor(veps, den[half], EPS, den[half], ALU.mult, ALU.mult).then_inc(step, 1)
                    dve.wait_ge(step, 2)
                    nc.vector.tensor_tensor(veps, mv[:, 1:2 * RING:2], veps, ALU.add).then_inc(var3, 1)

            def finish(g, half, first):
                dve.wait_ge(std3, g + 1)
                nc.vector.reciprocal(rstd, std).then_inc(fin, 1)
                dve.wait_ge(fin, g + RING // 2 + 4)
                for r in R:
                    if not first:
                        dve.wait_ge(out_done[r], 16 * g)
                    nc.vector.tensor_scalar(o[r], acc[RING * half + r][:, 0:C], mv[:, 2 * r:2 * r + 1], rstd[:, r:r + 1], ALU.subtract, ALU.mult).then_inc(out_ready, 1)

            def group(g, half, stage):
                v = load_values(nc, dve, plan[:, ds(g, 1), :], 1, 16 * K * GROUPS)
                for r in R:
                    scores(g, half, r, v[r], v[RING + r])
                    if r < 2:
                        if stage > 0:
                            summed(g - 1, 1 - half, RING - 2 + r)
                    else:
                        if r == 2 and stage > 0:
                            finish(g - 1, 1 - half, stage == 1)
                        summed(g, half, r - 2)

            group(0, 0, 0)
            group(1, 1, 1)
            with dve.Fori(1, GROUPS // 2) as i:
                for half in range(2):
                    group(2 * i + half, half, 2)
            for r in (RING - 2, RING - 1):
                dve.sem_clear(step)
                summed(GROUPS - 1, 1, r)
            finish(GROUPS - 1, 1, False)


def part_four(nc, ctx, io, mem):
    sem = lambda name: ctx.enter_context(nc.semaphore(name))
    A, bank = mem["A"], mem["bank"]
    at = [0]

    def carve(cols):
        a = at[0]
        at[0] += cols
        return A[:, a:a + cols]

    qrow, xrow, qT, xT, kT = (carve(N) for _ in range(5))
    wk = carve(C)
    H, kcol = [carve(N) for _ in range(2)], [carve(1) for _ in range(2)]
    adj, mask, scT, masked, att, attT = (carve(N) for _ in range(6))
    pcol, nmax, den, rden, veps, std, rstd = (carve(1) for _ in range(7))
    st, mv, y, o = carve(6), carve(2), carve(C), carve(C)
    tb, sb_, ab, yb = bank[0:2], bank[2:4], bank[4:6], bank[6]

    d_in = sem("d_in")
    d_adj = sem("d_adj")
    d_out = sem("d_out")
    d_rowT = sem("d_rowT")
    d_colT = sem("d_colT")
    d_k = sem("d_k")
    d_h = sem("d_h")
    d_s = sem("d_s")
    d_sT = sem("d_sT")
    d_sc = sem("d_sc")
    d_m = sem("d_m")
    d_mx = sem("d_mx")
    d_e = sem("d_e")
    d_eT = sem("d_eT")
    d_w = sem("d_w")
    d_y = sem("d_y")
    d_v = sem("d_v")
    d_r = sem("d_r")
    d_o = sem("d_o")
    block = ctx.enter_context(nc.Block())
    qx = io["qx"][0:NODES, :].rearrange("(b t p) c -> b p t c", b=B, p=P)
    adj4 = io["adj"].rearrange("b (t p) m -> b t p m", p=P)
    dve_on4 = sem("dve_on4")

    @block.sync
    def _(sp):
        full = sp.value_load(mem["full"][0:1, 0:1], min_val=0, max_val=NODES)
        with sp.If(full > 0):
            with nc.allow_non_contiguous_dma(reason="one column"):
                sp.dma_start(pcol, io["p"].rearrange("(c o) -> c o", o=1)).then_inc(d_in, 16)
            sp.dma_start(wk, io["WK"]).then_inc(d_in, 16)

            def graph(b, first):
                if not first:
                    sp.wait_ge(d_o, MT * b)
                for dst, c in ((qrow, 0), (xrow, C)):
                    sp.dma_start(dst.rearrange("p (t c) -> p t c", c=C), qx[ds(b, 1), :, :, c:c + C].rearrange("o p t c -> p (o t) c")).then_inc(d_in, 16)

                def load(t):
                    sp.dma_start(adj, adj4[ds(b, 1), ds(t, 1)].rearrange("o u p m -> (o u p) m")).then_inc(d_adj, 16)

                def store(t):
                    sp.wait_ge(d_o, MT * b + t + 1)
                    sp.dma_start(io["out"][ds(b * N + t * P, P), :], o).then_inc(d_out, 16)
                load(0)
                with sp.Fori(0, MT - 1) as t:
                    store(t)
                    load(t + 1)
                store(MT - 1)
            graph(0, True)
            with sp.Fori(1, B) as b:
                graph(b, False)
            sp.wait_ge(d_out, 16 * TILES)

    @block.tensor
    def _(pe):
        full = pe.value_load(mem["full"][0:1, 0:1], min_val=0, max_val=NODES)
        with pe.If(full > 0):
            with pe.Fori(0, B) as b:
                pe.wait_ge(d_in, 32 * b + 64)
                for i in range(6):
                    if i >= 2:
                        pe.wait_ge(d_colT, 6 * b + i - 1)
                    if i >= 4:
                        last = nc.tensor.matmul(tb[i % 2][:, :], wk, xT[:, (i - 4) * HALF:(i - 3) * HALF], start=True, stop=True)
                    else:
                        for t in range(QH):
                            m = (i % 2) * QH + t
                            last = nc.tensor.transpose(tb[i % 2][:, t * P:(t + 1) * P], (qrow, xrow)[i // 2][:, m * C:(m + 1) * C], mem["ident"][:, :])
                    last.then_inc(d_rowT, 1)
                with pe.Fori(0, MT) as t:
                    tile = MT * b + t
                    with pe.Fori(0, P // 2) as i:
                        for u in range(2):
                            pe.wait_ge(d_h, P * tile + 2 * i + u + 1)
                            for j in range(MT):
                                last = nc.tensor.matmul(sb_[j // QH][:, ds(2 * i + u + (j % QH) * P, 1)], H[u][:, j * P:(j + 1) * P], pcol, start=True, stop=True)
                            last.then_inc(d_s, 1)
                    for q in range(2):
                        pe.wait_ge(d_sT, 2 * tile + q + 1)
                        for j in range(QH):
                            last = nc.tensor.transpose(tb[q][:, j * P:(j + 1) * P], scT[:, (q * QH + j) * P:(q * QH + j + 1) * P], mem["ident"][:, :])
                        last.then_inc(d_sc, 1)
                    pe.wait_ge(d_e, tile + 1)
                    for q in range(2):
                        for j in range(QH):
                            last = nc.tensor.transpose(ab[q][:, j * P:(j + 1) * P], att[:, (q * QH + j) * P:(q * QH + j + 1) * P], mem["ident"][:, :])
                        last.then_inc(d_eT, 1)
                    for j in range(MT):
                        if j % QH == 0:
                            pe.wait_ge(d_w, 2 * tile + j // QH + 1)
                        last = nc.tensor.matmul(yb[:, 0:C], attT[:, j * P:(j + 1) * P], xrow[:, j * C:(j + 1) * C], start=(j == 0), stop=(j == MT - 1))
                    last.then_inc(d_y, 1)

    @block.scalar
    def _(act):
        full = act.value_load(mem["full"][0:1, 0:1], min_val=0, max_val=NODES)
        with act.If(full > 0):
            with act.Fori(0, B) as b:
                for i in range(6):
                    act.wait_ge(d_rowT, 6 * b + i + 1)
                    nc.scalar.activation((qT, xT, kT)[i // 2][:, (i % 2) * HALF:(i % 2 + 1) * HALF], tb[i % 2][:, :], ACT.Copy).then_inc(d_colT, 1)
                with act.Fori(0, MT) as t:
                    tile = MT * b + t
                    act.wait_ge(d_s, P * (tile + 1))
                    for q in range(2):
                        nc.scalar.activation(scT[:, q * HALF:(q + 1) * HALF], sb_[q][:, :], ACT.Copy).then_inc(d_sT, 1)
                    act.wait_ge(d_mx, tile + 1)
                    nc.scalar.activation(att, masked, ACT.Exp, bias=nmax, accum_out=den).then_inc(d_e, 1)
                    for q in range(2):
                        act.wait_ge(d_eT, 2 * tile + q + 1)
                        nc.scalar.activation(attT[:, q * HALF:(q + 1) * HALF], ab[q][:, :], ACT.Copy).then_inc(d_w, 1)
                    act.wait_ge(d_v, tile + 1)
                    nc.scalar.activation(std, veps, ACT.Sqrt).then_inc(d_r, 1)

    @block.vector
    def _(dve):
        full = dve.value_load(mem["full"][0:1, 0:1], min_val=0, max_val=NODES)
        with dve.If(full > 0):
            def node(tile, t, i, u, first):
                n = P * tile + 2 * i + u
                if not first:
                    dve.wait_ge(d_s, n - 1)
                nc.vector.tensor_copy(kcol[u], kT[:, ds(t * P + 2 * i + u, 1)]).then_inc(d_k, 1)
                dve.wait_ge(d_k, n + 1)
                nc.vector.tensor_scalar(H[u], qT, kcol[u], 0.0, ALU.add, ALU.max).then_inc(d_h, 1)

            def tile_of(b, t, first_out):
                tile = MT * b + t
                dve.sem_clear(d_m)

                def step(ins, n):
                    ins.then_inc(d_m, 1)
                    dve.wait_ge(d_m, n)
                dve.wait_ge(d_adj, 16 * (tile + 1))
                step(nc.vector.tensor_scalar(mask, adj, 0.0, -NEG, ALU.is_gt, ALU.mult), 1)
                for q in range(2):
                    half = slice(q * HALF, (q + 1) * HALF)
                    dve.wait_ge(d_sc, 2 * tile + q + 1)
                    step(nc.vector.scalar_tensor_tensor(masked[:, half], mask[:, half], NEG, tb[q][:, :], ALU.add, ALU.add), 2 + q)
                step(nc.vector.tensor_reduce(nmax, masked, AX.X, ALU.max), 4)
                nc.vector.tensor_scalar(nmax, nmax, -1.0, None, ALU.mult).then_inc(d_mx, 1)
                dve.wait_ge(d_y, tile + 1)
                step(nc.vector.reciprocal(rden, den), 5)
                step(nc.vector.scalar_tensor_tensor(y, yb[:, 0:C], rden, xrow[:, ds(t * C, C)], ALU.mult, ALU.add), 6)
                step(nc.vector.bn_stats(st, y), 7)
                step(nc.vector.bn_aggr(mv, st), 8)
                nc.vector.tensor_scalar(veps, mv[:, 1:2], EPS, None, ALU.add).then_inc(d_v, 1)
                dve.wait_ge(d_r, tile + 1)
                step(nc.vector.reciprocal(rstd, std), 9)
                if not first_out:
                    dve.wait_ge(d_out, 16 * tile)
                nc.vector.tensor_scalar(o, y, mv[:, 0:1], rstd, ALU.subtract, ALU.mult).then_inc(d_o, 1)

            def whole(b, t, first):
                if first:
                    for u in range(2):
                        node(0, 0, 0, u, True)
                    with dve.Fori(1, P // 2) as i:
                        for u in range(2):
                            node(0, 0, i, u, False)
                else:
                    with dve.Fori(0, P // 2) as i:
                        for u in range(2):
                            node(MT * b + t, t, i, u, False)
                tile_of(b, t, first)

            dve.wait_ge(d_colT, 6)
            whole(0, 0, True)
            with dve.Fori(1, MT) as t:
                whole(0, t, False)
            with dve.Fori(1, B) as b:
                hold(dve, d_colT, 6 * b + 6, dve_on4)
                with dve.Fori(0, MT) as t:
                    whole(b, t, False)


def program(nc, io):
    ctx = ExitStack()
    with ctx:
        sb = lambda name, cols, dt=f32: ctx.enter_context(nc.sbuf_tensor(name, [P, cols], dt))
        mem = {
            "bank": [ctx.enter_context(nc.psum_tensor(f"bank{i}", [P, HALF], f32)) for i in range(8)],
            "A": sb("A", (2 * RES + 2) * UNIT), "hT": sb("hT", NODES), "hst": sb("hst", N), "hws": sb("hws", N),
            "E": sb("E", (QH + 1) * N), "W": sb("W", LAYERS * C),
            "vec": sb("vec", 3 * LAYERS), "ident": sb("ident", P), "iota": sb("iota", N, f16),
            "key": [sb(f"key{k}", N, f16) for k in range(3)], "top": [sb(f"top{k}", K, f16) for k in range(3)],
            "keys": sb("keys", TILES * K, f16), "bcol": sb("bcol", 1), "st": sb("st", 6 * CHUNKS), "bn": sb("bn", 8),
            "others": sb("others", P, f16), "diag": sb("diag", TILES), "small": sb("small", 6 * TILES + 96), "of_class": sb("of_class", K),
            "own": sb("own", TILES, i32), "graph0": sb("graph0", TILES),
            "tomean": sb("tomean", TILES), "classes": sb("classes", K), "rank0": sb("rank0", TILES), "slot": sb("slot", K),
            "ones": sb("ones", P), "below": sb("below", P), "ranki": sb("ranki", TILES, i32),
            "plan": sb("plan", 2 * TILES, i32), "full": sb("full", 1, i32),
        }
        mem["nat"] = [mem["E"][:, k * N:(k + 1) * N] for k in range(QH)]
        mem["xs"] = mem["E"][:, QH * N:(QH + 1) * N]
        for part in (part_one, part_two, part_three, part_four):
            with ExitStack() as own:
                part(nc, own, io, mem)


_NAMES = (("x", "x"), ("adj", "adj"), ("W", "L0_gnn_W"), ("b", "L0_gnn_b"), ("gamma", "L0_gnn_gamma"), ("beta", "L0_gnn_beta"),
          ("WQ", "L1_gnn_WQ"), ("WK", "L1_gnn_WK"), ("p", "L1_gnn_p"))


def kernel(**inputs):
    import concourse.bacc as bacc
    from concourse.bass_utils import run_bass_kernel_spmd

    nc = bacc.Bacc("TRN2", target_bir_lowering=False, num_devices=1)
    io, arrays = {}, {}
    for short, name in _NAMES:
        a = np.ascontiguousarray(inputs[name])
        arrays[f"in_{short}"] = a
        io[short] = nc.dram_tensor(f"in_{short}", a.shape, mybir.dt.from_np(a.dtype), kind="ExternalInput").ap()
    io["adjT"] = nc.dram_tensor("adj_transposed", [STREAM, 2, P, UNIT], f32, kind="Internal").ap()
    io["qx"] = nc.dram_tensor("rows_qx", [NODES + B, 2 * C], f32, kind="Internal").ap()
    io["sorted"] = nc.dram_tensor("rows_sorted", [NODES, ROW], f32, kind="Internal").ap()
    io["out"] = nc.dram_tensor("out", [NODES, C], f32, kind="ExternalOutput").ap()
    program(nc, io)
    result = run_bass_kernel_spmd(nc, [arrays], core_ids=[0])
    return result.results[0]["out"].reshape(B, N, C)
```
